# Optimizing a Trainium2 kernel written in Bass

```python
import numpy as np
import jax
import jax.numpy as jnp

def _softmax(x, axis=-1):
    return jax.nn.softmax(x, axis=axis)

def _gelu(x):
    return jax.nn.gelu(x, approximate=True)

def _silu(x):
    return jax.nn.silu(x)

def _sigmoid(x):
    return jax.nn.sigmoid(x)

def _layernorm(x, axis=-1, eps=1e-05):
    m = jnp.mean(x, axis=axis, keepdims=True)
    v = jnp.var(x, axis=axis, keepdims=True)
    return (x - m) / jnp.sqrt(v + eps)

def _scatter_add(tgt, idx, src, axis=0):
    return tgt.at[idx].add(src)

def _segment_sum(src, seg, n):
    return jax.ops.segment_sum(src, seg, n)
kernel_name = 'mk_audio_tower_d2_tok_audfeat512_r4_de65a2'

def setup_inputs(seed: int=0):
    np.random.seed(seed)
    _w = jnp.asarray

    def _rec_inputs():
        import jax
        import jax.numpy as jnp
        _rk = jax.random.key(seed)
        x = -0.00190633 + 1.00279 * jax.random.normal(jax.random.fold_in(_rk, 1), (32, 256, 7), jnp.float32)
        return x
    x = _rec_inputs()

    def _L0_tok_setup():
        import jax, jax.numpy as jnp
        import numpy as np
        SIG_DEPTH = 4

        def _outer(a, b):
            return (a[:, :, None] * b[:, None, :]).reshape(a.shape[0], -1)
        key = jax.random.key(seed)
        k1, k2 = jax.random.split(key)
        B, L, Cin = (64, 64, 7)
        out_dim = 128
        C = Cin + 1
        sig_channels = sum((C ** k for k in range(1, SIG_DEPTH + 1)))
        inp = jax.random.normal(k1, (B, L, Cin), dtype=jnp.float32)
        W = jax.random.normal(k2, (out_dim, sig_channels), dtype=jnp.float32) * 0.02
        b = jnp.zeros((out_dim,), dtype=jnp.float32)
        return {'inp': inp, 'W': W, 'b': b}
    _L0_tok_all = _L0_tok_setup()
    _L0_tok_in = {k: v for k, v in _L0_tok_all.items() if k in ('W', 'b')}
    del _L0_tok_all

    def _L0_attn_setup():
        import jax, jax.numpy as jnp
        import numpy as np
        A, Bp, Cp, Dp = (0.0, 0.3, 0.7, 1.0)

        def fuzzy_membership(p):
            rise = (p - A) / (Bp - A)
            fall = (Dp - p) / (Dp - Cp)
            return jnp.maximum(jnp.minimum(rise, fall), 0.0)
        key = jax.random.key(seed)
        k1, k2, k3, k4, k5 = jax.random.split(key, 5)
        B, S, D = (8, 512, 128)
        x = jax.random.normal(k1, (B, S, D), dtype=jnp.float32)
        s = 1.0 / np.sqrt(D)
        Wq = jax.random.uniform(k2, (D, D), jnp.float32, -s, s)
        bq = jax.random.uniform(k3, (D,), jnp.float32, -s, s)
        Wk = jax.random.uniform(k4, (D, D), jnp.float32, -s, s)
        bk = jax.random.uniform(k5, (D,), jnp.float32, -s, s)
        return {'x': x, 'Wq': Wq, 'bq': bq, 'Wk': Wk, 'bk': bk}
    _L0_attn_all = _L0_attn_setup()
    _L0_attn_in = {k: v for k, v in _L0_attn_all.items() if k in ('Wq', 'bq', 'Wk', 'bk')}
    del _L0_attn_all

    def _L0_ffn_setup():
        import jax, jax.numpy as jnp
        import numpy as np
        B, S, D = (8, 1024, 128)
        H = 512
        O = 128
        E = 8
        TOP_K = 1
        key = jax.random.key(seed)
        ks = jax.random.split(key, 8)
        sc = 0.02
        return {'x': jax.random.normal(ks[0], (B, S, D), dtype=jnp.float32), 'Wr': jax.random.normal(ks[1], (D, E), dtype=jnp.float32) * sc, 'br': jnp.zeros((E,), dtype=jnp.float32), 'W1': jax.random.normal(ks[2], (E, D, H), dtype=jnp.float32) * sc, 'b1': jnp.zeros((E, H), dtype=jnp.float32), 'W2': jax.random.normal(ks[3], (E, H, O), dtype=jnp.float32) * sc, 'b2': jnp.zeros((E, O), dtype=jnp.float32)}
    _L0_ffn_all = _L0_ffn_setup()
    _L0_ffn_in = {k: v for k, v in _L0_ffn_all.items() if k in ('Wr', 'br', 'W1', 'b1', 'W2', 'b2')}
    del _L0_ffn_all

    def _L1_attn_setup():
        import jax, jax.numpy as jnp
        import numpy as np
        import math
        B, T, C = (8, 256, 128)
        H = 8
        HD = C // H
        MAX_REL = 64 + 4

        def _rel_index(t):
            r = jnp.arange(t)
            dist = jnp.clip(r[None, :] - r[:, None], -MAX_REL, MAX_REL)
            return dist + MAX_REL
        key = jax.random.key(seed)
        ks = jax.random.split(key, 12)
        xavier = lambda k, shape: jax.random.uniform(k, shape, jnp.float32, -1.0, 1.0) * math.sqrt(6.0 / (shape[0] + shape[1]))
        return {'x': jax.random.normal(ks[0], (B, T, C), jnp.float32), 'Wq': xavier(ks[1], (C, C)), 'bq': jnp.zeros((C,), jnp.float32), 'Wk': xavier(ks[2], (C, C)), 'bk': jnp.zeros((C,), jnp.float32), 'Wv': xavier(ks[3], (C, C)), 'bv': jnp.zeros((C,), jnp.float32), 'Wo': xavier(ks[4], (C, C)), 'bo': jnp.zeros((C,), jnp.float32), 'rel_k': xavier(ks[5], (2 * MAX_REL + 1, HD)), 'rel_v': xavier(ks[6], (2 * MAX_REL + 1, HD))}
    _L1_attn_all = _L1_attn_setup()
    _L1_attn_in = {k: v for k, v in _L1_attn_all.items() if k in ('Wq', 'bq', 'Wk', 'bk', 'Wv', 'bv', 'Wo', 'bo', 'rel_k', 'rel_v')}
    del _L1_attn_all

    def _L1_ffn_setup():
        import jax, jax.numpy as jnp
        import numpy as np
        E = 64
        K = 2
        D = 128
        H = 64
        NSH = 2
        ROUTE_SCALE = 2.5
        CAP = 256
        STD = 0.02
        key = jax.random.key(seed)
        ks = jax.random.split(key, 8)
        x = jax.random.normal(ks[0], (4, 512, D), dtype=jnp.float32)
        gate_w = jax.random.normal(ks[1], (E, D), dtype=jnp.float32) * STD
        w1 = jax.random.normal(ks[2], (E, D, H), dtype=jnp.float32) * STD
        w3 = jax.random.normal(ks[3], (E, D, H), dtype=jnp.float32) * STD
        w2 = jax.random.normal(ks[4], (E, H, D), dtype=jnp.float32) * STD
        sw1 = jax.random.normal(ks[5], (D, H * NSH), dtype=jnp.float32) * STD
        sw3 = jax.random.normal(ks[6], (D, H * NSH), dtype=jnp.float32) * STD
        sw2 = jax.random.normal(ks[7], (H * NSH, D), dtype=jnp.float32) * STD
        return {'x': x, 'gate_w': gate_w, 'w1': w1, 'w3': w3, 'w2': w2, 'sw1': sw1, 'sw3': sw3, 'sw2': sw2}
    _L1_ffn_all = _L1_ffn_setup()
    _L1_ffn_in = {k: v for k, v in _L1_ffn_all.items() if k in ('gate_w', 'w1', 'w3', 'w2', 'sw1', 'sw3', 'sw2')}
    del _L1_ffn_all
    return {'x': x, 'L0_tok_W': _L0_tok_in['W'], 'L0_tok_b': _L0_tok_in['b'], 'L0_attn_Wq': _L0_attn_in['Wq'], 'L0_attn_bq': _L0_attn_in['bq'], 'L0_attn_Wk': _L0_attn_in['Wk'], 'L0_attn_bk': _L0_attn_in['bk'], 'L0_ffn_Wr': _L0_ffn_in['Wr'], 'L0_ffn_br': _L0_ffn_in['br'], 'L0_ffn_W1': _L0_ffn_in['W1'], 'L0_ffn_b1': _L0_ffn_in['b1'], 'L0_ffn_W2': _L0_ffn_in['W2'], 'L0_ffn_b2': _L0_ffn_in['b2'], 'L1_attn_Wq': _L1_attn_in['Wq'], 'L1_attn_bq': _L1_attn_in['bq'], 'L1_attn_Wk': _L1_attn_in['Wk'], 'L1_attn_bk': _L1_attn_in['bk'], 'L1_attn_Wv': _L1_attn_in['Wv'], 'L1_attn_bv': _L1_attn_in['bv'], 'L1_attn_Wo': _L1_attn_in['Wo'], 'L1_attn_bo': _L1_attn_in['bo'], 'L1_attn_rel_k': _L1_attn_in['rel_k'], 'L1_attn_rel_v': _L1_attn_in['rel_v'], 'L1_ffn_gate_w': _L1_ffn_in['gate_w'], 'L1_ffn_w1': _L1_ffn_in['w1'], 'L1_ffn_w3': _L1_ffn_in['w3'], 'L1_ffn_w2': _L1_ffn_in['w2'], 'L1_ffn_sw1': _L1_ffn_in['sw1'], 'L1_ffn_sw3': _L1_ffn_in['sw3'], 'L1_ffn_sw2': _L1_ffn_in['sw2']}

def reference(x, L0_tok_W, L0_tok_b, L0_attn_Wq, L0_attn_bq, L0_attn_Wk, L0_attn_bk, L0_ffn_Wr, L0_ffn_br, L0_ffn_W1, L0_ffn_b1, L0_ffn_W2, L0_ffn_b2, L1_attn_Wq, L1_attn_bq, L1_attn_Wk, L1_attn_bk, L1_attn_Wv, L1_attn_bv, L1_attn_Wo, L1_attn_bo, L1_attn_rel_k, L1_attn_rel_v, L1_ffn_gate_w, L1_ffn_w1, L1_ffn_w3, L1_ffn_w2, L1_ffn_sw1, L1_ffn_sw3, L1_ffn_sw2):
    import jax
    import jax.numpy as jnp

    def _L0_tok_ref(inp, W, b):
        import jax, jax.numpy as jnp
        import numpy as np
        SIG_DEPTH = 4

        def _outer(a, b):
            return (a[:, :, None] * b[:, None, :]).reshape(a.shape[0], -1)
        B, L, Cin = inp.shape
        t = jnp.broadcast_to(jnp.linspace(0.0, 1.0, L, dtype=inp.dtype)[None, :, None], (B, L, 1))
        x = jnp.concatenate([t, inp], axis=-1)
        C = Cin + 1
        d = SIG_DEPTH
        dx = jnp.transpose(x[:, 1:] - x[:, :-1], (1, 0, 2))
        init = tuple((jnp.zeros((B, C ** (k + 1)), x.dtype) for k in range(d)))

        def step(levels, v):
            e = [v]
            for k in range(1, d):
                e.append(_outer(e[-1], v) / (k + 1))
            new = []
            for k in range(d):
                acc = levels[k] + e[k]
                for i in range(k):
                    acc = acc + _outer(levels[i], e[k - 1 - i])
                new.append(acc)
            sig = jnp.concatenate(new, axis=-1)
            return (tuple(new), sig)
        _, sigs = jax.lax.scan(step, init, dx)
        sigs = jnp.transpose(sigs, (1, 0, 2))
        return sigs @ W.T + b

    def _L0_attn_ref(x, Wq, bq, Wk, bk):
        import jax, jax.numpy as jnp
        import numpy as np
        A, Bp, Cp, Dp = (0.0, 0.3, 0.7, 1.0)

        def fuzzy_membership(p):
            rise = (p - A) / (Bp - A)
            fall = (Dp - p) / (Dp - Cp)
            return jnp.maximum(jnp.minimum(rise, fall), 0.0)
        q = jnp.einsum('bsd,ed->bse', x, Wq) + bq
        k = jnp.einsum('bsd,ed->bse', x, Wk) + bk
        scores = jnp.einsum('bqd,bkd->bqk', q, k)
        attn = jax.nn.softmax(scores, axis=-1)
        attn = fuzzy_membership(attn)
        return jnp.einsum('bqk,bkd->bqd', attn, x)

    def _L0_ffn_ref(x, Wr, br, W1, b1, W2, b2):
        import jax, jax.numpy as jnp
        import numpy as np
        B, S, D = (8, 1024, 128)
        H = 512
        O = 128
        E = 8
        TOP_K = 1
        b, s, d = x.shape
        xf = x.reshape(-1, d)
        router_logits = xf @ Wr + br
        topk_logits, topk_idx = jax.lax.top_k(router_logits, TOP_K)
        topk_gates = jax.nn.softmax(topk_logits, axis=1)
        out = jnp.zeros((xf.shape[0], O), dtype=x.dtype)
        for k in range(TOP_K):
            idx_k = topk_idx[:, k]
            gate_k = topk_gates[:, k:k + 1]
            for e in range(E):
                h = jax.nn.relu(xf @ W1[e] + b1[e])
                oe = h @ W2[e] + b2[e]
                mask = (idx_k == e)[:, None]
                out = out + jnp.where(mask, gate_k * oe, 0.0)
        return out.reshape(b, s, O)

    def _L1_attn_ref(x, Wq, bq, Wk, bk, Wv, bv, Wo, bo, rel_k, rel_v):
        import jax, jax.numpy as jnp
        import numpy as np
        import math
        B, T, C = (8, 256, 128)
        H = 8
        HD = C // H
        MAX_REL = 64 + 4

        def _rel_index(t):
            r = jnp.arange(t)
            dist = jnp.clip(r[None, :] - r[:, None], -MAX_REL, MAX_REL)
            return dist + MAX_REL
        b, t, c = x.shape
        h, hd = (H, HD)
        q = x @ Wq + bq
        k = x @ Wk + bk
        v = x @ Wv + bv
        rq = q.reshape(b, t, h, hd).transpose(0, 2, 1, 3)
        rk = k.reshape(b, t, h, hd).transpose(0, 2, 1, 3)
        rv = v.reshape(b, t, h, hd).transpose(0, 2, 1, 3)
        idx = _rel_index(t)
        rk2 = rel_k[idx]
        rv2 = rel_v[idx]
        attn1 = jnp.einsum('bhqd,bhkd->bhqk', rq, rk)
        attn2 = jnp.einsum('bhqd,qkd->bhqk', rq, rk2)
        attn = jax.nn.softmax((attn1 + attn2) * (1.0 / math.sqrt(c)), axis=-1)
        w1 = jnp.einsum('bhqk,bhkd->bhqd', attn, rv)
        w2 = jnp.einsum('bhqk,qkd->bhqd', attn, rv2)
        out = (w1 + w2).transpose(0, 2, 1, 3).reshape(b, t, c)
        return out @ Wo + bo

    def _L1_ffn_ref(x, gate_w, w1, w3, w2, sw1, sw3, sw2):
        import jax, jax.numpy as jnp
        import numpy as np
        E = 64
        K = 2
        D = 128
        H = 64
        NSH = 2
        ROUTE_SCALE = 2.5
        CAP = 256
        STD = 0.02
        bs, slen, d = x.shape
        xf = x.reshape(-1, d)
        logits = xf @ gate_w.T
        scores = jax.nn.sigmoid(logits.astype(jnp.float32))
        top_scores, top_idx = jax.lax.top_k(scores, K)
        top_scores = top_scores / (top_scores.sum(-1, keepdims=True) + 1e-20)
        top_scores = top_scores * ROUTE_SCALE
        flat_e = top_idx.reshape(-1)
        x_pairs = jnp.repeat(xf, K, axis=0)
        oh = jax.nn.one_hot(flat_e, E, dtype=jnp.int32)
        pos = jnp.take_along_axis(jnp.cumsum(oh, axis=0), flat_e[:, None], axis=1)[:, 0] - 1
        buf = jnp.zeros((E, CAP, d), dtype=xf.dtype).at[flat_e, pos].set(x_pairs, mode='drop')
        h = jax.nn.silu(jnp.einsum('ecd,edh->ech', buf, w1)) * jnp.einsum('ecd,edh->ech', buf, w3)
        y = jnp.einsum('ech,ehd->ecd', h, w2)
        valid = (pos < CAP)[:, None]
        y_pairs = jnp.where(valid, y[flat_e, jnp.minimum(pos, CAP - 1)], 0.0)
        routed = (y_pairs.reshape(-1, K, d) * top_scores[..., None].astype(xf.dtype)).sum(axis=1)
        shared = jax.nn.silu(xf @ sw1) * (xf @ sw3) @ sw2
        return (shared + routed).reshape(bs, slen, d)
    h = _L0_tok_ref(x, L0_tok_W, L0_tok_b)
    h = h + _L0_attn_ref(_layernorm(h, axis=-1), L0_attn_Wq, L0_attn_bq, L0_attn_Wk, L0_attn_bk)
    h = h + _L0_ffn_ref(_layernorm(h, axis=-1), L0_ffn_Wr, L0_ffn_br, L0_ffn_W1, L0_ffn_b1, L0_ffn_W2, L0_ffn_b2)
    h = h + _L1_attn_ref(_layernorm(h, axis=-1), L1_attn_Wq, L1_attn_bq, L1_attn_Wk, L1_attn_bk, L1_attn_Wv, L1_attn_bv, L1_attn_Wo, L1_attn_bo, L1_attn_rel_k, L1_attn_rel_v)
    h = h + _L1_ffn_ref(_layernorm(h, axis=-1), L1_ffn_gate_w, L1_ffn_w1, L1_ffn_w3, L1_ffn_w2, L1_ffn_sw1, L1_ffn_sw3, L1_ffn_sw2)
    return h

_drawn_inputs = setup_inputs


def setup_inputs(seed=0):
    import zlib

    import numpy as np

    out = dict(_drawn_inputs(seed))
    spreads = {'L0_tok_b': (0.0, 0.8),
     'L0_ffn_br': (0.0, 0.8),
     'L0_ffn_b1': (0.0, 0.8),
     'L0_ffn_b2': (0.0, 0.8),
     'L1_attn_bq': (0.0, 0.8),
     'L1_attn_bk': (0.0, 2.0),
     'L1_attn_bv': (0.0, 0.8),
     'L1_attn_bo': (0.0, 2.0)}
    factors = {'L0_attn_bq': 8.0,
     'L0_attn_bk': 64.0,
     'L0_ffn_Wr': 8.0,
     'L0_ffn_W1': 8.0,
     'L0_ffn_W2': 8.0,
     'L1_attn_Wq': 8.0,
     'L1_attn_Wk': 8.0,
     'L1_attn_Wv': 3.716,
     'L1_attn_Wo': 3.646,
     'L1_attn_rel_k': 8.0,
     'L1_attn_rel_v': 8.0,
     'L1_ffn_gate_w': 8.0,
     'L1_ffn_w1': 8.0,
     'L1_ffn_w3': 8.0,
     'L1_ffn_w2': 8.0,
     'L1_ffn_sw1': 8.0,
     'L1_ffn_sw3': 8.0,
     'L1_ffn_sw2': 8.0}
    for name, (base, spread) in spreads.items():
        noise = np.random.default_rng([zlib.crc32(name.encode()), seed]).standard_normal(out[name].shape)
        drawn = base * np.exp(spread * noise) if base else spread * noise
        out[name] = jnp.asarray(drawn.astype(out[name].dtype))
    for name, factor in factors.items():
        out[name] = (out[name] * factor).astype(out[name].dtype)
    return out
```

```python
import concourse.bass as bass
from concourse import mybir
from contextlib import ExitStack
import numpy as np

FP32 = mybir.dt.float32
BF16 = mybir.dt.bfloat16
I32 = mybir.dt.int32
U32 = mybir.dt.uint32
ALU = mybir.AluOpType
ACT = mybir.ActivationFunctionType
AX = mybir.AxisListType

P = 128
B, T, CIN, D = 32, 256, 7, 128
L = T - 1
ROWS = (P, L - P)
C = CIN + 1
NT = 2 * B
EPS = 1e-5
G = 4


class Bench:

    def __init__(self, nc, stage):
        self.nc, self.stage, self.stack, self.sems = nc, stage, ExitStack(), []

    def __enter__(self):
        self.stack.__enter__()
        return self

    def __exit__(self, *e):
        if self.sems:
            self.nc.clear_and_free_semaphores(self.sems)
            self.nc.all_engine_barrier()
        return self.stack.__exit__(*e)

    def sb(self, name, shape, dt=FP32):
        return self.stack.enter_context(self.nc.sbuf_tensor(f"{self.stage}_{name}", shape, dt))

    def ps(self, name, shape, dt=FP32):
        return self.stack.enter_context(self.nc.psum_tensor(f"{self.stage}_{name}", shape, dt))

    def sem(self, name):
        self.sems.append(self.nc.alloc_semaphore(f"{self.stage}_{name}"))
        return self.sems[-1]


class Chain:

    def __init__(self, eng, sem, base=0):
        self.eng, self.sem, self.n = eng, sem, base

    def __call__(self, instruction):
        instruction.then_inc(self.sem, 1)
        self.n = self.n + 1
        self.eng.wait_ge(self.sem, self.n)


def outer(nc_eng, out, left, right, n, a, c):
    return nc_eng.tensor_tensor(
        out,
        left.unsqueeze(3).to_broadcast([P, n, a, c]),
        right.unsqueeze(2).to_broadcast([P, n, a, c]),
        ALU.mult)


def signature_tokens(nc, K, h, stats, x_t, step_time, w_main, w_low, tok_b):
    NA = C ** 3 // P
    LOW = C ** 2 + C + 1
    after, upto, ident = K["after"], K["upto"], K["ident"]
    with Bench(nc, "tok") as m:
        x0 = m.sb("x0", [P, 2, B * CIN])
        x1 = m.sb("x1", [P, 2, B * CIN])
        dt_sb = m.sb("dt", [P, 2])
        v = m.sb("v", [P, B, 2, C])
        v_s = m.sb("v_scaled", [P, B, 2, C])
        g1 = m.sb("g1", [P, B, 2, C])
        g1v = m.sb("g1v", [P, NT, C, C])
        r2_pre = m.sb("r2_pre", [P, NT, C, C])
        q2_pre = m.sb("q2_pre", [P, NT, C, C])
        low = m.sb("low", [P, 2, LOW])
        q2 = m.sb("q2", [P, 2, C * C])
        r2v = m.sb("r2v", [P, 2, C ** 3])
        q2v = m.sb("q2v", [P, 2, C ** 3])
        feat = m.sb("feat", [P, 2, NA + 1, P])
        w = m.sb("w", [P, NA + 1, C * D])
        bias = m.sb("bias", [P, D])
        prod = m.sb("prod", [P, 2, C, D])
        inc = m.sb("inc", [P, 2, D])
        a3_ps = m.ps("a3_ps", [P, NA, 2, P])
        low_ps = m.ps("low_ps", [P, 512])
        small_ps = m.ps("small_ps", [P, 512])
        main_ps = [m.ps(f"main_ps{s}", [P, C * D]) for s in range(2)]
        e1_ps = main_ps[0]
        lowT_ps = low_ps[:, 0:2 * P]
        h_ps = small_ps[:, 0:2 * D].rearrange("p (s d) -> p s d", s=2)
        e2_ps = small_ps[:, 2 * D:2 * D + 2 * C * C]

        x_in, w_in, zeroed = m.sem("x_in"), m.sem("w_in"), m.sem("zeroed")
        vec, v_ready, e1_ready = m.sem("vec"), m.sem("v_ready"), m.sem("e1_ready")
        pre_ready = m.sem("pre_ready")
        e2_ready, low_ready, q2_ready = m.sem("e2_ready"), m.sem("low_ready"), m.sem("q2_ready")
        r2v_ready, q2v_ready = m.sem("r2v_ready"), m.sem("q2v_ready")
        a3_ready, feat_ready = m.sem("a3_ready"), m.sem("feat_ready")
        main_ready, prod_ready, inc_ready = m.sem("main_ready"), m.sem("prod_ready"), m.sem("inc_ready")
        h_ready, h_done = m.sem("h_ready"), m.sem("h_done")

        with nc.Block() as block:

            @block.sync
            def _(sp):
                sp.dma_start(x0[:, 0, :], x_t[0:P, :]).then_inc(x_in, 16)
                sp.dma_start(x1[:, 0, :], x_t[1:P + 1, :]).then_inc(x_in, 16)
                sp.dma_start(x0[0:ROWS[1], 1, :], x_t[P:L, :]).then_inc(x_in, 16)
                sp.dma_start(x1[0:ROWS[1], 1, :], x_t[P + 1:T, :]).then_inc(x_in, 16)
                sp.dma_start(dt_sb[:], step_time).then_inc(x_in, 16)
                for j in range(NA):
                    sp.dma_start(w[:, j, :], w_main[j * P:(j + 1) * P, :]).then_inc(w_in, 16)
                sp.dma_start(w[0:LOW, NA, :], w_low).then_inc(w_in, 16)
                sp.dma_start(bias[:], tok_b.partition_broadcast(P)).then_inc(w_in, 16)
                sp.wait_ge(w_in, 16 * (NA + 2))

            def tile_view(t):
                return t[:].rearrange("p b s c -> p (b s) c")

            @block.vector
            def _(dve):
                link = Chain(dve, vec)
                link(nc.vector.memset(v[:], 0.0))
                nc.vector.memset(low[:, :, LOW - 1:LOW], 1.0)
                dve.wait_ge(x_in, 16 * 5)
                for s in range(2):
                    n = ROWS[s]
                    nc.vector.tensor_tensor(
                        v[0:n, :, s, 1:C],
                        x1[0:n, s, :].rearrange("p (b c) -> p b c", c=CIN),
                        x0[0:n, s, :].rearrange("p (b c) -> p b c", c=CIN), ALU.subtract)
                    link(nc.vector.tensor_copy(v[:, :, s, 0:1],
                                               dt_sb[:, s:s + 1].unsqueeze(1).to_broadcast([P, B, 1])))
                nc.vector.memset(q2[:], 0.0).then_inc(v_ready, 1)
                e1 = e1_ps[:, 0:NT * C].rearrange("p (b s c) -> p b s c", b=B, s=2)
                dve.wait_ge(e1_ready, 1)
                link(nc.vector.scalar_tensor_tensor(g1[:], v[:], 0.5, e1, ALU.mult, ALU.add))
                link(outer(nc.vector, g1v[:], tile_view(g1), tile_view(v), NT, C, C))
                for div, scale, pre in ((3.0, 0.5, r2_pre), (4.0, 1.0 / 6.0, q2_pre)):
                    link(nc.vector.scalar_tensor_tensor(v_s[:], v[:], 1.0 / div, e1, ALU.mult, ALU.add))
                    link(nc.vector.tensor_scalar(v_s[:], v_s[:], scale, None, ALU.mult))
                    link(outer(nc.vector, pre[:], tile_view(v_s), tile_view(v), NT, C, C))
                nc.vector.memset(inc[:], 0.0).then_inc(pre_ready, 1)

                vt, g1t = tile_view(v), tile_view(g1)

                def features(b, first=False):
                    dve.wait_ge(e2_ready, b + 1)
                    e2 = e2_ps.rearrange("p (s k) -> p s k", s=2)
                    flat = "p n a c -> p n (a c)"
                    nc.vector.tensor_tensor(low[:, :, 0:C * C], e2,
                                            r2_pre[:, bass.ds(2 * b, 2)].rearrange(flat), ALU.add)
                    nc.vector.tensor_copy(low[:, :, C * C:C * C + C], g1t[:, bass.ds(2 * b, 2), :])\
                        .then_inc(low_ready, 1)
                    if not first:
                        dve.wait_ge(q2v_ready, b)
                    nc.vector.scalar_tensor_tensor(q2[:], e2, 0.5, q2_pre[:, bass.ds(2 * b, 2)].rearrange(flat),
                                                   ALU.mult, ALU.add).then_inc(q2_ready, 1)
                    dve.wait_ge(low_ready, b + 1)
                    outer(nc.vector, r2v[:].rearrange("p n (a c) -> p n a c", c=C), low[:, :, 0:C * C],
                          vt[:, bass.ds(2 * b, 2), :], 2, C * C, C).then_inc(r2v_ready, 1)

                def combine(b, s, first=False):
                    dve.wait_ge(main_ready, 2 * b + s + 1)
                    if not first:
                        dve.wait_ge(inc_ready, 2 * b + s - 1)
                    nc.vector.tensor_tensor(
                        prod[:, s], main_ps[s][:].rearrange("p (c o) -> p c o", c=C),
                        vt[:, bass.ds(2 * b + s, 1), :].rearrange("p n c -> p (n c)").unsqueeze(2)
                        .to_broadcast([P, C, D]), ALU.mult).then_inc(prod_ready, 1)
                    dve.wait_ge(prod_ready, 2 * b + s + 1)
                    nc.vector.tensor_reduce(inc[:, s, :], prod[:, s].rearrange("p c o -> p o c"),
                                            AX.X, ALU.add).then_inc(inc_ready, 1)

                def finish(b):
                    dve.wait_ge(h_ready, b + 1)
                    nc.vector.tensor_tensor(h[:, bass.ds(2 * b, 2), :], h_ps,
                                            bias[:].unsqueeze(1).to_broadcast([P, 2, D]),
                                            ALU.add).then_inc(h_done, 1)
                    dve.wait_ge(h_done, b + 1)
                    for s in range(2):
                        nc.vector.bn_stats(stats[:, bass.ds(2 * b + s, 1), :].rearrange("p n k -> p (n k)"),
                                           h[:, bass.ds(2 * b + s, 1), :].rearrange("p n k -> p (n k)"))

                dve.wait_ge(w_in, 16 * (NA + 2))
                features(0, first=True)
                features(1)
                combine(0, 0, first=True)
                combine(0, 1, first=True)
                with nc.vector.Fori(1, B - 1) as b:
                    features(b + 1)
                    dve.wait_ge(h_ready, b)
                    combine(b, 0)
                    finish(b - 1)
                    combine(b, 1)
                dve.wait_ge(h_ready, B - 1)
                combine(B - 1, 0)
                finish(B - 2)
                combine(B - 1, 1)
                finish(B - 1)

            @block.gpsimd
            def _(pool):
                vt = tile_view(v)

                def outer_q2(b):
                    pool.wait_ge(q2_ready, b + 1)
                    outer(nc.gpsimd, q2v[:].rearrange("p n (a c) -> p n a c", c=C), q2[:],
                          vt[:, bass.ds(2 * b, 2), :], 2, C * C, C).then_inc(q2v_ready, 1)

                outer_q2(0)
                with nc.gpsimd.Fori(1, B) as b:
                    pool.wait_ge(e2_ready, b + 1)
                    outer_q2(b)

            @block.scalar
            def _(act):
                def evacuate(b, s, first=False):
                    act.wait_ge(a3_ready, b + 1)
                    if not first:
                        act.wait_ge(main_ready, 2 * b - 1 + s)
                    nc.scalar.activation(feat[:, s, 0:NA, :], a3_ps[:, :, s, :], ACT.Copy)
                    nc.scalar.activation(feat[0:LOW, s, NA, :], lowT_ps[0:LOW, s * P:(s + 1) * P],
                                         ACT.Copy).then_inc(feat_ready, 1)

                evacuate(0, 0, first=True)
                evacuate(0, 1, first=True)
                with nc.scalar.Fori(1, B) as b:
                    evacuate(b, 0)
                    evacuate(b, 1)

            @block.tensor
            def _(pe):
                def level2(b, first=False):
                    if not first:
                        pe.wait_ge(h_done, b - 2)
                    gv = g1v[:].rearrange("p n a c -> p n (a c)")
                    nc.tensor.matmul(e2_ps[:, 0:64], after[:, 0:P], gv[:, bass.ds(2 * b, 1), :],
                                     start=True, stop=True)
                    nc.tensor.matmul(e2_ps[:, 64:128], after[:, P:T], gv[:, bass.ds(2 * b, 1), :],
                                     start=True, stop=False)
                    nc.tensor.matmul(e2_ps[:, 64:128], after[:, 0:P], gv[:, bass.ds(2 * b + 1, 1), :],
                                     start=False, stop=True).then_inc(e2_ready, 1)

                def level3(b, first=False):
                    pe.wait_ge(r2v_ready, b + 1)
                    pe.wait_ge(low_ready, b + 1)
                    if not first:
                        pe.wait_ge(feat_ready, 2 * b)
                    for s in range(2):
                        nc.tensor.transpose(lowT_ps[0:LOW, s * P:(s + 1) * P], low[:, s, :], ident[:])
                    pe.wait_ge(q2v_ready, b + 1)
                    for j in range(NA):
                        cols = slice(j * P, (j + 1) * P)
                        for s in range(2):
                            nc.tensor.matmul(a3_ps[:, j, s, :], q2v[:, s, cols], ident[:], start=(s == 0),
                                             stop=False, skip_group_check=True)
                        nc.tensor.matmul(a3_ps[:, j, 1, :], r2v[:, 1, cols], after[:, 0:P],
                                         start=False, stop=False, skip_group_check=True)
                        last = nc.tensor.matmul(a3_ps[:, j], r2v[:, 0, cols], after[:],
                                                start=False, stop=True, skip_group_check=True)
                    last.then_inc(a3_ready, 1)

                def main(b, s, first=False):
                    pe.wait_ge(feat_ready, 2 * b + s + 1)
                    if not first:
                        pe.wait_ge(prod_ready, 2 * b + s - 1)
                    for half in range(2):
                        cols = slice(half * 512, (half + 1) * 512)
                        for j in range(NA + 1):
                            n = P if j < NA else LOW
                            last = nc.tensor.matmul(main_ps[s][:, cols], feat[0:n, s, j, :],
                                                    w[0:n, j, cols], start=(j == 0), stop=(j == NA))
                    last.then_inc(main_ready, 1)

                def running_sum(b, first=False, ahead=3):
                    pe.wait_ge(q2_ready, b + ahead)
                    pe.wait_ge(inc_ready, 2 * b + 2)
                    if not first:
                        pe.wait_ge(h_done, b)
                    nc.tensor.matmul(h_ps[:, 0, :], upto[:, 0:P], inc[:, 0, :], start=True, stop=True)
                    nc.tensor.matmul(h_ps[:, 1, :], upto[:, P:T], inc[:, 0, :], start=True, stop=False)
                    nc.tensor.matmul(h_ps[:, 1, :], upto[:, 0:P], inc[:, 1, :], start=False,
                                     stop=True).then_inc(h_ready, 1)

                pe.wait_ge(v_ready, 1)
                e1 = e1_ps[:, 0:NT * C].rearrange("p (b s c) -> p b s c", b=B, s=2)
                nc.tensor.matmul(e1[:, :, 0, :], after[:, 0:P], v[:, :, 0, :], start=True, stop=False,
                                 skip_group_check=True)
                nc.tensor.matmul(e1[:, :, 1, :], after[:, P:T], v[:, :, 0, :], start=False, stop=False,
                                 skip_group_check=True)
                nc.tensor.matmul(e1[:, :, 1, :], after[:, 0:P], v[:, :, 1, :], start=False,
                                 stop=True, skip_group_check=True).then_inc(e1_ready, 1)
                pe.wait_ge(pre_ready, 1)
                level2(0, first=True)
                level3(0, first=True)
                pe.wait_ge(w_in, 16 * (NA + 2))
                level2(1, first=True)
                main(0, 0, first=True)
                level3(1)
                main(0, 1, first=True)
                level2(2, first=True)
                main(1, 0)
                running_sum(0, first=True)
                level3(2)
                main(1, 1)
                with nc.tensor.Fori(2, B - 1) as b:
                    level2(b + 1)
                    main(b, 0)
                    running_sum(b - 1)
                    level3(b + 1)
                    main(b, 1)
                main(B - 1, 0)
                running_sum(B - 2, ahead=2)
                main(B - 1, 1)
                running_sum(B - 1, ahead=1)


def norm_factors(nc, stats, mean, rstd, stage):
    with Bench(nc, stage) as m:
        spread = m.sb("spread", [P, NT])
        var = m.sb("var", [P, NT])
        vec, var_ready, std_ready = m.sem("vec"), m.sem("var_ready"), m.sem("std_ready")
        mean_e, m2_e, mean_o, m2_o = (stats[:, :, k] for k in (1, 2, 4, 5))
        with nc.Block() as block:
            @block.vector
            def _(dve):
                link = Chain(dve, vec)
                link(nc.vector.tensor_tensor(mean[:], mean_e, mean_o, ALU.add))
                link(nc.vector.tensor_scalar(mean[:], mean[:], 0.5, None, ALU.mult))
                link(nc.vector.tensor_tensor(spread[:], mean_e, mean_o, ALU.subtract))
                link(nc.vector.scalar_tensor_tensor(spread[:], spread[:], 0.25, spread[:],
                                                    ALU.mult, ALU.mult))
                link(nc.vector.tensor_tensor(var[:], m2_e, m2_o, ALU.add))
                link(nc.vector.scalar_tensor_tensor(var[:], var[:], 1.0 / D, spread[:],
                                                    ALU.mult, ALU.add))
                nc.vector.tensor_scalar(var[:], var[:], EPS, None, ALU.add).then_inc(var_ready, 1)
                dve.wait_ge(std_ready, 1)
                nc.vector.reciprocal(rstd[:], var[:])

            @block.scalar
            def _(act):
                act.wait_ge(var_ready, 1)
                nc.scalar.activation(var[:], var[:], ACT.Sqrt).then_inc(std_ready, 1)


def one_tile(t, n):
    return t[:, bass.ds(n, 1), :].rearrange("p n k -> p (n k)")


def one_column(t, n):
    return t[:, bass.ds(n, 1)]


def normalise(nc, out, h, mean, rstd, n):
    return nc.vector.tensor_scalar(out, one_tile(h, n), one_column(mean, n), one_column(rstd, n),
                                   ALU.subtract, ALU.mult)


def fuzzy_attention(nc, K, h, mean, rstd, stats, wq, bq, wk, bk):
    ident = K["ident"]
    INV = 1.0 / 0.3
    with Bench(nc, "fuz") as m:
        wq_sb, wk_sb = m.sb("wq", [P, D]), m.sb("wk", [P, D])
        bq_sb, bk_sb = m.sb("bq", [P, 1]), m.sb("bk", [P, 1])
        x = [m.sb(f"x{j}", [P, 2, D]) for j in range(G)]
        xT = [m.sb(f"xT{j}", [P, T]) for j in range(G)]
        qT = [m.sb(f"qT{j}", [P, T]) for j in range(G)]
        kT = [m.sb(f"kT{j}", [P, T]) for j in range(G)]
        e = [m.sb(f"e{j}", [P, 2, T]) for j in range(G)]
        fall = [m.sb(f"fall{j}", [P, 2, T]) for j in range(G)]
        f = [m.sb(f"f{j}", [P, 2, T]) for j in range(G)]
        fT = [m.sb(f"fT{j}", [P, 2, T]) for j in range(G)]
        neg_max = [m.sb(f"neg_max{j}", [P, 2]) for j in range(G)]
        total = [m.sb(f"total{j}", [P, 2]) for j in range(G)]
        inv = [m.sb(f"inv{j}", [P, 2]) for j in range(G)]
        rise_by = [m.sb(f"rise_by{j}", [P, 2]) for j in range(G)]
        fall_by = [m.sb(f"fall_by{j}", [P, 2]) for j in range(G)]
        pa = [m.ps(f"pa{j}", [P, 2, T]) for j in range(G)]
        pb = [m.ps(f"pb{j}", [P, 2, T]) for j in range(G)]
        w_in, zeroed = m.sem("w_in"), m.sem("zeroed")
        (x_ready, xT_ps, xT_ready, qk_ps, qk_ready, score_ps, max_ready, e_ready, inv_ready, by_ready,
         fall_ready, f_ready, fT_ps, fT_ready, out_ps, h_ready) = (m.sem(n) for n in (
             "x_ready xT_ps xT_ready qk_ps qk_ready score_ps max_ready e_ready inv_ready by_ready "
             "fall_ready f_ready fT_ps fT_ready out_ps h_ready").split())

        with nc.Block() as block:
            @block.sync
            def _(sp):
                for dst, src in ((wq_sb, wq), (wk_sb, wk), (bq_sb, bq), (bk_sb, bk)):
                    sp.dma_start(dst[:], src).then_inc(w_in, 16)
                sp.wait_ge(w_in, 64)

            @block.vector
            def _(dve):
                for j in range(G):
                    nc.vector.memset(f[j][:, :, L:T], 0.0)
                with nc.vector.Fori(0, B // G) as i:
                    for j in range(G):
                        b = i * G + j
                        nc.vector.tensor_scalar(x[j][:, 0, :], one_tile(h, 2 * b), one_column(mean, 2 * b),
                                                one_column(rstd, 2 * b), ALU.subtract, ALU.mult)
                        normalise(nc, x[j][:, 1, :], h, mean, rstd, 2 * b + 1).then_inc(x_ready, 1)
                    for j in range(G):
                        dve.wait_ge(score_ps, i * G + j + 1)
                        nc.vector.tensor_reduce(neg_max[j][:], pa[j][:, :, 0:L], AX.X, ALU.max,
                                                negate=True).then_inc(max_ready, 1)
                    for j in range(G):
                        dve.wait_ge(e_ready, i * G + j + 1)
                        nc.vector.reciprocal(inv[j][:], total[j][:]).then_inc(inv_ready, 1)
                        dve.wait_ge(inv_ready, i * G + j + 1)
                        nc.vector.tensor_scalar(rise_by[j][:], inv[j][:], INV, None, ALU.mult)
                        nc.vector.tensor_scalar(fall_by[j][:], inv[j][:], -INV, None, ALU.mult)\
                            .then_inc(by_ready, 1)
                    for j in range(G):
                        dve.wait_ge(fall_ready, i * G + j + 1)
                        for s in range(2):
                            last = nc.vector.scalar_tensor_tensor(
                                f[j][:, s, 0:L], e[j][:, s, 0:L], rise_by[j][:, s:s + 1],
                                fall[j][:, s, 0:L], ALU.mult, ALU.min)
                        last.then_inc(f_ready, 1)
                    for j in range(G):
                        b = i * G + j
                        dve.wait_ge(out_ps, b + 1)
                        hb = h[:, bass.ds(2 * b, 2), :]
                        nc.vector.tensor_tensor(hb, hb, pa[j][:, :, 0:D], ALU.add).then_inc(h_ready, 1)
                        dve.wait_ge(h_ready, b + 1)
                        for s in range(2):
                            nc.vector.bn_stats(one_tile(stats, 2 * b + s), one_tile(h, 2 * b + s))

            @block.scalar
            def _(act):
                act.wait_ge(w_in, 64)
                with nc.scalar.Fori(0, B // G) as i:
                    for j in range(G):
                        act.wait_ge(xT_ps, i * G + j + 1)
                        nc.scalar.activation(xT[j][:], pa[j][:, 0, :], ACT.Copy).then_inc(xT_ready, 1)
                    for j in range(G):
                        act.wait_ge(qk_ps, i * G + j + 1)
                        nc.scalar.activation(qT[j][:], pb[j][:, 0, :], ACT.Identity, bias=bq_sb[:])
                        nc.scalar.activation(kT[j][:], pb[j][:, 1, :], ACT.Identity, bias=bk_sb[:])\
                            .then_inc(qk_ready, 1)
                    for j in range(G):
                        act.wait_ge(max_ready, i * G + j + 1)
                        for s in range(2):
                            last = nc.scalar.activation(e[j][:, s, 0:L], pa[j][:, s, 0:L], ACT.Exp,
                                                        bias=neg_max[j][:, s:s + 1],
                                                        accum_out=total[j][:, s:s + 1])
                        last.then_inc(e_ready, 1)
                    for j in range(G):
                        act.wait_ge(by_ready, i * G + j + 1)
                        for s in range(2):
                            last = nc.scalar.activation(fall[j][:, s, 0:L], e[j][:, s, 0:L], ACT.Relu,
                                                        bias=K["inv03"][:], scale=fall_by[j][:, s:s + 1])
                        last.then_inc(fall_ready, 1)
                    for j in range(G):
                        act.wait_ge(fT_ps, i * G + j + 1)
                        nc.scalar.activation(fT[j][:], pb[j][:], ACT.Copy).then_inc(fT_ready, 1)

            @block.tensor
            def _(pe):
                pe.wait_ge(w_in, 64)
                with nc.tensor.Fori(0, B // G) as i:
                    for j in range(G):
                        pe.wait_ge(x_ready, i * G + j + 1)
                        for s in range(2):
                            last = nc.tensor.transpose(pa[j][:, 0, s * P:(s + 1) * P], x[j][:, s, :], ident[:])
                        last.then_inc(xT_ps, 1)
                    for j in range(G):
                        pe.wait_ge(xT_ready, i * G + j + 1)
                        nc.tensor.matmul(pb[j][:, 0, :], wq_sb[:], xT[j][:], start=True, stop=True)
                        nc.tensor.matmul(pb[j][:, 1, :], wk_sb[:], xT[j][:], start=True, stop=True)\
                            .then_inc(qk_ps, 1)
                    for j in range(G):
                        pe.wait_ge(qk_ready, i * G + j + 1)
                        for s in range(2):
                            last = nc.tensor.matmul(pa[j][:, s, 0:L], qT[j][:, s * P:(s + 1) * P],
                                                    kT[j][:, 0:L], start=True, stop=True)
                        last.then_inc(score_ps, 1)
                    for j in range(G):
                        pe.wait_ge(f_ready, i * G + j + 1)
                        for s in range(2):
                            for t in range(2):
                                last = nc.tensor.transpose(pb[j][:, t, s * P:(s + 1) * P],
                                                           f[j][:, s, t * P:(t + 1) * P], ident[:])
                        last.then_inc(fT_ps, 1)
                    for j in range(G):
                        pe.wait_ge(fT_ready, i * G + j + 1)
                        for s in range(2):
                            for t in range(2):
                                last = nc.tensor.matmul(pa[j][:, s, 0:D], fT[j][:, t, s * P:(s + 1) * P],
                                                        x[j][:, t, :], start=(t == 0), stop=(t == 1))
                        last.then_inc(out_ps, 1)


E0, HID0 = 8, 512
ST0 = (B * L + E0 * (P - 1)) // P + 1
ST0 += -ST0 % G
E1N, HID1, CAP, TOPK1 = 64, 64, 256, 2
SLOTS0, SLOTS1 = ST0 * P, E1N * CAP
SLOTS = max(SLOTS0, SLOTS1)


CLEARS = SLOTS // (16 * P) + 2


def clear_slots(x_slots, results, zeros, cleared, eng):
    n = zeros.shape[1] // D
    for r in range(0, SLOTS, P * n):
        eng.dma_start(x_slots[r:r + P * n, :].rearrange("(p n) d -> p (n d)", p=P), zeros[:])\
            .then_inc(cleared, 16)
    for y_slots, rows in results:
        eng.dma_start(y_slots[rows:rows + 1, :], zeros[0:1, 0:D]).then_inc(cleared, 16)


def router_logits(nc, K, h, mean, rstd, logits, gate, gate_bias, n_exp, stage):
    ident = K["ident"]
    with Bench(nc, stage) as m:
        gate_sb = m.sb("gate", [P, n_exp])
        bias = m.sb("bias", [P, n_exp])
        x = [m.sb(f"x{j}", [P, D]) for j in range(G)]
        xT = [m.sb(f"xT{j}", [P, P]) for j in range(G)]
        pt = [m.ps(f"pt{j}", [P, 512]) for j in range(G)]
        pl = [m.ps(f"pl{j}", [P, 512]) for j in range(G)]
        w_in, x_ready, xT_ps, xT_ready, logit_ps, read = (m.sem(n) for n in (
            "w_in", "x_ready", "xT_ps", "xT_ready", "logit_ps", "read"))
        loads = 1 if gate_bias is None else 2
        with nc.Block() as block:
            @block.sync
            def _(sp):
                sp.dma_start(gate_sb[:], gate).then_inc(w_in, 16)
                if gate_bias is not None:
                    sp.dma_start(bias[:], gate_bias.partition_broadcast(P)).then_inc(w_in, 16)
                sp.wait_ge(w_in, 16 * loads)

            @block.vector
            def _(dve):
                dve.wait_ge(w_in, 16 * loads)
                with nc.vector.Fori(0, NT // G) as i:
                    for j in range(G):
                        normalise(nc, x[j][:], h, mean, rstd, i * G + j).then_inc(x_ready, 1)
                    for j in range(G):
                        dve.wait_ge(logit_ps, i * G + j + 1)
                        to, src = one_tile(logits, i * G + j), pl[j][:, 0:n_exp]
                        if gate_bias is None:
                            nc.vector.tensor_copy(to, src).then_inc(read, 1)
                        else:
                            nc.vector.tensor_tensor(to, src, bias[:], ALU.add).then_inc(read, 1)

            @block.scalar
            def _(act):
                with nc.scalar.Fori(0, NT // G) as i:
                    for j in range(G):
                        act.wait_ge(xT_ps, i * G + j + 1)
                        nc.scalar.activation(xT[j][:], pt[j][:, 0:P], ACT.Copy).then_inc(xT_ready, 1)

            @block.tensor
            def _(pe):
                pe.wait_ge(w_in, 16 * loads)
                with nc.tensor.Fori(0, NT // G) as i:
                    for j in range(G):
                        pe.wait_ge(x_ready, i * G + j + 1)
                        nc.tensor.transpose(pt[j][:, 0:P], x[j][:], ident[:]).then_inc(xT_ps, 1)
                    for j in range(G):
                        pe.wait_ge(xT_ready, i * G + j + 1)
                        nc.tensor.matmul(pl[j][:, 0:n_exp], xT[j][:], gate_sb[:], start=True,
                                         stop=True).then_inc(logit_ps, 1)


def route_top1(nc, K, logits, scatter_at, gather_at, tile_expert):
    wide = [P, NT, E0]
    with Bench(nc, "route0") as m:
        best, first, slot = m.sb("best", [P, NT]), m.sb("first", [P, NT]), m.sb("slot", [P, NT])
        work, onehot = m.sb("work", wide), m.sb("onehot", wide)
        onehot_b = m.sb("onehot_b", wide, BF16)
        total = m.sb("total", wide)
        runs = [m.sb(f"run{k}", wide) for k in range(2)]
        ends = [m.sb(f"ends{k}", [P, E0]) for k in range(2)]
        n_tiles, starts = m.sb("n_tiles", [P, E0]), m.sb("starts", [P, E0])
        more = m.sb("more", [P, E0, NT])
        past = m.sb("past", [P, ST0, E0])
        expert_f = m.sb("expert_f", [P, ST0])
        within_ps, total_ps = m.ps("within_ps", wide), m.ps("total_ps", wide)
        vec, onehot_ready, counted = m.sem("vec"), m.sem("onehot_ready"), m.sem("counted")
        with nc.Block() as block:
            @block.vector
            def _(dve):
                link = Chain(dve, vec)
                rank = K["rank0"][:].unsqueeze(1).to_broadcast(wide)
                link(nc.vector.tensor_reduce(best[:], logits[:], AX.X, ALU.max))
                link(nc.vector.tensor_tensor(work[:], logits[:], best[:].unsqueeze(2).to_broadcast(wide),
                                             ALU.is_equal))
                link(nc.vector.tensor_tensor(work[:], work[:], rank, ALU.mult))
                link(nc.vector.tensor_reduce(first[:], work[:], AX.X, ALU.max))
                link(nc.vector.tensor_tensor(work[:], rank, first[:].unsqueeze(2).to_broadcast(wide),
                                             ALU.is_equal))
                link(nc.vector.tensor_tensor(onehot[:], work[:],
                                             K["real"][:].unsqueeze(2).to_broadcast(wide), ALU.mult))
                nc.vector.tensor_copy(onehot_b[:], onehot[:]).then_inc(onehot_ready, 1)
                dve.wait_ge(counted, 1)
                link(nc.vector.tensor_copy(total[:], total_ps[:]))
                now, then = total, runs[0]
                k = 1
                flip = 0
                while k < NT:
                    then = runs[flip]
                    nc.vector.tensor_copy(then[:, 0:k], now[:, 0:k])
                    link(nc.vector.tensor_tensor(then[:, k:NT], now[:, k:NT], now[:, 0:NT - k], ALU.add))
                    now, flip, k = then, 1 - flip, 2 * k
                count = now[:, NT - 1, :]
                link(nc.vector.tensor_tensor(more[:], count.unsqueeze(2).to_broadcast([P, E0, NT]),
                                             K["multiples"][:].unsqueeze(1).to_broadcast([P, E0, NT]),
                                             ALU.is_gt))
                link(nc.vector.tensor_reduce(n_tiles[:], more[:], AX.X, ALU.add))
                upto, k, flip2 = n_tiles, 1, 0
                while k < E0:
                    nxt = ends[flip2]
                    nc.vector.tensor_copy(nxt[:, 0:k], upto[:, 0:k])
                    link(nc.vector.tensor_tensor(nxt[:, k:E0], upto[:, k:E0], upto[:, 0:E0 - k], ALU.add))
                    upto, flip2, k = nxt, 1 - flip2, 2 * k
                link(nc.vector.tensor_tensor(starts[:], upto[:], n_tiles[:], ALU.subtract))
                link(nc.vector.tensor_scalar(starts[:], starts[:], float(P), None, ALU.mult))
                link(nc.vector.tensor_tensor(past[:], K["tile_no"][:, 0:ST0].unsqueeze(2).to_broadcast([P, ST0, E0]),
                                             upto[:].unsqueeze(1).to_broadcast([P, ST0, E0]), ALU.is_ge))
                link(nc.vector.tensor_reduce(expert_f[:], past[:], AX.X, ALU.add))
                nc.vector.tensor_scalar(tile_expert[:], expert_f[:], float(E0 - 1), None, ALU.min)
                link(nc.vector.tensor_tensor(work[:], now[:], total[:], ALU.subtract))
                link(nc.vector.tensor_tensor(work[:], work[:], within_ps[:], ALU.add))
                link(nc.vector.tensor_tensor(work[:], work[:], starts[:].unsqueeze(1).to_broadcast(wide), ALU.add))
                link(nc.vector.tensor_tensor(work[:], work[:], onehot[:], ALU.mult))
                link(nc.vector.tensor_reduce(slot[:], work[:], AX.X, ALU.add))
                nc.vector.tensor_tensor(scatter_at[:, 0, :], slot[:], K["pad_to"][:], ALU.add)
                nc.vector.tensor_tensor(gather_at[:, 0, :], slot[:], K["pad_from"][:], ALU.add)

            @block.tensor
            def _(pe):
                pe.wait_ge(onehot_ready, 1)
                nc.tensor.matmul(within_ps[:], K["after_b"][:], onehot_b[:], start=True, stop=True)
                nc.tensor.matmul(total_ps[:], K["ones_b"][:], onehot_b[:], start=True, stop=True)\
                    .then_inc(counted, 1)


def scatter_rows(nc, h, mean, rstd, x_slots, scatter_at, n_to, stage):
    with Bench(nc, stage) as m:
        x = [m.sb(f"x{j}", [P, D]) for j in range(G)]
        tick = m.sb("tick", [P, 2])
        at = [m.sb(f"at{j}", [P, n_to], U32) for j in range(G)]
        x_ready, tick_ready = m.sem("x_ready"), m.sem("tick_ready")
        sent = [m.sem(f"sent{j}") for j in range(G)]
        with nc.Block() as block:
            @block.vector
            def _(dve):
                def rows(i, first=False):
                    for j in range(G):
                        if not first:
                            dve.wait_ge(sent[j], 16 * n_to * i)
                        nc.vector.tensor_copy(at[j][:].unsqueeze(2), scatter_at[:, 0:n_to, bass.ds(i * G + j, 1)])
                        normalise(nc, x[j][:], h, mean, rstd, i * G + j).then_inc(x_ready, 1)

                rows(0, first=True)
                with nc.vector.Fori(1, NT // G) as i:
                    rows(i)

            @block.gpsimd
            def _(pool):
                nc.gpsimd.memset(tick[:], 0.0).then_inc(tick_ready, 1)
                pool.wait_ge(tick_ready, 1)
                with nc.gpsimd.Fori(0, NT // G) as i:
                    for j in range(G):
                        pool.wait_ge(tick_ready, i * G + j + 1)
                        pool.wait_ge(x_ready, i * G + j + 1)
                        nc.gpsimd.tensor_tensor(tick[:, 1:2], tick[:, 0:1], tick[:, 0:1], ALU.mult)\
                            .then_inc(tick_ready, 1)
                        for k in range(n_to):
                            nc.gpsimd.indirect_dma_start(
                                x_slots[:], bass.IndirectOffsetOnAxis(ap=at[j][:, k:k + 1], axis=0),
                                x[j][:], None).then_inc(sent[j], 16)
                for j in range(G):
                    pool.wait_ge(sent[j], 16 * n_to * (NT // G))


def gather_rows(nc, h, stats, y_slots, gather_at, weight, n_from, stage):
    with Bench(nc, stage) as m:
        y = [m.sb(f"y{j}", [P, n_from, D]) for j in range(2 * G)]
        tick = m.sb("tick", [P, 2])
        at = [m.sb(f"at{j}", [P, n_from], U32) for j in range(2 * G)]
        at_ready, h_ready, tick_ready = m.sem("at_ready"), m.sem("h_ready"), m.sem("tick_ready")
        got = [m.sem(f"got{j}") for j in range(2 * G)]
        W = 2 * G
        with nc.Block() as block:
            @block.vector
            def _(dve):
                def indices(i, j):
                    nc.vector.tensor_copy(at[j][:].unsqueeze(2), gather_at[:, 0:n_from, bass.ds(i * W + j, 1)])\
                        .then_inc(at_ready, 1)

                def add(i, j):
                    dve.wait_ge(got[j], 16 * n_from * (i + 1))
                    n = i * W + j
                    for k in range(n_from):
                        ht = one_tile(h, n)
                        if weight is None:
                            nc.vector.tensor_tensor(ht, ht, y[j][:, k, :], ALU.add).then_inc(h_ready, 1)
                        else:
                            nc.vector.scalar_tensor_tensor(ht, y[j][:, k, :], one_column(weight[k], n), ht,
                                                           ALU.mult, ALU.add).then_inc(h_ready, 1)
                        dve.wait_ge(h_ready, n_from * n + k + 1)
                    if stats is not None:
                        nc.vector.bn_stats(one_tile(stats, n), one_tile(h, n))

                for j in range(W):
                    indices(0, j)
                with nc.vector.Fori(0, NT // W - 1) as i:
                    for j in range(W):
                        add(i, j)
                        indices(i + 1, j)
                for j in range(W):
                    add(NT // W - 1, j)

            @block.gpsimd
            def _(pool):
                nc.gpsimd.memset(tick[:], 0.0).then_inc(tick_ready, 1)
                pool.wait_ge(tick_ready, 1)
                with nc.gpsimd.Fori(0, NT // W) as i:
                    for j in range(W):
                        pool.wait_ge(tick_ready, i * W + j + 1)
                        pool.wait_ge(at_ready, i * W + j + 1)
                        nc.gpsimd.tensor_tensor(tick[:, 1:2], tick[:, 0:1], tick[:, 0:1], ALU.mult)\
                            .then_inc(tick_ready, 1)
                        for k in range(n_from):
                            nc.gpsimd.indirect_dma_start(
                                y[j][:, k, :], None, y_slots[:],
                                bass.IndirectOffsetOnAxis(ap=at[j][:, k:k + 1], axis=0)).then_inc(got[j], 16)


def experts_top1(nc, K, x_slots, y_slots, tile_expert, w1, w2, b2):
    ident = K["ident"]
    HC = HID0 // P
    WIDE = HID0 + HC
    with Bench(nc, "exp0") as m:
        w1_sb = m.sb("w1", [P, E0, WIDE])
        w2_sb = m.sb("w2", [P, E0, HC * D])
        b2_sb = m.sb("b2", [P, E0, D])
        w1j = [m.sb(f"w1_{j}", [P, WIDE]) for j in range(G)]
        w2j = [m.sb(f"w2_{j}", [P, HC * D]) for j in range(G)]
        x = [m.sb(f"x{j}", [P, D]) for j in range(G)]
        xT = [m.sb(f"xT{j}", [P, P]) for j in range(G)]
        hid = [m.sb(f"hid{j}", [P, HC, P]) for j in range(G)]
        y = [m.sb(f"y{j}", [P, D]) for j in range(G)]
        pa = [m.ps(f"pa{j}", [P, 512]) for j in range(G)]
        pb = [m.ps(f"pb{j}", [P, HC, P]) for j in range(G)]
        w_in = m.sem("w_in")
        x_in = [m.sem(f"x_in{j}") for j in range(G)]
        y_out = [m.sem(f"y_out{j}") for j in range(G)]
        xT_ps, xT_ready, w1_ready, w2_ready, hid_ps, hid_a, hid_v, y_ps, y_ready = (m.sem(n) for n in (
            "xT_ps xT_ready w1_ready w2_ready hid_ps hid_a hid_v y_ps y_ready").split())
        N = ST0 // G
        with nc.Block() as block:
            @block.sync
            def _(sp):
                def rows(n):
                    return x_slots[bass.ds(n * P, P), :]

                for j in range(G):
                    sp.dma_start(x[j][:], rows(j)).then_inc(x_in[j], 16)
                sp.dma_start(w1_sb[:], w1).then_inc(w_in, 16)
                sp.dma_start(w2_sb[:], w2).then_inc(w_in, 16)
                sp.dma_start(b2_sb[:].rearrange("p e d -> p (e d)"),
                             b2.partition_broadcast(P)).then_inc(w_in, 16)

                def store(i):
                    for j in range(G):
                        sp.wait_ge(y_ready, i * G + j + 1)
                        sp.dma_start(y_slots[bass.ds((i * G + j) * P, P), :], y[j][:]).then_inc(y_out[j], 16)

                with nc.sync.Fori(0, N - 1) as i:
                    for j in range(G):
                        sp.wait_ge(xT_ps, i * G + j + 1)
                        sp.dma_start(x[j][:], rows((i + 1) * G + j)).then_inc(x_in[j], 16)
                    store(i)
                store(N - 1)
                sp.wait_ge(w_in, 48)
                for j in range(G):
                    sp.wait_ge(y_out[j], 16 * N)

            @block.vector
            def _(dve):
                dve.wait_ge(w_in, 48)

                def expert(n):
                    return nc.vector.value_load(tile_expert[0:1, bass.ds(n, 1)], min_val=0, max_val=E0 - 1)

                def pass_(i, first=False):
                    for j in range(G):
                        ex = expert(i * G + j)
                        if not first:
                            dve.wait_ge(hid_ps, i * G + j + 1 - G)
                            dve.wait_ge(hid_a, i * G + j + 1 - G)
                            dve.wait_ge(hid_v, i * G + j + 1 - G)
                        nc.vector.tensor_copy(w1j[j][:], w1_sb[:, bass.ds(ex, 1), :].rearrange("p a n -> p (a n)"))\
                            .then_inc(w1_ready, 1)
                    for j in range(G):
                        dve.wait_ge(hid_a, i * G + j + 1)
                        for c in range(HC // 2, HC):
                            last = nc.vector.tensor_scalar(hid[j][:, c, :], pb[j][:, c, :],
                                                           w1j[j][:, HID0 + c:HID0 + c + 1], 0.0,
                                                           ALU.add, ALU.max)
                        last.then_inc(hid_v, 1)
                    for j in range(G):
                        ex = expert(i * G + j)
                        dve.wait_ge(y_ps, i * G + j + 1)
                        if not first:
                            dve.wait_ge(y_out[j], 16 * i)
                        nc.vector.tensor_tensor(y[j][:], pa[j][:, P:2 * P],
                                                b2_sb[:, bass.ds(ex, 1), :].rearrange("p a n -> p (a n)"),
                                                ALU.add).then_inc(y_ready, 1)

                pass_(0, first=True)
                with nc.vector.Fori(1, N) as i:
                    pass_(i)

            @block.scalar
            def _(act):
                act.wait_ge(w_in, 48)

                def pass_(i, first=False):
                    for j in range(G):
                        act.wait_ge(xT_ps, i * G + j + 1)
                        nc.scalar.activation(xT[j][:], pa[j][:, 0:P], ACT.Copy).then_inc(xT_ready, 1)
                    for j in range(G):
                        ex = nc.scalar.value_load(tile_expert[0:1, bass.ds(i * G + j, 1)],
                                                  min_val=0, max_val=E0 - 1)
                        nc.scalar.activation(w2j[j][:], w2_sb[:, bass.ds(ex, 1), :].rearrange("p a n -> p (a n)"),
                                             ACT.Copy).then_inc(w2_ready, 1)
                    for j in range(G):
                        act.wait_ge(hid_ps, i * G + j + 1)
                        for c in range(HC // 2):
                            last = nc.scalar.activation(hid[j][:, c, :], pb[j][:, c, :], ACT.Relu,
                                                        bias=w1j[j][:, HID0 + c:HID0 + c + 1])
                        last.then_inc(hid_a, 1)

                with nc.scalar.Fori(0, N) as i:
                    pass_(i)

            @block.tensor
            def _(pe):
                def pass_(i, first=False):
                    for j in range(G):
                        pe.wait_ge(x_in[j], 16 * (i + 1))
                        if not first:
                            pe.wait_ge(y_ready, i * G + j + 1 - G)
                        nc.tensor.transpose(pa[j][:, 0:P], x[j][:], ident[:]).then_inc(xT_ps, 1)
                    for j in range(G):
                        pe.wait_ge(xT_ready, i * G + j + 1)
                        pe.wait_ge(w1_ready, i * G + j + 1)
                        for c in range(HC):
                            last = nc.tensor.matmul(pb[j][:, c, :], w1j[j][:, c * P:(c + 1) * P], xT[j][:],
                                                    start=True, stop=True)
                        last.then_inc(hid_ps, 1)
                    for j in range(G):
                        pe.wait_ge(hid_v, i * G + j + 1)
                        pe.wait_ge(w2_ready, i * G + j + 1)
                        for c in range(HC):
                            last = nc.tensor.matmul(pa[j][:, P:2 * P], hid[j][:, c, :],
                                                    w2j[j][:, c * D:(c + 1) * D],
                                                    start=(c == 0), stop=(c == HC - 1))
                        last.then_inc(y_ps, 1)

                pass_(0, first=True)
                with nc.tensor.Fori(1, N) as i:
                    pass_(i)


H, HD, MAX_REL = 8, 16, 68
HALF = 8
BQ = 2 * HALF
NBLK = T // BQ
GB = 4
NGRP = NBLK // GB
REACH = MAX_REL - 1
KWIN = 2 * REACH + BQ + HALF
VWIN = P + T


def relative_attention(nc, K, h, mean, rstd, stats, wq, bq, wk, bk, wv, bv, wo, bo,
                       wq_rep, bq_rep, key_ends, key_table, value_table):
    SCALE = 1.0 / float(D) ** 0.5
    ident = K["ident"]
    with Bench(nc, "rel") as m:
        wq_sb, wk_sb, wv_sb, wo_sb = (m.sb(n, [P, D]) for n in ("wq", "wk", "wv", "wo"))
        bq_sb, bk_sb = m.sb("bq", [P, 1]), m.sb("bk", [P, 1])
        bv_sb, bo_sb = m.sb("bv", [P, D]), m.sb("bo", [P, D])
        wrep_sb, brep_sb = m.sb("wq_rep", [P, H, P]), m.sb("bq_rep", [P, H])
        ends_sb, kbias = m.sb("key_ends", [P, 2]), m.sb("kbias", [P, 3])
        ktab, vtab = m.sb("ktab", [P, KWIN]), m.sb("vtab", [P, VWIN, HD])
        x, xT, qT = m.sb("x", [P, 2, D]), m.sb("xT", [P, T]), m.sb("qT", [P, T])
        kT = [m.sb(f"kT{r}", [P, 3, T]) for r in range(2)]
        v = [m.sb(f"v{r}", [P, 2, D]) for r in range(2)]
        q_head = [m.sb(f"q_head{r}", [P, 2 * NBLK, H, HALF]) for r in range(2)]
        q_pos = [m.sb(f"q_pos{r}", [P, 2 * NBLK, H, HALF]) for r in range(2)]
        den = [m.sb(f"den{r}", [P, NBLK]) for r in range(2)]
        e = [m.sb(f"e{r}", [P, GB, T]) for r in range(2)]
        neg_max = [m.sb(f"neg_max{r}", [P, GB]) for r in range(2)]
        bias = [m.sb(f"bias{r}", [P, GB]) for r in range(2)]
        eT = m.sb("eT", [P, GB, 2, P])
        kept = m.sb("kept", [P, GB, 2 * D])
        o, o_norm, rden = m.sb("o", [P, NBLK, HD]), m.sb("o_norm", [P, NBLK, HD]), m.sb("rden", [P, NBLK])
        o_head = m.sb("o_head", [P, NBLK, H, HD])
        oT = m.sb("oT", [P, T])
        s_ps = m.ps("s_ps", [P, GB, T])
        t_ps = m.ps("t_ps", [P, GB, 2, P])
        pv_ps = m.ps("pv_ps", [P, GB, 2 * D])
        pa, pb = m.ps("pa", [P, 2, T]), m.ps("pb", [P, 2, T])
        (w_in, ready, vec, x_ready, xT_done, xT_ready, qk_done, q_ready, k_ready, qh_ready, qp_done,
         qp_ready, v_done, v_ready, s_done, max_ready, bias_ready, e_ready, t_done, eT_a, eT_v,
         pv_done, kept_ready, o_part, rden_ready, o_ready, oh_ready, oT_done, oT_ready, out_done,
         h_ready) = (m.sem(n) for n in (
             "w_in ready vec x_ready xT_done xT_ready qk_done q_ready k_ready qh_ready qp_done "
             "qp_ready v_done v_ready s_done max_ready bias_ready e_ready t_done eT_a eT_v "
             "pv_done kept_ready o_part rden_ready o_ready oh_ready oT_done oT_ready out_done "
             "h_ready").split())
        mask16, mask_pv, mask_row, sel_q = K["mask16"], K["mask_pv"], K["mask_row"], K["sel_q"]
        loads = [(wq_sb, wq), (wk_sb, wk), (bq_sb, bq), (bk_sb, bk), (ends_sb, key_ends),
                 (wrep_sb, wq_rep), (brep_sb, bq_rep), (wv_sb, wv), (bv_sb, bv.partition_broadcast(P)),
                 (ktab, key_table), (vtab, value_table), (wo_sb, wo), (bo_sb, bo.partition_broadcast(P))]

        def run(engine, slot, head, tail):
            def pair(i, first=False, last=False):
                for r in range(2):
                    for g in range(NGRP):
                        slot(2 * i + r, g, r, first and r == 0, last and r == 1)
            head()
            pair(0, first=True)
            with engine.Fori(1, B // 2 - 1) as i:
                pair(i)
            pair(B // 2 - 1, last=True)
            tail()

        with nc.Block() as block:
            @block.sync
            def _(sp):
                for dst, src in loads:
                    sp.dma_start(dst[:], src).then_inc(w_in, 16)
                sp.wait_ge(w_in, 16 * len(loads))

            @block.tensor
            def _(pe):
                def turn_x(b):
                    pe.wait_ge(x_ready, b + 1)
                    for s in range(2):
                        last = nc.tensor.transpose(pa[:, 0, s * P:(s + 1) * P], x[:, s, :], ident[:])
                    last.then_inc(xT_done, 1)

                def project_qk(b):
                    pe.wait_ge(xT_ready, b + 1)
                    nc.tensor.matmul(pa[:, 0, :], wq_sb[:], xT[:], start=True, stop=True)
                    nc.tensor.matmul(pa[:, 1, :], wk_sb[:], xT[:], start=True, stop=True).then_inc(qk_done, 1)

                def project_rest(b):
                    pe.wait_ge(q_ready, b + 1)
                    pe.wait_ge(k_ready, b + 1)
                    for c in range(H // 2):
                        if c >= 2:
                            pe.wait_ge(qp_ready, 4 * b + c - 1)
                        for n in range(2):
                            last = nc.tensor.matmul((pa, pb)[c % 2][:, n, :], wrep_sb[:, 2 * c + n, :], xT[:],
                                                    start=True, stop=True)
                        last.then_inc(qp_done, 1)
                    pe.wait_ge(qp_ready, 4 * b + 3)
                    for s in range(2):
                        last = nc.tensor.matmul(pa[:, 0, s * P:(s + 1) * P], xT[:, s * P:(s + 1) * P], wv_sb[:],
                                                start=True, stop=True)
                    last.then_inc(v_done, 1)

                def scores(b, g, r, first=False):
                    if g == 0:
                        pe.wait_ge(qh_ready, b + 1)
                        pe.wait_ge(qp_ready, 4 * b + 4)
                    if not first:
                        pe.wait_ge(e_ready, NGRP * b + g)
                    for n in range(GB):
                        blk = GB * g + n
                        q0 = BQ * blk
                        near = max(0, q0 - REACH), min(L, q0 + BQ + REACH)
                        stationary = q_head[r][:, 2 * blk:2 * blk + 2].rearrange("p a h i -> p (a h i)")
                        parts = [(0, near[0], near[1])]
                        if near[0] > 0:
                            parts.append((1, 0, near[0]))
                        if near[1] < L:
                            parts.append((2, near[1], L))
                        for k, (which, lo, hi) in enumerate(parts):
                            nc.tensor.matmul(s_ps[:, n, lo:hi], stationary, kT[r][:, which, lo:hi],
                                             start=(k == 0), stop=False, skip_group_check=True)
                        for a in range(2):
                            off = REACH + HALF - q0 - HALF * a
                            last = nc.tensor.matmul(
                                s_ps[64 * a:64 * a + 64, n, near[0]:near[1]],
                                q_pos[r][:, 2 * blk + a].rearrange("p h i -> p (h i)"),
                                ktab[:, near[0] + off:near[1] + off], start=False, stop=True,
                                skip_group_check=True)
                    last.then_inc(s_done, 1)

                def turn_e(b, g):
                    pe.wait_ge(e_ready, NGRP * b + g + 1)
                    for n in range(GB):
                        for t in range(2):
                            last = nc.tensor.transpose(t_ps[:, n, t, :], e[g % 2][:, n, t * P:(t + 1) * P], ident[:])
                    last.then_inc(t_done, 1)

                def values(b, g, r, first=False):
                    pe.wait_ge(eT_a, NGRP * b + g + 1)
                    pe.wait_ge(eT_v, NGRP * b + g + 1)
                    if g == 0:
                        pe.wait_ge(v_ready, b + 1)
                    if not first:
                        pe.wait_ge(kept_ready, NGRP * b + g)
                    for n in range(GB):
                        blk = GB * g + n
                        for t in range(2):
                            nc.tensor.matmul(pv_ps[:, n, 0:D], eT[:, n, t, :], v[r][:, t, :],
                                             start=(t == 0), stop=(t == 1), skip_group_check=True)
                        for a in range(2):
                            for t in range(2):
                                u = P + BQ * blk + HALF * a - P * t
                                last = nc.tensor.matmul(
                                    pv_ps[64 * a:64 * a + 64, n, D:2 * D], eT[:, n, t, 64 * a:64 * a + 64],
                                    vtab[:, u:u + HALF, :].rearrange("p u d -> p (u d)"),
                                    start=(t == 0), stop=(t == 1), skip_group_check=True)
                    last.then_inc(pv_done, 1)

                def turn_o(b):
                    pe.wait_ge(oh_ready, b + 1)
                    for blk in range(NBLK):
                        last = nc.tensor.matmul(pb[:, 0, BQ * blk:BQ * blk + BQ],
                                                o_head[:, blk].rearrange("p h d -> p (h d)"), sel_q[:],
                                                start=True, stop=True)
                    last.then_inc(oT_done, 1)

                def project_out(b):
                    pe.wait_ge(oT_ready, b + 1)
                    for s in range(2):
                        last = nc.tensor.matmul(pb[:, 0, s * P:(s + 1) * P], oT[:, s * P:(s + 1) * P], wo_sb[:],
                                                start=True, stop=True)
                    last.then_inc(out_done, 1)

                def slot(b, g, r, first, last):
                    turn_e(b, g)
                    if g + 1 < NGRP:
                        scores(b, g + 1, r)
                    elif not last:
                        scores(b + 1, 0, 1 - r)
                    if g == 0 and not last:
                        turn_x(b + 1)
                    if g == 1:
                        if not last:
                            project_qk(b + 1)
                        if not first:
                            turn_o(b - 1)
                    if g == 2:
                        if not first:
                            pe.wait_ge(oT_ready, b)
                        if not last:
                            project_rest(b + 1)
                        if not first:
                            if not last:
                                pe.wait_ge(qp_ready, 4 * b + 8)
                            project_out(b - 1)
                    if g == 3 and not first:
                        pe.wait_ge(h_ready, 2 * b - 1)
                    values(b, g, r, first and g == 0)

                def head():
                    pe.wait_ge(w_in, 16 * len(loads))
                    turn_x(0)
                    project_qk(0)
                    project_rest(0)
                    scores(0, 0, 0, first=True)

                def tail():
                    turn_o(B - 1)
                    project_out(B - 1)

                run(nc.tensor, slot, head, tail)

            @block.scalar
            def _(act):
                def read_x(b):
                    act.wait_ge(xT_done, b + 1)
                    nc.scalar.activation(xT[:], pa[:, 0, :], ACT.Copy).then_inc(xT_ready, 1)

                def read_qk(b, r):
                    act.wait_ge(qk_done, b + 1)
                    nc.scalar.activation(qT[:], pa[:, 0, :], ACT.Identity, bias=bq_sb[:]).then_inc(q_ready, 1)
                    for n in range(3):
                        last = nc.scalar.activation(kT[r][:, n, :], pa[:, 1, :], ACT.Identity,
                                                    bias=kbias[:, n:n + 1])
                    last.then_inc(k_ready, 1)

                def exps(b, g, r):
                    act.wait_ge(bias_ready, NGRP * b + g + 1)
                    for n in range(GB):
                        last = nc.scalar.activation(e[g % 2][:, n, 0:L], s_ps[:, n, 0:L], ACT.Exp,
                                                    bias=bias[g % 2][:, n:n + 1], scale=SCALE,
                                                    accum_out=den[r][:, GB * g + n:GB * g + n + 1])
                    last.then_inc(e_ready, 1)

                def read_eT(b, g):
                    act.wait_ge(t_done, NGRP * b + g + 1)
                    nc.scalar.activation(eT[:, 0:2], t_ps[:, 0:2], ACT.Copy).then_inc(eT_a, 1)

                def read_o(b):
                    act.wait_ge(oT_done, b + 1)
                    nc.scalar.activation(oT[:], pb[:, 0, :], ACT.Copy).then_inc(oT_ready, 1)

                def slot(b, g, r, first, last):
                    read_eT(b, g)
                    if g + 1 < NGRP:
                        exps(b, g + 1, r)
                    elif not last:
                        exps(b + 1, 0, 1 - r)
                    if g == 0 and not last:
                        read_x(b + 1)
                    if g == 1:
                        if not last:
                            read_qk(b + 1, 1 - r)
                        if not first:
                            read_o(b - 1)

                def head():
                    act.wait_ge(ready, 1)
                    read_x(0)
                    read_qk(0, 0)
                    exps(0, 0, 0)

                run(nc.scalar, slot, head, lambda: read_o(B - 1))

            @block.gpsimd
            def _(pool):
                def queries(b, r):
                    pool.wait_ge(q_ready, b + 1)
                    wide = [P, 2 * NBLK, H, HALF]
                    nc.gpsimd.tensor_tensor(
                        q_head[r][:], qT[:].rearrange("p (n i) -> p n i", i=HALF).unsqueeze(2).to_broadcast(wide),
                        mask16[:].unsqueeze(1).unsqueeze(3).to_broadcast(wide), ALU.mult).then_inc(qh_ready, 1)

                def heads(b):
                    pool.wait_ge(o_ready, b + 1)
                    wide = [P, NBLK, H, HD]
                    nc.gpsimd.tensor_tensor(
                        o_head[:], o_norm[:].unsqueeze(2).to_broadcast(wide),
                        mask_row[:].unsqueeze(1).unsqueeze(3).to_broadcast(wide), ALU.mult).then_inc(oh_ready, 1)

                def slot(b, g, r, first, last):
                    if g == 1 and not last:
                        queries(b + 1, 1 - r)
                    if g == 3:
                        heads(b)

                run(nc.gpsimd, slot, lambda: queries(0, 0), lambda: None)

            @block.vector
            def _(dve):
                def read_x(b):
                    normalise(nc, x[:, 0, :], h, mean, rstd, 2 * b)
                    normalise(nc, x[:, 1, :], h, mean, rstd, 2 * b + 1).then_inc(x_ready, 1)

                def read_rest(b, r):
                    for c in range(H // 2):
                        dve.wait_ge(qp_done, 4 * b + c + 1)
                        for n in range(2):
                            hd = 2 * c + n
                            last = nc.vector.scalar_tensor_tensor(
                                q_pos[r][:, :, hd, :],
                                (pa, pb)[c % 2][:, n, :].rearrange("p (n i) -> p n i", i=HALF),
                                brep_sb[:, hd:hd + 1],
                                mask16[:].unsqueeze(1).to_broadcast([P, 2 * NBLK, HALF]), ALU.add, ALU.mult)
                        last.then_inc(qp_ready, 1)
                    dve.wait_ge(v_done, b + 1)
                    nc.vector.tensor_tensor(v[r][:], pa[:, 0, :].rearrange("p (s d) -> p s d", s=2),
                                            bv_sb[:].unsqueeze(1).to_broadcast([P, 2, D]), ALU.add)\
                        .then_inc(v_ready, 1)

                def maxima(b, g):
                    dve.wait_ge(s_done, NGRP * b + g + 1)
                    nc.vector.tensor_reduce(neg_max[g % 2][:], s_ps[:, :, 0:L], AX.X, ALU.max, negate=True)\
                        .then_inc(max_ready, 1)
                    dve.wait_ge(max_ready, NGRP * b + g + 1)
                    nc.vector.tensor_scalar(bias[g % 2][:], neg_max[g % 2][:], SCALE, None, ALU.mult)\
                        .then_inc(bias_ready, 1)

                def read_eT(b, g):
                    dve.wait_ge(t_done, NGRP * b + g + 1)
                    nc.vector.tensor_copy(eT[:, 2:4], t_ps[:, 2:4]).then_inc(eT_v, 1)

                def keep(b, g, r, first):
                    dve.wait_ge(pv_done, NGRP * b + g + 1)
                    if not first:
                        dve.wait_ge(o_part, NGRP * b + g)
                        if g == 0:
                            dve.wait_ge(o_ready, b)
                    nc.vector.tensor_tensor(kept[:], pv_ps[:], mask_pv[:].unsqueeze(1).to_broadcast([P, GB, 2 * D]),
                                            ALU.mult).then_inc(kept_ready, 1)
                    dve.wait_ge(kept_ready, NGRP * b + g + 1)
                    nc.vector.tensor_reduce(o[:, GB * g:GB * g + GB, :],
                                            kept[:].rearrange("p n (k d) -> p n d k", d=HD), AX.X, ALU.add)\
                        .then_inc(o_part, 1)
                    if g == NGRP - 1:
                        nc.vector.reciprocal(rden[:], den[r][:]).then_inc(rden_ready, 1)
                        dve.wait_ge(rden_ready, b + 1)
                        dve.wait_ge(o_part, NGRP * b + NGRP)
                        nc.vector.tensor_tensor(o_norm[:], o[:], rden[:].unsqueeze(2).to_broadcast([P, NBLK, HD]),
                                                ALU.mult).then_inc(o_ready, 1)

                def add_out(b):
                    dve.wait_ge(out_done, b + 1)
                    hb = h[:, bass.ds(2 * b, 2), :]
                    nc.vector.tensor_tensor(hb, hb, pb[:, 0, :].rearrange("p (s d) -> p s d", s=2), ALU.add)\
                        .then_inc(h_ready, 1)
                    dve.wait_ge(h_ready, 2 * b + 1)
                    nc.vector.tensor_tensor(hb, hb, bo_sb[:].unsqueeze(1).to_broadcast([P, 2, D]), ALU.add)\
                        .then_inc(h_ready, 1)
                    dve.wait_ge(h_ready, 2 * b + 2)
                    for s in range(2):
                        nc.vector.bn_stats(one_tile(stats, 2 * b + s), one_tile(h, 2 * b + s))

                def slot(b, g, r, first, last):
                    if g == 0 and not last:
                        read_x(b + 1)
                    read_eT(b, g)
                    if g + 1 < NGRP:
                        maxima(b, g + 1)
                    elif not last:
                        maxima(b + 1, 0)
                    if g == 2:
                        if not last:
                            read_rest(b + 1, 1 - r)
                        if not first:
                            add_out(b - 1)
                    keep(b, g, r, first and g == 0)

                def head():
                    for r in range(2):
                        nc.vector.memset(e[r][:, :, L:T], 0.0)
                    dve.wait_ge(w_in, 16 * len(loads))
                    nc.vector.tensor_copy(kbias[:, 0:1], bk_sb[:])
                    nc.vector.tensor_tensor(kbias[:, 1:3], ends_sb[:], bk_sb[:].to_broadcast([P, 2]), ALU.add)\
                        .then_inc(ready, 1)
                    read_x(0)
                    read_rest(0, 0)
                    maxima(0, 0)

                run(nc.vector, slot, head, lambda: add_out(B - 1))


ROUTE_SCALE = 2.5


def route_top2(nc, K, logits, scatter_at, gather_at, weight):
    wide = [P, NT, E1N]
    CH = 512 // E1N
    with Bench(nc, "route1") as m:
        work, total = m.sb("work", wide), m.sb("total", wide)
        onehot = [m.sb(f"onehot{k}", wide) for k in range(TOPK1)]
        both = m.sb("both", wide, BF16)
        run = m.sb("run", wide)
        best, first = m.sb("best", [P, TOPK1, NT]), m.sb("first", [P, TOPK1, NT])
        place, valid = m.sb("place", [P, TOPK1, NT]), m.sb("valid", [P, TOPK1, NT])
        row, other = m.sb("row", [P, TOPK1, NT]), m.sb("other", [P, TOPK1, NT])
        sig, sums = m.sb("sig", [P, TOPK1, NT]), m.sb("sums", [P, NT])
        count_ps = m.ps("count_ps", wide)
        vec, both_ready, totals_done, totals_read, within_done = (m.sem(n) for n in (
            "vec", "both_ready", "totals_done", "totals_read", "within_done"))
        best_ready, sig_ready = m.sem("best_ready"), m.sem("sig_ready")
        with nc.Block() as block:
            @block.vector
            def _(dve):
                link = Chain(dve, vec)
                rank = K["rank1"][:].unsqueeze(1).to_broadcast(wide)
                real = K["real"][:].unsqueeze(2).to_broadcast(wide)
                values = logits
                for k in range(TOPK1):
                    link(nc.vector.tensor_reduce(best[:, k], values[:], AX.X, ALU.max))
                    link(nc.vector.tensor_tensor(work[:], values[:],
                                                 best[:, k].unsqueeze(2).to_broadcast(wide), ALU.is_equal))
                    link(nc.vector.tensor_tensor(work[:], work[:], rank, ALU.mult))
                    link(nc.vector.tensor_reduce(first[:, k], work[:], AX.X, ALU.max))
                    link(nc.vector.tensor_tensor(onehot[k][:], rank,
                                                 first[:, k].unsqueeze(2).to_broadcast(wide), ALU.is_equal))
                    if k == 0:
                        link(nc.vector.scalar_tensor_tensor(logits[:], onehot[0][:], -3.0e38, logits[:],
                                                            ALU.mult, ALU.add))
                nc.vector.memset(sums[:], 0.0).then_inc(best_ready, 1)
                link(nc.vector.tensor_tensor(work[:], onehot[0][:], onehot[1][:], ALU.add))
                nc.vector.tensor_tensor(both[:], work[:], real, ALU.mult).then_inc(both_ready, 1)
                dve.wait_ge(totals_done, 1)
                nc.vector.tensor_copy(total[:], count_ps[:]).then_inc(totals_read, 1)
                dve.wait_ge(totals_read, 1)
                now, then, k = total, run, 1
                spare = work
                while k < NT:
                    nc.vector.tensor_copy(then[:, 0:k], now[:, 0:k])
                    link(nc.vector.tensor_tensor(then[:, k:NT], now[:, k:NT], now[:, 0:NT - k], ALU.add))
                    now, then, k = then, (spare if then is run else run), 2 * k
                dve.wait_ge(within_done, 1)
                link(nc.vector.tensor_tensor(then[:], now[:], total[:], ALU.subtract))
                link(nc.vector.tensor_tensor(then[:], then[:], count_ps[:], ALU.add))
                for k in range(TOPK1):
                    link(nc.vector.tensor_tensor(onehot[k][:], onehot[k][:], then[:], ALU.mult))
                    link(nc.vector.tensor_reduce(place[:, k], onehot[k][:], AX.X, ALU.add))
                real2 = K["real"][:].unsqueeze(1).to_broadcast([P, TOPK1, NT])
                link(nc.vector.tensor_scalar(valid[:], place[:], float(CAP), None, ALU.is_lt))
                link(nc.vector.tensor_tensor(valid[:], valid[:], real2, ALU.mult))
                link(nc.vector.tensor_scalar(row[:], first[:], -float(CAP), float(CAP * E1N), ALU.mult, ALU.add))
                link(nc.vector.tensor_tensor(row[:], row[:], place[:], ALU.add))
                link(nc.vector.tensor_tensor(row[:], row[:], valid[:], ALU.mult))
                link(nc.vector.tensor_scalar(other[:], valid[:], -1.0, 1.0, ALU.mult, ALU.add))
                link(nc.vector.scalar_tensor_tensor(place[:], other[:], float(SLOTS1), row[:], ALU.mult, ALU.add))
                link(nc.vector.tensor_copy(gather_at[:], place[:]))
                link(nc.vector.tensor_tensor(other[:], other[:], K["spill"][:].rearrange("p (k n) -> p k n", k=TOPK1),
                                             ALU.mult))
                link(nc.vector.tensor_tensor(other[:], other[:], row[:], ALU.add))
                nc.vector.tensor_copy(scatter_at[:], other[:])
                dve.wait_ge(sig_ready, 1)
                link(nc.vector.tensor_tensor(sums[:], sig[:, 0], sig[:, 1], ALU.add))
                link(nc.vector.tensor_scalar(sums[:], sums[:], 1e-20, None, ALU.add))
                link(nc.vector.reciprocal(sums[:], sums[:]))
                link(nc.vector.tensor_tensor(sig[:], sig[:], sums[:].unsqueeze(1).to_broadcast([P, TOPK1, NT]),
                                             ALU.mult))
                link(nc.vector.scalar_tensor_tensor(weight[:], sig[:], ROUTE_SCALE, valid[:], ALU.mult, ALU.mult))

            @block.scalar
            def _(act):
                act.wait_ge(best_ready, 1)
                nc.scalar.activation(sig[:], best[:], ACT.Sigmoid).then_inc(sig_ready, 1)

            @block.tensor
            def _(pe):
                def count(ones):
                    for c in range(NT // CH):
                        last = nc.tensor.matmul(count_ps[:, CH * c:CH * c + CH, :], ones[:],
                                                both[:, CH * c:CH * c + CH, :], start=True, stop=True)
                    return last

                pe.wait_ge(both_ready, 1)
                count(K["ones_b"]).then_inc(totals_done, 1)
                pe.wait_ge(totals_read, 1)
                count(K["after_b"]).then_inc(within_done, 1)


def scatter_and_share(nc, K, h, mean, rstd, x_slots, scatter_at, sw1, sw3, sw2):
    ident = K["ident"]
    with Bench(nc, "share") as m:
        sw1_sb, sw3_sb, sw2_sb = m.sb("sw1", [P, P]), m.sb("sw3", [P, P]), m.sb("sw2", [P, D])
        x = [m.sb(f"x{j}", [P, D]) for j in range(2 * G)]
        tick = m.sb("tick", [P, 2])
        at = [m.sb(f"at{j}", [P, TOPK1], U32) for j in range(2 * G)]
        xT, gate, act1 = m.sb("xT", [P, G * P]), m.sb("gate", [P, G * P]), m.sb("act1", [P, G * P])
        pt, p1, p3, py = (m.ps(n, [P, G * P]) for n in ("pt", "p1", "p3", "py"))
        w_in, x_ready, tick_ready, xT_ps, xT_ready, up_done, gate_ready, half_ready, act_ready, y_done, h_ready = (
            m.sem(n) for n in "w_in x_ready tick_ready xT_ps xT_ready up_done gate_ready half_ready act_ready y_done h_ready".split())
        sent = [m.sem(f"sent{j}") for j in range(2 * G)]
        NG = NT // G
        with nc.Block() as block:
            @block.sync
            def _(sp):
                for dst, src in ((sw1_sb, sw1), (sw3_sb, sw3), (sw2_sb, sw2)):
                    sp.dma_start(dst[:], src).then_inc(w_in, 16)
                sp.wait_ge(w_in, 48)

            @block.vector
            def _(dve):
                def rows(i, r, first=False):
                    for j in range(G):
                        q = r * G + j
                        n = (2 * i + r) * G + j
                        if not first:
                            dve.wait_ge(sent[q], 16 * TOPK1 * i)
                        nc.vector.tensor_copy(at[q][:].unsqueeze(2), scatter_at[:, :, bass.ds(n, 1)])
                        normalise(nc, x[q][:], h, mean, rstd, n).then_inc(x_ready, 1)

                def share(g):
                    dve.wait_ge(gate_ready, g + 1)
                    nc.vector.tensor_tensor(act1[:], gate[:], p1[:], ALU.mult).then_inc(half_ready, 1)
                    dve.wait_ge(half_ready, g + 1)
                    nc.vector.tensor_tensor(act1[:], act1[:], p3[:], ALU.mult).then_inc(act_ready, 1)
                    dve.wait_ge(y_done, g + 1)
                    ht = h[:, bass.ds(g * G, G), :]
                    nc.vector.tensor_tensor(ht, ht, py[:].rearrange("p (n d) -> p n d", d=D), ALU.add)\
                        .then_inc(h_ready, 1)

                rows(0, 0, first=True)
                rows(0, 1, first=True)
                share(0)
                with nc.vector.Fori(1, NG // 2) as i:
                    rows(i, 0)
                    share(2 * i - 1)
                    rows(i, 1)
                    share(2 * i)
                share(NG - 1)

            @block.gpsimd
            def _(pool):
                nc.gpsimd.memset(tick[:], 0.0).then_inc(tick_ready, 1)
                with nc.gpsimd.Fori(0, NG // 2) as i:
                    for q in range(2 * G):
                        pool.wait_ge(tick_ready, i * 2 * G + q + 1)
                        pool.wait_ge(x_ready, i * 2 * G + q + 1)
                        nc.gpsimd.tensor_tensor(tick[:, 1:2], tick[:, 0:1], tick[:, 0:1], ALU.mult)\
                            .then_inc(tick_ready, 1)
                        for k in range(TOPK1):
                            nc.gpsimd.indirect_dma_start(
                                x_slots[:], bass.IndirectOffsetOnAxis(ap=at[q][:, k:k + 1], axis=0),
                                x[q][:], None).then_inc(sent[q], 16)
                for q in range(2 * G):
                    pool.wait_ge(sent[q], 16 * TOPK1 * (NG // 2))

            @block.scalar
            def _(act):
                with nc.scalar.Fori(0, NG) as g:
                    act.wait_ge(xT_ps, g + 1)
                    nc.scalar.activation(xT[:], pt[:], ACT.Copy).then_inc(xT_ready, 1)
                    act.wait_ge(up_done, g + 1)
                    nc.scalar.activation(gate[:], p1[:], ACT.Sigmoid).then_inc(gate_ready, 1)

            @block.tensor
            def _(pe):
                def group(g, r, first=False):
                    for j in range(G):
                        pe.wait_ge(x_ready, g * G + j + 1)
                        last = nc.tensor.transpose(pt[:, j * P:(j + 1) * P], x[r * G + j][:], ident[:])
                    last.then_inc(xT_ps, 1)
                    pe.wait_ge(xT_ready, g + 1)
                    nc.tensor.matmul(p1[:], sw1_sb[:], xT[:], start=True, stop=True)
                    nc.tensor.matmul(p3[:], sw3_sb[:], xT[:], start=True, stop=True).then_inc(up_done, 1)
                    pe.wait_ge(act_ready, g + 1)
                    if not first:
                        pe.wait_ge(h_ready, g)
                    for j in range(G):
                        last = nc.tensor.matmul(py[:, j * P:(j + 1) * P], act1[:, j * P:(j + 1) * P], sw2_sb[:],
                                                start=True, stop=True)
                    last.then_inc(y_done, 1)

                pe.wait_ge(w_in, 48)
                group(0, 0, first=True)
                group(1, 1)
                with nc.tensor.Fori(1, NG // 2) as i:
                    group(2 * i, 0)
                    group(2 * i + 1, 1)


def experts_top2(nc, K, x_slots, y_slots, w13, w2):
    ident = K["ident"]
    RT = CAP // P
    with Bench(nc, "exp1") as m:
        x = [m.sb(f"x{j}", [P, RT, D]) for j in range(G)]
        wu = [m.sb(f"wu{j}", [P, 2 * HID1]) for j in range(G)]
        wd = [m.sb(f"wd{j}", [HID1, D]) for j in range(G)]
        xT = [m.sb(f"xT{j}", [P, CAP]) for j in range(G)]
        gate = [m.sb(f"gate{j}", [HID1, CAP]) for j in range(G)]
        half = [m.sb(f"half{j}", [HID1, CAP]) for j in range(G)]
        hid = [m.sb(f"hid{j}", [HID1, CAP]) for j in range(G)]
        y = [m.sb(f"y{j}", [P, RT, D]) for j in range(G)]
        pa = [m.ps(f"pa{j}", [P, 512]) for j in range(G)]
        pb = [m.ps(f"pb{j}", [P, 2, CAP]) for j in range(G)]
        x_in = [m.sem(f"x_in{j}") for j in range(G)]
        y_out = [m.sem(f"y_out{j}") for j in range(G)]
        xT_ps, xT_ready, up_done, gate_ready, half_ready, hid_ready, y_done, y_ready = (
            m.sem(n) for n in "xT_ps xT_ready up_done gate_ready half_ready hid_ready y_done y_ready".split())
        N = E1N // G
        with nc.Block() as block:
            @block.sync
            def _(sp):
                def load(ex, j):
                    sp.dma_start(x[j][:], x_slots[bass.ds(ex * CAP, CAP), :].rearrange("(t p) d -> p t d", p=P))\
                        .then_inc(x_in[j], 16)
                    sp.dma_start(wu[j][:], w13[bass.ds(ex * D, D), :]).then_inc(x_in[j], 16)
                    sp.dma_start(wd[j][:], w2[bass.ds(ex * HID1, HID1), :]).then_inc(x_in[j], 16)

                def store(i):
                    for j in range(G):
                        sp.wait_ge(y_ready, i * G + j + 1)
                        sp.dma_start(y_slots[bass.ds((i * G + j) * CAP, CAP), :].rearrange("(t p) d -> p t d", p=P),
                                     y[j][:]).then_inc(y_out[j], 16)

                for j in range(G):
                    load(j, j)
                with nc.sync.Fori(0, N - 1) as i:
                    for j in range(G):
                        sp.wait_ge(y_ready, i * G + j + 1)
                        load((i + 1) * G + j, j)
                    store(i)
                store(N - 1)
                for j in range(G):
                    sp.wait_ge(y_out[j], 16 * N)

            @block.vector
            def _(dve):
                def pass_(i, first=False):
                    for j in range(G):
                        n = i * G + j
                        dve.wait_ge(gate_ready, n + 1)
                        nc.vector.tensor_tensor(half[j][:], gate[j][:], pb[j][0:HID1, 0, :], ALU.mult)\
                            .then_inc(half_ready, 1)
                        dve.wait_ge(half_ready, n + 1)
                        nc.vector.tensor_tensor(hid[j][:], half[j][:], pb[j][0:HID1, 1, :], ALU.mult)\
                            .then_inc(hid_ready, 1)
                    for j in range(G):
                        dve.wait_ge(y_done, i * G + j + 1)
                        if not first:
                            dve.wait_ge(y_out[j], 16 * i)
                        nc.vector.tensor_copy(y[j][:], pa[j][:, CAP:2 * CAP].rearrange("p (t d) -> p t d", d=D))\
                            .then_inc(y_ready, 1)

                pass_(0, first=True)
                with nc.vector.Fori(1, N) as i:
                    pass_(i)

            @block.scalar
            def _(act):
                with nc.scalar.Fori(0, N) as i:
                    for j in range(G):
                        act.wait_ge(xT_ps, i * G + j + 1)
                        nc.scalar.activation(xT[j][:], pa[j][:, 0:CAP], ACT.Copy).then_inc(xT_ready, 1)
                    for j in range(G):
                        act.wait_ge(up_done, i * G + j + 1)
                        nc.scalar.activation(gate[j][:], pb[j][0:HID1, 0, :], ACT.Sigmoid).then_inc(gate_ready, 1)

            @block.tensor
            def _(pe):
                with nc.tensor.Fori(0, N) as i:
                    for j in range(G):
                        pe.wait_ge(x_in[j], 48 * (i + 1))
                        for t in range(RT):
                            last = nc.tensor.transpose(pa[j][:, t * P:(t + 1) * P], x[j][:, t, :], ident[:])
                        last.then_inc(xT_ps, 1)
                    for j in range(G):
                        pe.wait_ge(xT_ready, i * G + j + 1)
                        for n in range(2):
                            last = nc.tensor.matmul(pb[j][0:HID1, n, :], wu[j][:, n * HID1:(n + 1) * HID1], xT[j][:],
                                                    start=True, stop=True)
                        last.then_inc(up_done, 1)
                    for j in range(G):
                        pe.wait_ge(hid_ready, i * G + j + 1)
                        for t in range(RT):
                            last = nc.tensor.matmul(pa[j][:, CAP + t * P:CAP + (t + 1) * P],
                                                    hid[j][:, t * P:(t + 1) * P], wd[j][:], start=True, stop=True)
                        last.then_inc(y_done, 1)


def load_constants(nc, K, tables, in_bf16, x_slots, results, zeros, cleared):
    with Bench(nc, "const") as m:
        const_in, zeroed = m.sem("const_in"), m.sem("zeroed")
        wide = {n: m.sb(f"wide_{n}", list(K[n].shape)) for n in in_bf16}
        with nc.Block() as block:
            @block.sync
            def _(sp):
                for name in K:
                    sp.dma_start((wide.get(name) or K[name])[:], tables[name]).then_inc(const_in, 16)
                sp.wait_ge(zeroed, 1)
                clear_slots(x_slots, results, zeros, cleared, sp)
                sp.wait_ge(const_in, 16 * len(K))

            @block.vector
            def _(dve):
                nc.vector.memset(zeros[:], 0.0).then_inc(zeroed, 1)
                dve.wait_ge(const_in, 16 * len(K))
                for name in in_bf16:
                    nc.vector.tensor_copy(K[name][:], wide[name][:])


def await_cleared(nc, cleared):
    with nc.Block() as block:
        @block.sync
        def _(sp):
            sp.wait_ge(cleared, 16 * CLEARS)


def store_output(nc, h, out):
    with Bench(nc, "store") as m:
        stored = m.sem("stored")
        with nc.Block() as block:
            @block.sync
            def _(sp):
                for s in range(2):
                    sp.dma_start(out[:, s * P:s * P + ROWS[s], :].rearrange("b p d -> p b d"),
                                 h[0:ROWS[s]].rearrange("p (b s) d -> p b s d", s=2)[:, :, s, :])\
                        .then_inc(stored, 16)
                sp.wait_ge(stored, 32)


def shape_tables():
    f = np.float32
    p, col = np.arange(P)[:, None], np.arange(T)[None, :]
    after = (col > p).astype(f)
    real = np.ones((P, NT), f)
    real[ROWS[1]:, 1::2] = 0
    tile, k = np.arange(NT)[None, :], np.arange(TOPK1)[None, :, None]
    half, head, query = p // (P // 2), p // HALF % H, p % HALF
    spill = SLOTS + k * (NT * P) + np.arange(NT)[None, None, :] * P + p[:, :, None]
    inc = {
        "after": after,
        "upto": (col >= p).astype(f),
        "ident": np.eye(P, dtype=f),
        "inv03": np.full((P, 1), 1.0 / 0.3, f),
        "after_b": after[:, :P],
        "ones_b": np.ones((P, P), f),
        "real": real,
        "pad_to": (1 - real) * (SLOTS + tile),
        "pad_from": (1 - real) * SLOTS0,
        "spill": spill.reshape(P, TOPK1 * NT),
        "rank0": np.tile(np.arange(E0, 0, -1), (P, 1)),
        "rank1": np.tile(np.arange(E1N, 0, -1), (P, 1)),
        "multiples": np.tile(P * np.arange(NT), (P, 1)),
        "tile_no": np.tile(np.arange(ST0), (P, 1)),
        "mask16": p // HD == np.arange(H),
        "mask_row": head == np.arange(H),
        "mask_pv": np.concatenate([head == np.arange(D) // HD, query == np.arange(D) // HD], 1),
        "sel_q": half * HALF + query == np.arange(BQ),
    }
    return {n: np.ascontiguousarray(a, dtype=f) for n, a in inc.items()}


def layouts(a):
    W, NLOW = a["L0_tok_W"], C + C * C + C ** 3

    def level(lo, hi):
        return W[:, lo:hi].reshape(D, (hi - lo) // C, C).transpose(1, 2, 0).reshape(-1, C * D)

    query = np.arange(HALF)[:, None, None]
    key_at = np.clip(np.arange(KWIN) - (REACH + HALF) - query, -MAX_REL, MAX_REL) + MAX_REL
    value_at = np.clip(np.arange(P)[:, None] - (np.arange(VWIN)[None, :] - P), -MAX_REL, MAX_REL) + MAX_REL
    rel_k, rel_v = a["L1_attn_rel_k"], a["L1_attn_rel_v"]
    w1, b1, w2 = a["L0_ffn_W1"], a["L0_ffn_b1"], a["L0_ffn_W2"]
    lay = {
        "x_t": a["x"].transpose(1, 0, 2).reshape(T, B * CIN),
        "w_main": level(NLOW, W.shape[1]),
        "w_low": np.concatenate([level(C + C * C, NLOW), level(C, C + C * C), level(0, C)]),
        "tok_b": a["L0_tok_b"],
        "fuz_wq": a["L0_attn_Wq"].T, "fuz_bq": a["L0_attn_bq"][:, None],
        "fuz_wk": a["L0_attn_Wk"].T, "fuz_bk": a["L0_attn_bk"][:, None],
        "gate0": a["L0_ffn_Wr"], "gate0_b": a["L0_ffn_br"],
        "exp0_w1": np.concatenate([w1.transpose(1, 0, 2), b1.reshape(E0, HID0 // P, P).transpose(2, 0, 1)], 2),
        "exp0_w2": w2.reshape(E0, HID0 // P, P, D).transpose(2, 0, 1, 3).reshape(P, E0, -1),
        "exp0_b2": a["L0_ffn_b2"].reshape(-1),
        "rel_wq": a["L1_attn_Wq"], "rel_bq": a["L1_attn_bq"][:, None],
        "rel_wk": a["L1_attn_Wk"], "rel_bk": a["L1_attn_bk"][:, None],
        "rel_wv": a["L1_attn_Wv"], "rel_bv": a["L1_attn_bv"],
        "rel_wo": a["L1_attn_Wo"], "rel_bo": a["L1_attn_bo"],
        "rel_wq_rep": np.repeat(a["L1_attn_Wq"].reshape(D, H, 1, HD), HALF, axis=2).reshape(D, H, P),
        "rel_bq_rep": np.repeat(a["L1_attn_bq"].reshape(H, 1, HD), HALF, axis=1).reshape(H, P).T,
        "rel_ends": np.stack([np.tile(rel_k[0], H), np.tile(rel_k[2 * MAX_REL], H)], 1),
        "rel_ktab": rel_k[key_at, np.arange(HD)[None, :, None]].reshape(P, KWIN),
        "rel_vtab": rel_v[value_at],
        "gate1": a["L1_ffn_gate_w"].T,
        "sw1": a["L1_ffn_sw1"], "sw3": a["L1_ffn_sw3"], "sw2": a["L1_ffn_sw2"],
        "exp1_w13": np.concatenate([a["L1_ffn_w1"], a["L1_ffn_w3"]], 2).reshape(E1N * D, 2 * HID1),
        "exp1_w2": a["L1_ffn_w2"].reshape(E1N * HID1, D),
    }
    t = np.diff(np.linspace(0.0, 1.0, T, dtype=np.float32))
    lay["step_time"] = np.stack([t[:P], np.concatenate([t[P:], np.zeros(P - ROWS[1], np.float32)])], 1)
    return {n: np.ascontiguousarray(v) for n, v in lay.items()}


def build(nc, t, w, out):
    in_bf16 = ("after_b", "ones_b")
    x_slots = nc.dram_tensor("x_slots", (SLOTS + TOPK1 * NT * P, D), FP32, kind="Internal").ap()
    y0_slots = nc.dram_tensor("y0_slots", (SLOTS0 + 1, D), FP32, kind="Internal").ap()
    y1_slots = nc.dram_tensor("y1_slots", (SLOTS1 + 1, D), FP32, kind="Internal").ap()
    with Bench(nc, "all") as m:
        h = m.sb("h", [P, NT, D])
        stats, mean, rstd = m.sb("stats", [P, NT, 6]), m.sb("mean", [P, NT]), m.sb("rstd", [P, NT])
        cleared = m.sem("cleared")
        K = {n: m.sb(f"k_{n}", list(a.shape), BF16 if n in in_bf16 else FP32) for n, a in t.items()}
        with Bench(nc, "early") as early:
            zeros = early.sb("zeros", [P, 16 * D])
            load_constants(nc, K, t, in_bf16, x_slots, [(y0_slots, SLOTS0), (y1_slots, SLOTS1)], zeros, cleared)
            signature_tokens(nc, K, h, stats, w["x_t"], w["step_time"], w["w_main"], w["w_low"], w["tok_b"])
            norm_factors(nc, stats, mean, rstd, "norm0")
            fuzzy_attention(nc, K, h, mean, rstd, stats, w["fuz_wq"], w["fuz_bq"], w["fuz_wk"], w["fuz_bk"])
            norm_factors(nc, stats, mean, rstd, "norm1")
            await_cleared(nc, cleared)
        with Bench(nc, "moe0") as q:
            logits = q.sb("logits", [P, NT, E0])
            to, back = q.sb("to", [P, 1, NT], U32), q.sb("back", [P, 1, NT], U32)
            tile_expert = q.sb("tile_expert", [P, ST0], U32)
            router_logits(nc, K, h, mean, rstd, logits, w["gate0"], w["gate0_b"], E0, "logits0")
            route_top1(nc, K, logits, to, back, tile_expert)
            scatter_rows(nc, h, mean, rstd, x_slots, to, 1, "scatter0")
            experts_top1(nc, K, x_slots, y0_slots, tile_expert, w["exp0_w1"], w["exp0_w2"], w["exp0_b2"])
            gather_rows(nc, h, stats, y0_slots, back, None, 1, "gather0")
        norm_factors(nc, stats, mean, rstd, "norm2")
        relative_attention(nc, K, h, mean, rstd, stats, *(w[f"rel_{n}"] for n in (
            "wq bq wk bk wv bv wo bo wq_rep bq_rep ends ktab vtab").split()))
        norm_factors(nc, stats, mean, rstd, "norm3")
        with Bench(nc, "moe1") as q:
            to, back = q.sb("to", [P, TOPK1, NT], U32), q.sb("back", [P, TOPK1, NT], U32)
            weight = q.sb("weight", [P, TOPK1, NT])
            with Bench(nc, "choice") as c:
                logits = c.sb("logits", [P, NT, E1N])
                router_logits(nc, K, h, mean, rstd, logits, w["gate1"], None, E1N, "logits1")
                route_top2(nc, K, logits, to, back, weight)
            scatter_and_share(nc, K, h, mean, rstd, x_slots, to, w["sw1"], w["sw3"], w["sw2"])
            experts_top2(nc, K, x_slots, y1_slots, w["exp1_w13"], w["exp1_w2"])
            gather_rows(nc, h, None, y1_slots, back, [weight[:, 0], weight[:, 1]], TOPK1, "gather1")
        store_output(nc, h, out)


def kernel(**inputs):
    import numpy as _np
    import concourse.bacc as _bacc
    from concourse.bass_utils import run_bass_kernel_spmd as _run

    nc = _bacc.Bacc("TRN2", target_bir_lowering=False, num_devices=1)
    arrays = {}

    def dram(name, a):
        arrays[name] = a
        return nc.dram_tensor(name, a.shape, mybir.dt.from_np(a.dtype), kind="ExternalInput").ap()

    tables = {n: dram(f"table_{n}", a) for n, a in shape_tables().items()}
    laid = {n: dram(f"in_{n}", a) for n, a in layouts({k: _np.asarray(v) for k, v in inputs.items()}).items()}
    out = nc.dram_tensor("out_dram", (B, L, D), FP32, kind="ExternalOutput").ap()
    build(nc, tables, laid, out)
    r = _run(nc, [arrays], core_ids=[0])
    return r.results[0]["out_dram"]
```

```python
import concourse.bass as bass
from concourse import mybir
from contextlib import ExitStack
import numpy as np

FP32 = mybir.dt.float32
FP32R = mybir.dt.float32r
BF16 = mybir.dt.bfloat16
I32 = mybir.dt.int32
U32 = mybir.dt.uint32
ALU = mybir.AluOpType
ACT = mybir.ActivationFunctionType
AX = mybir.AxisListType

P = 128
B, T, CIN, D = 32, 256, 7, 128
L = T - 1
ROWS = (P, L - P)
C = CIN + 1
NT = 2 * B
EPS = 1e-5
G = 4


class Bench:

    def __init__(self, nc, stage):
        self.nc, self.stage, self.stack, self.sems = nc, stage, ExitStack(), []

    def __enter__(self):
        self.stack.__enter__()
        return self

    def __exit__(self, *e):
        if self.sems:
            self.nc.clear_and_free_semaphores(self.sems)
            self.nc.all_engine_barrier()
        return self.stack.__exit__(*e)

    def sb(self, name, shape, dt=FP32):
        return self.stack.enter_context(self.nc.sbuf_tensor(f"{self.stage}_{name}", shape, dt))

    def ps(self, name, shape, dt=FP32):
        return self.stack.enter_context(self.nc.psum_tensor(f"{self.stage}_{name}", shape, dt))

    def sem(self, name):
        self.sems.append(self.nc.alloc_semaphore(f"{self.stage}_{name}"))
        return self.sems[-1]


class Chain:

    def __init__(self, eng, sem, base=0):
        self.eng, self.sem, self.n = eng, sem, base

    def __call__(self, instruction):
        instruction.then_inc(self.sem, 1)
        self.n = self.n + 1
        self.eng.wait_ge(self.sem, self.n)


def outer(nc_eng, out, left, right, n, a, c):
    return nc_eng.tensor_tensor(
        out,
        left.unsqueeze(3).to_broadcast([P, n, a, c]),
        right.unsqueeze(2).to_broadcast([P, n, a, c]),
        ALU.mult)


THREE = ((0, 0), (0, 1), (1, 0))


def rest(engine, out, value, rounded):
    return engine.tensor_tensor(out, value, rounded.bitcast(FP32), ALU.subtract)


def signature_tokens(nc, K, h, stats, x_t, step_time, w_main, w_low, tok_b):
    NA = C ** 3 // P
    LOW = C ** 2 + C + 1
    after, upto, ident = K["after"], K["upto"], K["ident"]
    with Bench(nc, "tok") as m:
        x0 = m.sb("x0", [P, 2, B * CIN])
        x1 = m.sb("x1", [P, 2, B * CIN])
        dt_sb = m.sb("dt", [P, 2])
        v = m.sb("v", [P, B, 2, C])
        v_s = m.sb("v_scaled", [P, B, 2, C])
        g1 = m.sb("g1", [P, B, 2, C])
        g1v = m.sb("g1v", [P, NT, C, C])
        r2_pre = m.sb("r2_pre", [P, NT, C, C])
        q2_pre = m.sb("q2_pre", [P, NT, C, C])
        low = m.sb("low", [P, 2, LOW])
        q2 = m.sb("q2", [P, 2, C * C])
        r2v = m.sb("r2v", [P, 2, C ** 3])
        q2v = m.sb("q2v", [P, 2, C ** 3])
        r2v_p = [m.sb(f"r2v_{k}", [P, 2, C ** 3], FP32R) for k in "hl"]
        q2v_p = [m.sb(f"q2v_{k}", [P, 2, C ** 3], FP32R) for k in "hl"]
        feat = [m.sb(f"feat_{k}", [P, 2, NA + 1, P], FP32R) for k in "hl"]
        w = m.sb("w", [P, NA + 1, C * D])
        w_p = [m.sb(f"w_{k}", [P, NA + 1, C * D], FP32R) for k in "hl"]
        after_r, ident_r = m.sb("after_r", [P, T], FP32R), m.sb("ident_r", [P, P], FP32R)
        bias = m.sb("bias", [P, D])
        prod = m.sb("prod", [P, 2, C, D])
        inc = m.sb("inc", [P, 2, D])
        a3_ps = m.ps("a3_ps", [P, NA, 2, P])
        low_ps = m.ps("low_ps", [P, 512])
        small_ps = m.ps("small_ps", [P, 512])
        main_ps = [m.ps(f"main_ps{s}", [P, C * D]) for s in range(2)]
        e1_ps = main_ps[0]
        lowT_ps = low_ps[:, 0:2 * P]
        h_ps = small_ps[:, 0:2 * D].rearrange("p (s d) -> p s d", s=2)
        e2_ps = small_ps[:, 2 * D:2 * D + 2 * C * C]

        x_in, w_in, zeroed = m.sem("x_in"), m.sem("w_in"), m.sem("zeroed")
        vec, v_ready, e1_ready = m.sem("vec"), m.sem("v_ready"), m.sem("e1_ready")
        pre_ready = m.sem("pre_ready")
        e2_ready, low_ready, q2_ready = m.sem("e2_ready"), m.sem("low_ready"), m.sem("q2_ready")
        r2v_ready, q2v_ready = m.sem("r2v_ready"), m.sem("q2v_ready")
        r2v_round, r2v_rest = m.sem("r2v_round"), m.sem("r2v_rest")
        q2v_round, q2v_rest = m.sem("q2v_round"), m.sem("q2v_rest")
        w_round, w_rest = m.sem("w_round"), m.sem("w_rest")
        a3_ready, feat_round, feat_rest = m.sem("a3_ready"), m.sem("feat_round"), m.sem("feat_rest")
        main_ready, prod_ready, inc_ready = m.sem("main_ready"), m.sem("prod_ready"), m.sem("inc_ready")
        h_ready, h_done = m.sem("h_ready"), m.sem("h_done")

        with nc.Block() as block:

            @block.sync
            def _(sp):
                sp.dma_start(x0[:, 0, :], x_t[0:P, :]).then_inc(x_in, 16)
                sp.dma_start(x1[:, 0, :], x_t[1:P + 1, :]).then_inc(x_in, 16)
                sp.dma_start(x0[0:ROWS[1], 1, :], x_t[P:L, :]).then_inc(x_in, 16)
                sp.dma_start(x1[0:ROWS[1], 1, :], x_t[P + 1:T, :]).then_inc(x_in, 16)
                sp.dma_start(dt_sb[:], step_time).then_inc(x_in, 16)
                for j in range(NA):
                    sp.dma_start(w[:, j, :], w_main[j * P:(j + 1) * P, :]).then_inc(w_in, 16)
                sp.dma_start(w[0:LOW, NA, :], w_low).then_inc(w_in, 16)
                sp.dma_start(bias[:], tok_b.partition_broadcast(P)).then_inc(w_in, 16)
                sp.wait_ge(w_in, 16 * (NA + 2))

            def tile_view(t):
                return t[:].rearrange("p b s c -> p (b s) c")

            @block.vector
            def _(dve):
                link = Chain(dve, vec)
                link(nc.vector.memset(v[:], 0.0))
                nc.vector.tensor_copy(after_r[:], after[:])
                nc.vector.tensor_copy(ident_r[:], ident[:])
                nc.vector.memset(low[:, :, LOW - 1:LOW], 1.0)
                dve.wait_ge(x_in, 16 * 5)
                for s in range(2):
                    n = ROWS[s]
                    nc.vector.tensor_tensor(
                        v[0:n, :, s, 1:C],
                        x1[0:n, s, :].rearrange("p (b c) -> p b c", c=CIN),
                        x0[0:n, s, :].rearrange("p (b c) -> p b c", c=CIN), ALU.subtract)
                    link(nc.vector.tensor_copy(v[:, :, s, 0:1],
                                               dt_sb[:, s:s + 1].unsqueeze(1).to_broadcast([P, B, 1])))
                nc.vector.memset(q2[:], 0.0).then_inc(v_ready, 1)
                e1 = e1_ps[:, 0:NT * C].rearrange("p (b s c) -> p b s c", b=B, s=2)
                dve.wait_ge(e1_ready, 1)
                link(nc.vector.scalar_tensor_tensor(g1[:], v[:], 0.5, e1, ALU.mult, ALU.add))
                link(outer(nc.vector, g1v[:], tile_view(g1), tile_view(v), NT, C, C))
                for div, scale, pre in ((3.0, 0.5, r2_pre), (4.0, 1.0 / 6.0, q2_pre)):
                    link(nc.vector.scalar_tensor_tensor(v_s[:], v[:], 1.0 / div, e1, ALU.mult, ALU.add))
                    link(nc.vector.tensor_scalar(v_s[:], v_s[:], scale, None, ALU.mult))
                    link(outer(nc.vector, pre[:], tile_view(v_s), tile_view(v), NT, C, C))
                nc.vector.memset(inc[:], 0.0).then_inc(pre_ready, 1)

                vt, g1t = tile_view(v), tile_view(g1)

                def features(b, first=False):
                    dve.wait_ge(e2_ready, b + 1)
                    e2 = e2_ps.rearrange("p (s k) -> p s k", s=2)
                    flat = "p n a c -> p n (a c)"
                    nc.vector.tensor_tensor(low[:, :, 0:C * C], e2,
                                            r2_pre[:, bass.ds(2 * b, 2)].rearrange(flat), ALU.add)
                    nc.vector.tensor_copy(low[:, :, C * C:C * C + C], g1t[:, bass.ds(2 * b, 2), :])\
                        .then_inc(low_ready, 1)
                    if not first:
                        dve.wait_ge(q2v_ready, b)
                    nc.vector.scalar_tensor_tensor(q2[:], e2, 0.5, q2_pre[:, bass.ds(2 * b, 2)].rearrange(flat),
                                                   ALU.mult, ALU.add).then_inc(q2_ready, 1)
                    dve.wait_ge(low_ready, b + 1)
                    outer(nc.vector, r2v[:].rearrange("p n (a c) -> p n a c", c=C), low[:, :, 0:C * C],
                          vt[:, bass.ds(2 * b, 2), :], 2, C * C, C).then_inc(r2v_ready, 1)

                def combine(b, s, first=False):
                    dve.wait_ge(main_ready, 2 * b + s + 1)
                    if not first:
                        dve.wait_ge(inc_ready, 2 * b + s - 1)
                    nc.vector.tensor_tensor(
                        prod[:, s], main_ps[s][:].rearrange("p (c o) -> p c o", c=C),
                        vt[:, bass.ds(2 * b + s, 1), :].rearrange("p n c -> p (n c)").unsqueeze(2)
                        .to_broadcast([P, C, D]), ALU.mult).then_inc(prod_ready, 1)
                    dve.wait_ge(prod_ready, 2 * b + s + 1)
                    if s == 0 and not first:
                        dve.wait_ge(h_ready, b)
                    nc.vector.tensor_reduce(inc[:, s, :], prod[:, s].rearrange("p c o -> p o c"),
                                            AX.X, ALU.add).then_inc(inc_ready, 1)

                def finish(b):
                    dve.wait_ge(h_ready, b + 1)
                    nc.vector.tensor_tensor(h[:, bass.ds(2 * b, 2), :], h_ps,
                                            bias[:].unsqueeze(1).to_broadcast([P, 2, D]),
                                            ALU.add).then_inc(h_done, 1)
                    dve.wait_ge(h_done, b + 1)
                    for s in range(2):
                        nc.vector.bn_stats(stats[:, bass.ds(2 * b + s, 1), :].rearrange("p n k -> p (n k)"),
                                           h[:, bass.ds(2 * b + s, 1), :].rearrange("p n k -> p (n k)"))

                def q2v_remainder(b):
                    dve.wait_ge(q2v_round, b + 1)
                    rest(nc.vector, q2v_p[1][:], q2v[:], q2v_p[0][:]).then_inc(q2v_rest, 1)

                def feat_remainder(b, s):
                    dve.wait_ge(feat_round, 2 * b + s + 1)
                    rest(nc.vector, feat[1][:, s, 0:NA, :], a3_ps[:, :, s, :], feat[0][:, s, 0:NA, :])
                    rest(nc.vector, feat[1][0:LOW, s, NA, :], lowT_ps[0:LOW, s * P:(s + 1) * P],
                         feat[0][0:LOW, s, NA, :]).then_inc(feat_rest, 1)

                dve.wait_ge(w_in, 16 * (NA + 2))
                features(0, first=True)
                q2v_remainder(0)
                dve.wait_ge(w_round, 1)
                rest(nc.vector, w_p[1][:, 0:NA, :], w[:, 0:NA, :], w_p[0][:, 0:NA, :])
                rest(nc.vector, w_p[1][0:LOW, NA, :], w[0:LOW, NA, :], w_p[0][0:LOW, NA, :]).then_inc(w_rest, 1)
                feat_remainder(0, 0)
                feat_remainder(0, 1)
                features(1)
                q2v_remainder(1)
                combine(0, 0, first=True)
                feat_remainder(1, 0)
                features(2)
                combine(0, 1, first=True)
                feat_remainder(1, 1)
                q2v_remainder(2)
                with nc.vector.Fori(1, B - 2) as b:
                    combine(b, 0)
                    finish(b - 1)
                    feat_remainder(b + 1, 0)
                    features(b + 2)
                    combine(b, 1)
                    feat_remainder(b + 1, 1)
                    q2v_remainder(b + 2)
                combine(B - 2, 0)
                finish(B - 3)
                feat_remainder(B - 1, 0)
                combine(B - 2, 1)
                feat_remainder(B - 1, 1)
                combine(B - 1, 0)
                finish(B - 2)
                combine(B - 1, 1)
                finish(B - 1)

            @block.gpsimd
            def _(pool):
                vt = tile_view(v)

                def outer_q2(b):
                    pool.wait_ge(q2_ready, b + 1)
                    outer(nc.gpsimd, q2v[:].rearrange("p n (a c) -> p n a c", c=C), q2[:],
                          vt[:, bass.ds(2 * b, 2), :], 2, C * C, C).then_inc(q2v_ready, 1)

                def r2v_remainder(b):
                    pool.wait_ge(r2v_round, b + 1)
                    rest(nc.gpsimd, r2v_p[1][:], r2v[:], r2v_p[0][:]).then_inc(r2v_rest, 1)

                outer_q2(0)
                r2v_remainder(0)
                with nc.gpsimd.Fori(1, B) as b:
                    pool.wait_ge(e2_ready, b + 1)
                    outer_q2(b)
                    r2v_remainder(b)

            @block.scalar
            def _(act):
                def rounded(b):
                    act.wait_ge(r2v_ready, b + 1)
                    nc.scalar.activation(r2v_p[0][:], r2v[:], ACT.Copy).then_inc(r2v_round, 1)
                    act.wait_ge(q2v_ready, b + 1)
                    nc.scalar.activation(q2v_p[0][:], q2v[:], ACT.Copy).then_inc(q2v_round, 1)

                def evacuate(b, s, first=False):
                    act.wait_ge(a3_ready, b + 1)
                    if not first:
                        act.wait_ge(main_ready, 2 * b - 1 + s)
                        act.wait_ge(feat_rest, 2 * b + s)
                    nc.scalar.activation(feat[0][:, s, 0:NA, :], a3_ps[:, :, s, :], ACT.Copy)
                    nc.scalar.activation(feat[0][0:LOW, s, NA, :], lowT_ps[0:LOW, s * P:(s + 1) * P],
                                         ACT.Copy).then_inc(feat_round, 1)

                rounded(0)
                act.wait_ge(w_in, 16 * (NA + 2))
                nc.scalar.activation(w_p[0][:, 0:NA, :], w[:, 0:NA, :], ACT.Copy)
                nc.scalar.activation(w_p[0][0:LOW, NA, :], w[0:LOW, NA, :], ACT.Copy).then_inc(w_round, 1)
                evacuate(0, 0, first=True)
                act.wait_ge(feat_rest, 1)
                evacuate(0, 1, first=True)
                rounded(1)
                with nc.scalar.Fori(1, B - 1) as b:
                    evacuate(b, 0)
                    rounded(b + 1)
                    evacuate(b, 1)
                evacuate(B - 1, 0)
                evacuate(B - 1, 1)

            @block.tensor
            def _(pe):
                def level2(b, first=False):
                    if not first:
                        pe.wait_ge(h_done, b - 2)
                    gv = g1v[:].rearrange("p n a c -> p n (a c)")
                    nc.tensor.matmul(e2_ps[:, 0:64], after[:, 0:P], gv[:, bass.ds(2 * b, 1), :],
                                     start=True, stop=True)
                    nc.tensor.matmul(e2_ps[:, 64:128], after[:, P:T], gv[:, bass.ds(2 * b, 1), :],
                                     start=True, stop=False)
                    nc.tensor.matmul(e2_ps[:, 64:128], after[:, 0:P], gv[:, bass.ds(2 * b + 1, 1), :],
                                     start=False, stop=True).then_inc(e2_ready, 1)

                def level3(b, first=False):
                    pe.wait_ge(low_ready, b + 1)
                    if not first:
                        pe.wait_ge(feat_rest, 2 * b)
                    for s in range(2):
                        nc.tensor.transpose(lowT_ps[0:LOW, s * P:(s + 1) * P], low[:, s, :], ident[:])
                    pe.wait_ge(q2v_rest, b + 1)
                    pe.wait_ge(r2v_rest, b + 1)
                    for j in range(NA):
                        cols = slice(j * P, (j + 1) * P)
                        for k in range(2):
                            for s in range(2):
                                nc.tensor.matmul(a3_ps[:, j, s, :], q2v_p[k][:, s, cols], ident_r[:],
                                                 start=(k == 0 and s == 0), stop=False, skip_group_check=True)
                            nc.tensor.matmul(a3_ps[:, j, 1, :], r2v_p[k][:, 1, cols], after_r[:, 0:P],
                                             start=False, stop=False, skip_group_check=True)
                            last = nc.tensor.matmul(a3_ps[:, j], r2v_p[k][:, 0, cols], after_r[:],
                                                    start=False, stop=(k == 1), skip_group_check=True)
                    last.then_inc(a3_ready, 1)

                def main(b, s, first=False):
                    pe.wait_ge(feat_rest, 2 * b + s + 1)
                    if not first:
                        pe.wait_ge(prod_ready, 2 * b + s - 1)
                    for half in range(2):
                        cols = slice(half * 512, (half + 1) * 512)
                        for j in range(NA + 1):
                            n = P if j < NA else LOW
                            for fk, wk in THREE:
                                last = nc.tensor.matmul(main_ps[s][:, cols], feat[fk][0:n, s, j, :],
                                                        w_p[wk][0:n, j, cols],
                                                        start=(j == 0 and (fk, wk) == (0, 0)),
                                                        stop=(j == NA and (fk, wk) == (1, 0)))
                    last.then_inc(main_ready, 1)

                def running_sum(b, first=False, ahead=3):
                    pe.wait_ge(q2_ready, b + ahead)
                    pe.wait_ge(inc_ready, 2 * b + 2)
                    if not first:
                        pe.wait_ge(h_done, b)
                    nc.tensor.matmul(h_ps[:, 0, :], upto[:, 0:P], inc[:, 0, :], start=True, stop=True)
                    nc.tensor.matmul(h_ps[:, 1, :], upto[:, P:T], inc[:, 0, :], start=True, stop=False)
                    nc.tensor.matmul(h_ps[:, 1, :], upto[:, 0:P], inc[:, 1, :], start=False,
                                     stop=True).then_inc(h_ready, 1)

                pe.wait_ge(v_ready, 1)
                e1 = e1_ps[:, 0:NT * C].rearrange("p (b s c) -> p b s c", b=B, s=2)
                nc.tensor.matmul(e1[:, :, 0, :], after[:, 0:P], v[:, :, 0, :], start=True, stop=False,
                                 skip_group_check=True)
                nc.tensor.matmul(e1[:, :, 1, :], after[:, P:T], v[:, :, 0, :], start=False, stop=False,
                                 skip_group_check=True)
                nc.tensor.matmul(e1[:, :, 1, :], after[:, 0:P], v[:, :, 1, :], start=False,
                                 stop=True, skip_group_check=True).then_inc(e1_ready, 1)
                pe.wait_ge(pre_ready, 1)
                level2(0, first=True)
                level3(0, first=True)
                pe.wait_ge(w_rest, 1)
                level2(1, first=True)
                main(0, 0, first=True)
                level3(1)
                level2(2, first=True)
                main(0, 1, first=True)
                main(1, 0)
                running_sum(0, first=True)
                level3(2)
                level2(3)
                main(1, 1)
                with nc.tensor.Fori(2, B - 2) as b:
                    main(b, 0)
                    running_sum(b - 1)
                    level3(b + 1)
                    level2(b + 2)
                    main(b, 1)
                main(B - 2, 0)
                running_sum(B - 3)
                level3(B - 1)
                main(B - 2, 1)
                main(B - 1, 0)
                running_sum(B - 2, ahead=2)
                main(B - 1, 1)
                running_sum(B - 1, ahead=1)


def norm_factors(nc, stats, mean, rstd, stage):
    with Bench(nc, stage) as m:
        spread = m.sb("spread", [P, NT])
        var = m.sb("var", [P, NT])
        vec, var_ready, std_ready = m.sem("vec"), m.sem("var_ready"), m.sem("std_ready")
        mean_e, m2_e, mean_o, m2_o = (stats[:, :, k] for k in (1, 2, 4, 5))
        with nc.Block() as block:
            @block.vector
            def _(dve):
                link = Chain(dve, vec)
                link(nc.vector.tensor_tensor(mean[:], mean_e, mean_o, ALU.add))
                link(nc.vector.tensor_scalar(mean[:], mean[:], 0.5, None, ALU.mult))
                link(nc.vector.tensor_tensor(spread[:], mean_e, mean_o, ALU.subtract))
                link(nc.vector.scalar_tensor_tensor(spread[:], spread[:], 0.25, spread[:],
                                                    ALU.mult, ALU.mult))
                link(nc.vector.tensor_tensor(var[:], m2_e, m2_o, ALU.add))
                link(nc.vector.scalar_tensor_tensor(var[:], var[:], 1.0 / D, spread[:],
                                                    ALU.mult, ALU.add))
                nc.vector.tensor_scalar(var[:], var[:], EPS, None, ALU.add).then_inc(var_ready, 1)
                dve.wait_ge(std_ready, 1)
                nc.vector.reciprocal(rstd[:], var[:])

            @block.scalar
            def _(act):
                act.wait_ge(var_ready, 1)
                nc.scalar.activation(var[:], var[:], ACT.Sqrt).then_inc(std_ready, 1)


def one_tile(t, n):
    return t[:, bass.ds(n, 1), :].rearrange("p n k -> p (n k)")


def one_column(t, n):
    return t[:, bass.ds(n, 1)]


def normalise(nc, out, h, mean, rstd, n):
    return nc.vector.tensor_scalar(out, one_tile(h, n), one_column(mean, n), one_column(rstd, n),
                                   ALU.subtract, ALU.mult)


def fuzzy_attention(nc, K, h, mean, rstd, stats, wq, bq, wk, bk):
    ident = K["ident"]
    INV = 1.0 / 0.3
    with Bench(nc, "fuz") as m:
        wq_sb, wk_sb = m.sb("wq", [P, D]), m.sb("wk", [P, D])
        bq_sb, bk_sb = m.sb("bq", [P, 1]), m.sb("bk", [P, 1])
        x = [m.sb(f"x{j}", [P, 2, D]) for j in range(G)]
        xT = [m.sb(f"xT{j}", [P, T]) for j in range(G)]
        qT = [m.sb(f"qT{j}", [P, T]) for j in range(G)]
        kT = [m.sb(f"kT{j}", [P, T]) for j in range(G)]
        e = [m.sb(f"e{j}", [P, 2, T]) for j in range(G)]
        fall = [m.sb(f"fall{j}", [P, 2, T]) for j in range(G)]
        f = [m.sb(f"f{j}", [P, 2, T]) for j in range(G)]
        fT = [m.sb(f"fT{j}", [P, 2, T]) for j in range(G)]
        neg_max = [m.sb(f"neg_max{j}", [P, 2]) for j in range(G)]
        total = [m.sb(f"total{j}", [P, 2]) for j in range(G)]
        inv = [m.sb(f"inv{j}", [P, 2]) for j in range(G)]
        rise_by = [m.sb(f"rise_by{j}", [P, 2]) for j in range(G)]
        fall_by = [m.sb(f"fall_by{j}", [P, 2]) for j in range(G)]
        pa = [m.ps(f"pa{j}", [P, 2, T]) for j in range(G)]
        pb = [m.ps(f"pb{j}", [P, 2, T]) for j in range(G)]
        w_in, zeroed = m.sem("w_in"), m.sem("zeroed")
        (x_ready, xT_ps, xT_ready, qk_ps, qk_ready, score_ps, max_ready, e_ready, inv_ready, by_ready,
         fall_ready, f_ready, fT_ps, fT_ready, out_ps, h_ready) = (m.sem(n) for n in (
             "x_ready xT_ps xT_ready qk_ps qk_ready score_ps max_ready e_ready inv_ready by_ready "
             "fall_ready f_ready fT_ps fT_ready out_ps h_ready").split())

        with nc.Block() as block:
            @block.sync
            def _(sp):
                for dst, src in ((wq_sb, wq), (wk_sb, wk), (bq_sb, bq), (bk_sb, bk)):
                    sp.dma_start(dst[:], src).then_inc(w_in, 16)
                sp.wait_ge(w_in, 64)

            @block.vector
            def _(dve):
                for j in range(G):
                    nc.vector.memset(f[j][:, :, L:T], 0.0)
                with nc.vector.Fori(0, B // G) as i:
                    for j in range(G):
                        b = i * G + j
                        nc.vector.tensor_scalar(x[j][:, 0, :], one_tile(h, 2 * b), one_column(mean, 2 * b),
                                                one_column(rstd, 2 * b), ALU.subtract, ALU.mult)
                        normalise(nc, x[j][:, 1, :], h, mean, rstd, 2 * b + 1).then_inc(x_ready, 1)
                    for j in range(G):
                        dve.wait_ge(score_ps, i * G + j + 1)
                        nc.vector.tensor_reduce(neg_max[j][:], pa[j][:, :, 0:L], AX.X, ALU.max,
                                                negate=True).then_inc(max_ready, 1)
                    for j in range(G):
                        dve.wait_ge(e_ready, i * G + j + 1)
                        nc.vector.reciprocal(inv[j][:], total[j][:]).then_inc(inv_ready, 1)
                        dve.wait_ge(inv_ready, i * G + j + 1)
                        nc.vector.tensor_scalar(rise_by[j][:], inv[j][:], INV, None, ALU.mult)
                        nc.vector.tensor_scalar(fall_by[j][:], inv[j][:], -INV, None, ALU.mult)\
                            .then_inc(by_ready, 1)
                    for j in range(G):
                        dve.wait_ge(fall_ready, i * G + j + 1)
                        for s in range(2):
                            last = nc.vector.scalar_tensor_tensor(
                                f[j][:, s, 0:L], e[j][:, s, 0:L], rise_by[j][:, s:s + 1],
                                fall[j][:, s, 0:L], ALU.mult, ALU.min)
                        last.then_inc(f_ready, 1)
                    for j in range(G):
                        b = i * G + j
                        dve.wait_ge(out_ps, b + 1)
                        hb = h[:, bass.ds(2 * b, 2), :]
                        nc.vector.tensor_tensor(hb, hb, pa[j][:, :, 0:D], ALU.add).then_inc(h_ready, 1)
                        dve.wait_ge(h_ready, b + 1)
                        for s in range(2):
                            nc.vector.bn_stats(one_tile(stats, 2 * b + s), one_tile(h, 2 * b + s))

            @block.scalar
            def _(act):
                act.wait_ge(w_in, 64)
                with nc.scalar.Fori(0, B // G) as i:
                    for j in range(G):
                        act.wait_ge(xT_ps, i * G + j + 1)
                        nc.scalar.activation(xT[j][:], pa[j][:, 0, :], ACT.Copy).then_inc(xT_ready, 1)
                    for j in range(G):
                        act.wait_ge(qk_ps, i * G + j + 1)
                        nc.scalar.activation(qT[j][:], pb[j][:, 0, :], ACT.Identity, bias=bq_sb[:])
                        nc.scalar.activation(kT[j][:], pb[j][:, 1, :], ACT.Identity, bias=bk_sb[:])\
                            .then_inc(qk_ready, 1)
                    for j in range(G):
                        act.wait_ge(max_ready, i * G + j + 1)
                        for s in range(2):
                            last = nc.scalar.activation(e[j][:, s, 0:L], pa[j][:, s, 0:L], ACT.Exp,
                                                        bias=neg_max[j][:, s:s + 1],
                                                        accum_out=total[j][:, s:s + 1])
                        last.then_inc(e_ready, 1)
                    for j in range(G):
                        act.wait_ge(by_ready, i * G + j + 1)
                        for s in range(2):
                            last = nc.scalar.activation(fall[j][:, s, 0:L], e[j][:, s, 0:L], ACT.Relu,
                                                        bias=K["inv03"][:], scale=fall_by[j][:, s:s + 1])
                        last.then_inc(fall_ready, 1)
                    for j in range(G):
                        act.wait_ge(fT_ps, i * G + j + 1)
                        nc.scalar.activation(fT[j][:], pb[j][:], ACT.Copy).then_inc(fT_ready, 1)

            @block.tensor
            def _(pe):
                pe.wait_ge(w_in, 64)
                with nc.tensor.Fori(0, B // G) as i:
                    for j in range(G):
                        pe.wait_ge(x_ready, i * G + j + 1)
                        for s in range(2):
                            last = nc.tensor.transpose(pa[j][:, 0, s * P:(s + 1) * P], x[j][:, s, :], ident[:])
                        last.then_inc(xT_ps, 1)
                    for j in range(G):
                        pe.wait_ge(xT_ready, i * G + j + 1)
                        nc.tensor.matmul(pb[j][:, 0, :], wq_sb[:], xT[j][:], start=True, stop=True)
                        nc.tensor.matmul(pb[j][:, 1, :], wk_sb[:], xT[j][:], start=True, stop=True)\
                            .then_inc(qk_ps, 1)
                    for j in range(G):
                        pe.wait_ge(qk_ready, i * G + j + 1)
                        for s in range(2):
                            last = nc.tensor.matmul(pa[j][:, s, 0:L], qT[j][:, s * P:(s + 1) * P],
                                                    kT[j][:, 0:L], start=True, stop=True)
                        last.then_inc(score_ps, 1)
                    for j in range(G):
                        pe.wait_ge(f_ready, i * G + j + 1)
                        for s in range(2):
                            for t in range(2):
                                last = nc.tensor.transpose(pb[j][:, t, s * P:(s + 1) * P],
                                                           f[j][:, s, t * P:(t + 1) * P], ident[:])
                        last.then_inc(fT_ps, 1)
                    for j in range(G):
                        pe.wait_ge(fT_ready, i * G + j + 1)
                        for s in range(2):
                            for t in range(2):
                                last = nc.tensor.matmul(pa[j][:, s, 0:D], fT[j][:, t, s * P:(s + 1) * P],
                                                        x[j][:, t, :], start=(t == 0), stop=(t == 1))
                        last.then_inc(out_ps, 1)


E0, HID0 = 8, 512
ST0 = (B * L + E0 * (P - 1)) // P + 1
ST0 += -ST0 % G
E1N, HID1, CAP, TOPK1 = 64, 64, 256, 2
SLOTS0, SLOTS1 = ST0 * P, E1N * CAP
SLOTS = max(SLOTS0, SLOTS1)


CLEARS = SLOTS // (16 * P) + 2


def clear_slots(x_slots, results, zeros, cleared, eng):
    per, again = zeros.shape[1] // D, 4
    n = per * again
    for r in range(0, SLOTS, P * n):
        eng.dma_start(x_slots[r:r + P * n, :].rearrange("(p k n) d -> p k (n d)", p=P, k=again),
                      zeros[:].unsqueeze(1).to_broadcast([P, again, per * D])).then_inc(cleared, 16)
    for y_slots, rows in results:
        eng.dma_start(y_slots[rows:rows + 1, :], zeros[0:1, 0:D]).then_inc(cleared, 16)


def router_logits(nc, K, h, mean, rstd, logits, gate, gate_bias, n_exp, stage):
    ident = K["ident"]
    with Bench(nc, stage) as m:
        gate_sb = m.sb("gate", [P, n_exp])
        bias = m.sb("bias", [P, n_exp])
        x = [m.sb(f"x{j}", [P, D]) for j in range(G)]
        xT = [m.sb(f"xT{j}", [P, P]) for j in range(G)]
        pt = [m.ps(f"pt{j}", [P, 512]) for j in range(G)]
        pl = [m.ps(f"pl{j}", [P, 512]) for j in range(G)]
        w_in, x_ready, xT_ps, xT_ready, logit_ps, read = (m.sem(n) for n in (
            "w_in", "x_ready", "xT_ps", "xT_ready", "logit_ps", "read"))
        loads = 1 if gate_bias is None else 2
        with nc.Block() as block:
            @block.sync
            def _(sp):
                sp.dma_start(gate_sb[:], gate).then_inc(w_in, 16)
                if gate_bias is not None:
                    sp.dma_start(bias[:], gate_bias.partition_broadcast(P)).then_inc(w_in, 16)
                sp.wait_ge(w_in, 16 * loads)

            @block.vector
            def _(dve):
                dve.wait_ge(w_in, 16 * loads)
                with nc.vector.Fori(0, NT // G) as i:
                    for j in range(G):
                        normalise(nc, x[j][:], h, mean, rstd, i * G + j).then_inc(x_ready, 1)
                    for j in range(G):
                        dve.wait_ge(logit_ps, i * G + j + 1)
                        to, src = one_tile(logits, i * G + j), pl[j][:, 0:n_exp]
                        if gate_bias is None:
                            nc.vector.tensor_copy(to, src).then_inc(read, 1)
                        else:
                            nc.vector.tensor_tensor(to, src, bias[:], ALU.add).then_inc(read, 1)

            @block.scalar
            def _(act):
                with nc.scalar.Fori(0, NT // G) as i:
                    for j in range(G):
                        act.wait_ge(xT_ps, i * G + j + 1)
                        nc.scalar.activation(xT[j][:], pt[j][:, 0:P], ACT.Copy).then_inc(xT_ready, 1)

            @block.tensor
            def _(pe):
                pe.wait_ge(w_in, 16 * loads)
                with nc.tensor.Fori(0, NT // G) as i:
                    for j in range(G):
                        pe.wait_ge(x_ready, i * G + j + 1)
                        nc.tensor.transpose(pt[j][:, 0:P], x[j][:], ident[:]).then_inc(xT_ps, 1)
                    for j in range(G):
                        pe.wait_ge(xT_ready, i * G + j + 1)
                        nc.tensor.matmul(pl[j][:, 0:n_exp], xT[j][:], gate_sb[:], start=True,
                                         stop=True).then_inc(logit_ps, 1)


def route_top1(nc, K, logits, scatter_at, gather_at, tile_expert):
    wide = [P, NT, E0]
    with Bench(nc, "route0") as m:
        best, first, slot = m.sb("best", [P, NT]), m.sb("first", [P, NT]), m.sb("slot", [P, NT])
        work, onehot = m.sb("work", wide), m.sb("onehot", wide)
        onehot_b = m.sb("onehot_b", wide, BF16)
        total = m.sb("total", wide)
        runs = [m.sb(f"run{k}", wide) for k in range(2)]
        ends = [m.sb(f"ends{k}", [P, E0]) for k in range(2)]
        n_tiles, starts = m.sb("n_tiles", [P, E0]), m.sb("starts", [P, E0])
        more = m.sb("more", [P, E0, NT])
        past = m.sb("past", [P, ST0, E0])
        expert_f = m.sb("expert_f", [P, ST0])
        within_ps, total_ps = m.ps("within_ps", wide), m.ps("total_ps", wide)
        vec, onehot_ready, counted = m.sem("vec"), m.sem("onehot_ready"), m.sem("counted")
        with nc.Block() as block:
            @block.vector
            def _(dve):
                link = Chain(dve, vec)
                rank = K["rank0"][:].unsqueeze(1).to_broadcast(wide)
                link(nc.vector.tensor_reduce(best[:], logits[:], AX.X, ALU.max))
                link(nc.vector.tensor_tensor(work[:], logits[:], best[:].unsqueeze(2).to_broadcast(wide),
                                             ALU.is_equal))
                link(nc.vector.tensor_tensor(work[:], work[:], rank, ALU.mult))
                link(nc.vector.tensor_reduce(first[:], work[:], AX.X, ALU.max))
                link(nc.vector.tensor_tensor(work[:], rank, first[:].unsqueeze(2).to_broadcast(wide),
                                             ALU.is_equal))
                link(nc.vector.tensor_tensor(onehot[:], work[:],
                                             K["real"][:].unsqueeze(2).to_broadcast(wide), ALU.mult))
                nc.vector.tensor_copy(onehot_b[:], onehot[:]).then_inc(onehot_ready, 1)
                dve.wait_ge(counted, 1)
                link(nc.vector.tensor_copy(total[:], total_ps[:]))
                now, then = total, runs[0]
                k = 1
                flip = 0
                while k < NT:
                    then = runs[flip]
                    nc.vector.tensor_copy(then[:, 0:k], now[:, 0:k])
                    link(nc.vector.tensor_tensor(then[:, k:NT], now[:, k:NT], now[:, 0:NT - k], ALU.add))
                    now, flip, k = then, 1 - flip, 2 * k
                count = now[:, NT - 1, :]
                link(nc.vector.tensor_tensor(more[:], count.unsqueeze(2).to_broadcast([P, E0, NT]),
                                             K["multiples"][:].unsqueeze(1).to_broadcast([P, E0, NT]),
                                             ALU.is_gt))
                link(nc.vector.tensor_reduce(n_tiles[:], more[:], AX.X, ALU.add))
                upto, k, flip2 = n_tiles, 1, 0
                while k < E0:
                    nxt = ends[flip2]
                    nc.vector.tensor_copy(nxt[:, 0:k], upto[:, 0:k])
                    link(nc.vector.tensor_tensor(nxt[:, k:E0], upto[:, k:E0], upto[:, 0:E0 - k], ALU.add))
                    upto, flip2, k = nxt, 1 - flip2, 2 * k
                link(nc.vector.tensor_tensor(starts[:], upto[:], n_tiles[:], ALU.subtract))
                link(nc.vector.tensor_scalar(starts[:], starts[:], float(P), None, ALU.mult))
                link(nc.vector.tensor_tensor(past[:], K["tile_no"][:, 0:ST0].unsqueeze(2).to_broadcast([P, ST0, E0]),
                                             upto[:].unsqueeze(1).to_broadcast([P, ST0, E0]), ALU.is_ge))
                link(nc.vector.tensor_reduce(expert_f[:], past[:], AX.X, ALU.add))
                nc.vector.tensor_scalar(tile_expert[:], expert_f[:], float(E0 - 1), None, ALU.min)
                link(nc.vector.tensor_tensor(work[:], now[:], total[:], ALU.subtract))
                link(nc.vector.tensor_tensor(work[:], work[:], within_ps[:], ALU.add))
                link(nc.vector.tensor_tensor(work[:], work[:], starts[:].unsqueeze(1).to_broadcast(wide), ALU.add))
                link(nc.vector.tensor_tensor(work[:], work[:], onehot[:], ALU.mult))
                link(nc.vector.tensor_reduce(slot[:], work[:], AX.X, ALU.add))
                nc.vector.tensor_tensor(scatter_at[:, 0, :], slot[:], K["pad_to"][:], ALU.add)
                nc.vector.tensor_tensor(gather_at[:, 0, :], slot[:], K["pad_from"][:], ALU.add)

            @block.tensor
            def _(pe):
                pe.wait_ge(onehot_ready, 1)
                nc.tensor.matmul(within_ps[:], K["after_b"][:], onehot_b[:], start=True, stop=True)
                nc.tensor.matmul(total_ps[:], K["ones_b"][:], onehot_b[:], start=True, stop=True)\
                    .then_inc(counted, 1)


def scatter_rows(nc, h, mean, rstd, x_slots, scatter_at, n_to, stage):
    with Bench(nc, stage) as m:
        x = [m.sb(f"x{j}", [P, D]) for j in range(G)]
        tick = m.sb("tick", [P, 2])
        at = [m.sb(f"at{j}", [P, n_to], U32) for j in range(G)]
        x_ready, tick_ready = m.sem("x_ready"), m.sem("tick_ready")
        sent = [m.sem(f"sent{j}") for j in range(G)]
        with nc.Block() as block:
            @block.vector
            def _(dve):
                def rows(i, first=False):
                    for j in range(G):
                        if not first:
                            dve.wait_ge(sent[j], 16 * n_to * i)
                        nc.vector.tensor_copy(at[j][:].unsqueeze(2), scatter_at[:, 0:n_to, bass.ds(i * G + j, 1)])
                        normalise(nc, x[j][:], h, mean, rstd, i * G + j).then_inc(x_ready, 1)

                rows(0, first=True)
                with nc.vector.Fori(1, NT // G) as i:
                    rows(i)

            @block.gpsimd
            def _(pool):
                nc.gpsimd.memset(tick[:], 0.0).then_inc(tick_ready, 1)
                pool.wait_ge(tick_ready, 1)
                with nc.gpsimd.Fori(0, NT // G) as i:
                    for j in range(G):
                        pool.wait_ge(tick_ready, i * G + j + 1)
                        pool.wait_ge(x_ready, i * G + j + 1)
                        nc.gpsimd.tensor_tensor(tick[:, 1:2], tick[:, 0:1], tick[:, 0:1], ALU.mult)\
                            .then_inc(tick_ready, 1)
                        for k in range(n_to):
                            nc.gpsimd.indirect_dma_start(
                                x_slots[:], bass.IndirectOffsetOnAxis(ap=at[j][:, k:k + 1], axis=0),
                                x[j][:], None).then_inc(sent[j], 16)
                for j in range(G):
                    pool.wait_ge(sent[j], 16 * n_to * (NT // G))


def gather_rows(nc, h, stats, y_slots, gather_at, weight, n_from, stage):
    with Bench(nc, stage) as m:
        y = [m.sb(f"y{j}", [P, n_from, D]) for j in range(2 * G)]
        tick = m.sb("tick", [P, 2])
        at = [m.sb(f"at{j}", [P, n_from], U32) for j in range(2 * G)]
        at_ready, h_ready, tick_ready = m.sem("at_ready"), m.sem("h_ready"), m.sem("tick_ready")
        got = [m.sem(f"got{j}") for j in range(2 * G)]
        W = 2 * G
        with nc.Block() as block:
            @block.vector
            def _(dve):
                def indices(i, j):
                    nc.vector.tensor_copy(at[j][:].unsqueeze(2), gather_at[:, 0:n_from, bass.ds(i * W + j, 1)])\
                        .then_inc(at_ready, 1)

                def add(i, j):
                    dve.wait_ge(got[j], 16 * n_from * (i + 1))
                    n = i * W + j
                    for k in range(n_from):
                        ht = one_tile(h, n)
                        if weight is None:
                            nc.vector.tensor_tensor(ht, ht, y[j][:, k, :], ALU.add).then_inc(h_ready, 1)
                        else:
                            nc.vector.scalar_tensor_tensor(ht, y[j][:, k, :], one_column(weight[k], n), ht,
                                                           ALU.mult, ALU.add).then_inc(h_ready, 1)
                        dve.wait_ge(h_ready, n_from * n + k + 1)
                    if stats is not None:
                        nc.vector.bn_stats(one_tile(stats, n), one_tile(h, n))

                for j in range(W):
                    indices(0, j)
                with nc.vector.Fori(0, NT // W - 1) as i:
                    for j in range(W):
                        add(i, j)
                        indices(i + 1, j)
                for j in range(W):
                    add(NT // W - 1, j)

            @block.gpsimd
            def _(pool):
                nc.gpsimd.memset(tick[:], 0.0).then_inc(tick_ready, 1)
                pool.wait_ge(tick_ready, 1)
                with nc.gpsimd.Fori(0, NT // W) as i:
                    for j in range(W):
                        pool.wait_ge(tick_ready, i * W + j + 1)
                        pool.wait_ge(at_ready, i * W + j + 1)
                        nc.gpsimd.tensor_tensor(tick[:, 1:2], tick[:, 0:1], tick[:, 0:1], ALU.mult)\
                            .then_inc(tick_ready, 1)
                        for k in range(n_from):
                            nc.gpsimd.indirect_dma_start(
                                y[j][:, k, :], None, y_slots[:],
                                bass.IndirectOffsetOnAxis(ap=at[j][:, k:k + 1], axis=0)).then_inc(got[j], 16)


def experts_top1(nc, K, x_slots, y_slots, tile_expert, w1, w2, b2):
    ident = K["ident"]
    HC = HID0 // P
    WIDE = HID0 + HC
    with Bench(nc, "exp0") as m:
        w1_sb = m.sb("w1", [P, E0, WIDE])
        w2_sb = m.sb("w2", [P, E0, HC * D])
        b2_sb = m.sb("b2", [P, E0, D])
        w1j = [m.sb(f"w1_{j}", [P, WIDE]) for j in range(G)]
        w2j = [m.sb(f"w2_{j}", [P, HC * D]) for j in range(G)]
        x = [m.sb(f"x{j}", [P, D]) for j in range(G)]
        xT = [m.sb(f"xT{j}", [P, P]) for j in range(G)]
        hid = [m.sb(f"hid{j}", [P, HC, P]) for j in range(G)]
        y = [m.sb(f"y{j}", [P, D]) for j in range(G)]
        pa = [m.ps(f"pa{j}", [P, 512]) for j in range(G)]
        pb = [m.ps(f"pb{j}", [P, HC, P]) for j in range(G)]
        w_in = m.sem("w_in")
        x_in = [m.sem(f"x_in{j}") for j in range(G)]
        y_out = [m.sem(f"y_out{j}") for j in range(G)]
        xT_ps, xT_ready, w1_ready, w2_ready, hid_ps, hid_a, hid_v, y_ps, y_ready = (m.sem(n) for n in (
            "xT_ps xT_ready w1_ready w2_ready hid_ps hid_a hid_v y_ps y_ready").split())
        N = ST0 // G
        with nc.Block() as block:
            @block.sync
            def _(sp):
                def rows(n):
                    return x_slots[bass.ds(n * P, P), :]

                for j in range(G):
                    sp.dma_start(x[j][:], rows(j)).then_inc(x_in[j], 16)
                sp.dma_start(w1_sb[:], w1).then_inc(w_in, 16)
                sp.dma_start(w2_sb[:], w2).then_inc(w_in, 16)
                sp.dma_start(b2_sb[:].rearrange("p e d -> p (e d)"),
                             b2.partition_broadcast(P)).then_inc(w_in, 16)

                def store(i):
                    for j in range(G):
                        sp.wait_ge(y_ready, i * G + j + 1)
                        sp.dma_start(y_slots[bass.ds((i * G + j) * P, P), :], y[j][:]).then_inc(y_out[j], 16)

                with nc.sync.Fori(0, N - 1) as i:
                    for j in range(G):
                        sp.wait_ge(xT_ps, i * G + j + 1)
                        sp.dma_start(x[j][:], rows((i + 1) * G + j)).then_inc(x_in[j], 16)
                    store(i)
                store(N - 1)
                sp.wait_ge(w_in, 48)
                for j in range(G):
                    sp.wait_ge(y_out[j], 16 * N)

            @block.vector
            def _(dve):
                dve.wait_ge(w_in, 48)

                def expert(n):
                    return nc.vector.value_load(tile_expert[0:1, bass.ds(n, 1)], min_val=0, max_val=E0 - 1)

                def pass_(i, first=False):
                    for j in range(G):
                        ex = expert(i * G + j)
                        if not first:
                            dve.wait_ge(hid_ps, i * G + j + 1 - G)
                            dve.wait_ge(hid_a, i * G + j + 1 - G)
                            dve.wait_ge(hid_v, i * G + j + 1 - G)
                        nc.vector.tensor_copy(w1j[j][:], w1_sb[:, bass.ds(ex, 1), :].rearrange("p a n -> p (a n)"))\
                            .then_inc(w1_ready, 1)
                    for j in range(G):
                        dve.wait_ge(hid_a, i * G + j + 1)
                        for c in range(HC // 2, HC):
                            last = nc.vector.tensor_scalar(hid[j][:, c, :], pb[j][:, c, :],
                                                           w1j[j][:, HID0 + c:HID0 + c + 1], 0.0,
                                                           ALU.add, ALU.max)
                        last.then_inc(hid_v, 1)
                    for j in range(G):
                        ex = expert(i * G + j)
                        dve.wait_ge(y_ps, i * G + j + 1)
                        if not first:
                            dve.wait_ge(y_out[j], 16 * i)
                        nc.vector.tensor_tensor(y[j][:], pa[j][:, P:2 * P],
                                                b2_sb[:, bass.ds(ex, 1), :].rearrange("p a n -> p (a n)"),
                                                ALU.add).then_inc(y_ready, 1)

                pass_(0, first=True)
                with nc.vector.Fori(1, N) as i:
                    pass_(i)

            @block.scalar
            def _(act):
                act.wait_ge(w_in, 48)

                def pass_(i, first=False):
                    for j in range(G):
                        act.wait_ge(xT_ps, i * G + j + 1)
                        nc.scalar.activation(xT[j][:], pa[j][:, 0:P], ACT.Copy).then_inc(xT_ready, 1)
                    for j in range(G):
                        ex = nc.scalar.value_load(tile_expert[0:1, bass.ds(i * G + j, 1)],
                                                  min_val=0, max_val=E0 - 1)
                        nc.scalar.activation(w2j[j][:], w2_sb[:, bass.ds(ex, 1), :].rearrange("p a n -> p (a n)"),
                                             ACT.Copy).then_inc(w2_ready, 1)
                    for j in range(G):
                        act.wait_ge(hid_ps, i * G + j + 1)
                        for c in range(HC // 2):
                            last = nc.scalar.activation(hid[j][:, c, :], pb[j][:, c, :], ACT.Relu,
                                                        bias=w1j[j][:, HID0 + c:HID0 + c + 1])
                        last.then_inc(hid_a, 1)

                with nc.scalar.Fori(0, N) as i:
                    pass_(i)

            @block.tensor
            def _(pe):
                def pass_(i, first=False):
                    for j in range(G):
                        pe.wait_ge(x_in[j], 16 * (i + 1))
                        if not first:
                            pe.wait_ge(y_ready, i * G + j + 1 - G)
                        nc.tensor.transpose(pa[j][:, 0:P], x[j][:], ident[:]).then_inc(xT_ps, 1)
                    for j in range(G):
                        pe.wait_ge(xT_ready, i * G + j + 1)
                        pe.wait_ge(w1_ready, i * G + j + 1)
                        for c in range(HC):
                            last = nc.tensor.matmul(pb[j][:, c, :], w1j[j][:, c * P:(c + 1) * P], xT[j][:],
                                                    start=True, stop=True)
                        last.then_inc(hid_ps, 1)
                    for j in range(G):
                        pe.wait_ge(hid_v, i * G + j + 1)
                        pe.wait_ge(w2_ready, i * G + j + 1)
                        for c in range(HC):
                            last = nc.tensor.matmul(pa[j][:, P:2 * P], hid[j][:, c, :],
                                                    w2j[j][:, c * D:(c + 1) * D],
                                                    start=(c == 0), stop=(c == HC - 1))
                        last.then_inc(y_ps, 1)

                pass_(0, first=True)
                with nc.tensor.Fori(1, N) as i:
                    pass_(i)


H, HD, MAX_REL = 8, 16, 68
HALF = 8
BQ = 2 * HALF
NBLK = T // BQ
GB = 4
NGRP = NBLK // GB
REACH = MAX_REL - 1
KWIN = 2 * REACH + BQ + HALF
VWIN = P + T
FARWIN = 2 * T - BQ


def near_tiles(blk):
    q0 = BQ * blk
    return [t for t in range(2) if t * P - (q0 + BQ - 1) < MAX_REL and t * P + P - 1 - q0 > -MAX_REL]


def relative_attention(nc, K, h, mean, rstd, stats, o_rows, wq, bq, wk, bk, wv, bv, wo, bo,
                       rep, far_keys, value_ends, key_table, value_table):
    SCALE = 1.0 / float(D) ** 0.5
    ident = K["ident"]
    with Bench(nc, "rel") as m:
        wq_sb, wk_sb, wv_sb, wo_sb = (m.sb(n, [P, D]) for n in ("wq", "wk", "wv", "wo"))
        bq_sb, bk_sb = m.sb("bq", [P, 1]), m.sb("bk", [P, 1])
        bv_sb, bo_sb = m.sb("bv", [P, D]), m.sb("bo", [P, D])
        rep_sb, rep_r = m.sb("rep", [P, H, P]), m.sb("rep_r", [P, H, P], FP32R)
        far_sb, vends_sb = m.sb("far_keys", [P, FARWIN]), m.sb("value_ends", [P, 2, D])
        ktab, vtab = m.sb("ktab", [P, KWIN]), m.sb("vtab", [P, VWIN, HD])
        x, xT, qT = m.sb("x", [P, 2, D]), m.sb("xT", [P, T]), m.sb("qT", [P, T])
        q_p = [m.sb(f"qT_{k}", [P, T], FP32R) for k in "hl"]
        kT = [m.sb(f"kT{r}", [P, T]) for r in range(2)]
        k_grp = [m.sb(f"k_grp{r}", [P, GB, T]) for r in range(2)]
        v = [m.sb(f"v{r}", [P, 2, D]) for r in range(2)]
        v_far = [m.sb(f"v_far{r}", [P, 2, D]) for r in range(2)]
        q_head = [m.sb(f"q_head{r}", [P, 2 * NBLK, H, HALF]) for r in range(2)]
        q_pos = [m.sb(f"q_pos{r}", [P, 2 * NBLK, H, HALF]) for r in range(2)]
        den = [m.sb(f"den{r}", [P, NBLK]) for r in range(2)]
        e = [m.sb(f"e{r}", [P, GB, T]) for r in range(2)]
        neg_max = [m.sb(f"neg_max{r}", [P, GB]) for r in range(2)]
        bias = [m.sb(f"bias{r}", [P, GB]) for r in range(2)]
        eT = m.sb("eT", [P, GB, 2, P])
        kept = m.sb("kept", [P, GB, 2 * D])
        o, o_norm, rden = m.sb("o", [P, NBLK, HD]), m.sb("o_norm", [P, NBLK, HD]), m.sb("rden", [P, NBLK])
        o_tok = m.sb("o_tok", [P, 2, D])
        oT = m.sb("oT", [P, T])
        s_ps = m.ps("s_ps", [P, GB, T])
        t_ps = m.ps("t_ps", [P, GB, 2, P])
        pv_ps = m.ps("pv_ps", [P, GB, 2 * D])
        pa, pb = m.ps("pa", [P, 2, T]), m.ps("pb", [P, 2, T])
        (w_in, ready, x_ready, xT_done, xT_ready, qk_done, q_ready, k_ready, kg_ready, ql_ready, qh_ready, qp_done,
         qp_ready, v_done, v_ready, s_done, max_ready, bias_ready, e_ready, t_done, eT_a, eT_v,
         pv_done, kept_ready, o_part, rden_ready, o_ready, o_out, o_in, oT_done, oT_ready, out_done,
         h_ready) = (m.sem(n) for n in (
             "w_in ready x_ready xT_done xT_ready qk_done q_ready k_ready kg_ready ql_ready qh_ready qp_done "
             "qp_ready v_done v_ready s_done max_ready bias_ready e_ready t_done eT_a eT_v "
             "pv_done kept_ready o_part rden_ready o_ready o_out o_in oT_done oT_ready out_done "
             "h_ready").split())
        mask16, mask_pv = K["mask16"], K["mask_pv"]
        loads = [(wq_sb, wq), (wk_sb, wk), (bq_sb, bq), (bk_sb, bk), (rep_sb, rep), (far_sb, far_keys),
                 (vends_sb, value_ends.partition_broadcast(P)), (wv_sb, wv), (bv_sb, bv.partition_broadcast(P)),
                 (ktab, key_table), (vtab, value_table), (wo_sb, wo), (bo_sb, bo.partition_broadcast(P))]

        def run(engine, slot, head, tail):
            def pair(i, first=False, last=False):
                for r in range(2):
                    for g in range(NGRP):
                        slot(2 * i + r, g, r, first and r == 0, last and r == 1)
            head()
            pair(0, first=True)
            with engine.Fori(1, B // 2 - 1) as i:
                pair(i)
            pair(B // 2 - 1, last=True)
            tail()

        with nc.Block() as block:
            @block.sync
            def _(sp):
                for dst, src in loads:
                    sp.dma_start(dst[:], src).then_inc(w_in, 16)
                sp.wait_ge(w_in, 16 * len(loads))

                def turn_rows(b, r, first=False):
                    sp.wait_ge(o_ready, b + 1)
                    sp.dma_start(o_rows[r].rearrange("s p k -> p s k"),
                                 o_norm[:].rearrange("p (s n) d -> p s (n d)", s=2)).then_inc(o_out, 16)
                    sp.wait_ge(o_out, 16 * b + 16)
                    if not first:
                        sp.wait_ge(oT_done, b)
                    for s in range(2):
                        for a in range(2):
                            sp.dma_start(o_tok[64 * a:64 * a + 64, s, :].rearrange("p (h d) -> p h d", h=H),
                                         o_rows[r][s, 64 * a:64 * a + 64, :]
                                         .rearrange("(h i) (n d) -> (i n) h d", h=H, d=HD)).then_inc(o_in, 16)

                turn_rows(0, 0, first=True)
                turn_rows(1, 1)
                with nc.sync.Fori(1, B // 2) as i:
                    for r in range(2):
                        turn_rows(2 * i + r, r)
                sp.wait_ge(o_in, 64 * B)

            @block.tensor
            def _(pe):
                def turn_x(b):
                    pe.wait_ge(x_ready, b + 1)
                    for s in range(2):
                        last = nc.tensor.transpose(pa[:, 0, s * P:(s + 1) * P], x[:, s, :], ident[:])
                    last.then_inc(xT_done, 1)

                def project_qk(b):
                    pe.wait_ge(xT_ready, b + 1)
                    nc.tensor.matmul(pa[:, 0, :], wq_sb[:], xT[:], start=True, stop=True)
                    nc.tensor.matmul(pa[:, 1, :], wk_sb[:], xT[:], start=True, stop=True).then_inc(qk_done, 1)

                def project_rest(b, pb_free=False):
                    pe.wait_ge(ql_ready, b + 1)
                    pe.wait_ge(k_ready, b + 1)
                    for c in range(H // 2):
                        if c == 1 and not pb_free:
                            pe.wait_ge(h_ready, 2 * b - 5)
                        if c >= 2:
                            pe.wait_ge(qp_ready, 4 * b + c - 1)
                        for n in range(2):
                            for k in range(2):
                                last = nc.tensor.matmul((pa, pb)[c % 2][:, n, :], rep_r[:, 2 * c + n, :], q_p[k][:],
                                                        start=(k == 0), stop=(k == 1))
                        last.then_inc(qp_done, 1)
                    pe.wait_ge(qp_ready, 4 * b + 3)
                    for s in range(2):
                        last = nc.tensor.matmul(pa[:, 0, s * P:(s + 1) * P], xT[:, s * P:(s + 1) * P], wv_sb[:],
                                                start=True, stop=True)
                    last.then_inc(v_done, 1)

                def scores(b, g, r, first=False):
                    if g == 0:
                        pe.wait_ge(qh_ready, b + 1)
                        pe.wait_ge(qp_ready, 4 * b + 4)
                    pe.wait_ge(kg_ready, NGRP * b + g + 1)
                    if not first:
                        pe.wait_ge(e_ready, NGRP * b + g)
                    for n in range(GB):
                        blk = GB * g + n
                        q0 = BQ * blk
                        near = max(0, q0 - REACH), min(L, q0 + BQ + REACH)
                        stationary = q_head[r][:, 2 * blk:2 * blk + 2].rearrange("p a h i -> p (a h i)")
                        nc.tensor.matmul(s_ps[:, n, 0:L], stationary, k_grp[g % 2][:, n, 0:L],
                                         start=True, stop=False, skip_group_check=True)
                        for a in range(2):
                            off = REACH + HALF - q0 - HALF * a
                            last = nc.tensor.matmul(
                                s_ps[64 * a:64 * a + 64, n, near[0]:near[1]],
                                q_pos[r][:, 2 * blk + a].rearrange("p h i -> p (h i)"),
                                ktab[:, near[0] + off:near[1] + off], start=False, stop=True,
                                skip_group_check=True)
                    last.then_inc(s_done, 1)

                def turn_e(b, g):
                    pe.wait_ge(e_ready, NGRP * b + g + 1)
                    for n in range(GB):
                        for t in range(2):
                            last = nc.tensor.transpose(t_ps[:, n, t, :], e[g % 2][:, n, t * P:(t + 1) * P], ident[:])
                    last.then_inc(t_done, 1)

                def values(b, g, r, first=False):
                    pe.wait_ge(eT_a, NGRP * b + g + 1)
                    pe.wait_ge(eT_v, NGRP * b + g + 1)
                    if g == 0:
                        pe.wait_ge(v_ready, b + 1)
                    if not first:
                        pe.wait_ge(kept_ready, NGRP * b + g)
                    for n in range(GB):
                        blk = GB * g + n
                        for t in range(2):
                            values_of = v if t in near_tiles(blk) else v_far
                            nc.tensor.matmul(pv_ps[:, n, 0:D], eT[:, n, t, :], values_of[r][:, t, :],
                                             start=(t == 0), stop=(t == 1), skip_group_check=True)
                        for a in range(2):
                            near = near_tiles(blk)
                            for t in near:
                                u = P + BQ * blk + HALF * a - P * t
                                last = nc.tensor.matmul(
                                    pv_ps[64 * a:64 * a + 64, n, D:2 * D], eT[:, n, t, 64 * a:64 * a + 64],
                                    vtab[:, u:u + HALF, :].rearrange("p u d -> p (u d)"),
                                    start=(t == near[0]), stop=(t == near[-1]), skip_group_check=True)
                    last.then_inc(pv_done, 1)

                def turn_o(b, last=False):
                    pe.wait_ge(o_in, 64 * b + 64)
                    pe.wait_ge(qp_ready, 4 * b + (4 if last else 12))
                    for s in range(2):
                        last = nc.tensor.transpose(pb[:, 0, s * P:(s + 1) * P], o_tok[:, s, :], ident[:])
                    last.then_inc(oT_done, 1)

                def project_out(b):
                    pe.wait_ge(oT_ready, b + 1)
                    for s in range(2):
                        last = nc.tensor.matmul(pb[:, 0, s * P:(s + 1) * P], oT[:, s * P:(s + 1) * P], wo_sb[:],
                                                start=True, stop=True)
                    last.then_inc(out_done, 1)

                def slot(b, g, r, first, last):
                    turn_e(b, g)
                    if g + 1 < NGRP:
                        scores(b, g + 1, r)
                    elif not last:
                        scores(b + 1, 0, 1 - r)
                    if g == 0 and not last:
                        turn_x(b + 1)
                    if g == 1 and not last:
                        project_qk(b + 1)
                    if g == 2 and not last:
                        project_rest(b + 1, pb_free=isinstance(b, int) and b < 2)
                    if g == 3 and not first:
                        turn_o(b - 1, last)
                    values(b, g, r, first and g == 0)
                    if g == 3 and not first:
                        project_out(b - 1)

                def head():
                    pe.wait_ge(w_in, 16 * len(loads))
                    turn_x(0)
                    project_qk(0)
                    project_rest(0, pb_free=True)
                    scores(0, 0, 0, first=True)

                def tail():
                    pe.wait_ge(h_ready, 2 * B - 3)
                    turn_o(B - 1, last=True)
                    project_out(B - 1)

                run(nc.tensor, slot, head, tail)

            @block.scalar
            def _(act):
                def read_x(b):
                    act.wait_ge(xT_done, b + 1)
                    nc.scalar.activation(xT[:], pa[:, 0, :], ACT.Copy).then_inc(xT_ready, 1)

                def read_qk(b, r):
                    act.wait_ge(qk_done, b + 1)
                    nc.scalar.activation(qT[:], pa[:, 0, :], ACT.Identity, bias=bq_sb[:])
                    nc.scalar.activation(q_p[0][:], pa[:, 0, :], ACT.Identity, bias=bq_sb[:]).then_inc(q_ready, 1)
                    nc.scalar.activation(kT[r][:], pa[:, 1, :], ACT.Identity, bias=bk_sb[:]).then_inc(k_ready, 1)

                def exps(b, g, r):
                    act.wait_ge(bias_ready, NGRP * b + g + 1)
                    for n in range(GB):
                        last = nc.scalar.activation(e[g % 2][:, n, 0:L], s_ps[:, n, 0:L], ACT.Exp,
                                                    bias=bias[g % 2][:, n:n + 1], scale=SCALE,
                                                    accum_out=den[r][:, GB * g + n:GB * g + n + 1])
                    last.then_inc(e_ready, 1)

                def read_eT(b, g):
                    act.wait_ge(t_done, NGRP * b + g + 1)
                    nc.scalar.activation(eT[:, 0:2], t_ps[:, 0:2], ACT.Copy).then_inc(eT_a, 1)

                def read_o(b):
                    act.wait_ge(oT_done, b + 1)
                    for s in range(2):
                        last = nc.scalar.activation(
                            oT[:, s * P:(s + 1) * P].rearrange("p (n a i) -> p a i n", a=2, i=HALF),
                            pb[:, 0, s * P:(s + 1) * P].rearrange("p (a i n) -> p a i n", a=2, i=HALF), ACT.Copy)
                    last.then_inc(oT_ready, 1)

                def slot(b, g, r, first, last):
                    read_eT(b, g)
                    if g + 1 < NGRP:
                        exps(b, g + 1, r)
                    elif not last:
                        exps(b + 1, 0, 1 - r)
                    if g == 0 and not last:
                        read_x(b + 1)
                    if g == 1 and not last:
                        read_qk(b + 1, 1 - r)
                    if g == 3 and not first:
                        read_o(b - 1)

                def head():
                    act.wait_ge(ready, 1)
                    read_x(0)
                    read_qk(0, 0)
                    exps(0, 0, 0)

                run(nc.scalar, slot, head, lambda: read_o(B - 1))

            @block.gpsimd
            def _(pool):
                def queries(b, r):
                    pool.wait_ge(q_ready, b + 1)
                    wide = [P, 2 * NBLK, H, HALF]
                    nc.gpsimd.tensor_tensor(
                        q_head[r][:], qT[:].rearrange("p (n i) -> p n i", i=HALF).unsqueeze(2).to_broadcast(wide),
                        mask16[:].unsqueeze(1).unsqueeze(3).to_broadcast(wide), ALU.mult).then_inc(qh_ready, 1)

                def keys(b, g, r, early=False):
                    if g == 0:
                        pool.wait_ge(k_ready, b + 1)
                    if not early:
                        pool.wait_ge(s_done, NGRP * b + g - 1)
                    for n in range(GB):
                        u = T - BQ - BQ * (GB * g + n)
                        last = nc.gpsimd.tensor_tensor(k_grp[g % 2][:, n, :], kT[r][:], far_sb[:, u:u + T], ALU.add)
                    last.then_inc(kg_ready, 1)

                def slot(b, g, r, first, last):
                    if g < 2:
                        keys(b, g + 2, r)
                    elif not last:
                        keys(b + 1, g - 2, 1 - r)
                    if g == 1 and not last:
                        queries(b + 1, 1 - r)

                def head():
                    pool.wait_ge(w_in, 16 * len(loads))
                    keys(0, 0, 0, early=True)
                    queries(0, 0)
                    keys(0, 1, 0, early=True)

                run(nc.gpsimd, slot, head, lambda: None)

            @block.vector
            def _(dve):
                def read_x(b):
                    normalise(nc, x[:, 0, :], h, mean, rstd, 2 * b)
                    normalise(nc, x[:, 1, :], h, mean, rstd, 2 * b + 1).then_inc(x_ready, 1)

                def q_remainder(b):
                    dve.wait_ge(q_ready, b + 1)
                    rest(nc.vector, q_p[1][:], qT[:], q_p[0][:]).then_inc(ql_ready, 1)

                def read_rest(b, r):
                    for c in range(H // 2):
                        dve.wait_ge(qp_done, 4 * b + c + 1)
                        last = nc.vector.tensor_tensor(
                            q_pos[r][:, :, 2 * c:2 * c + 2, :],
                            (pa, pb)[c % 2][:].rearrange("p n (k i) -> p k n i", i=HALF),
                            mask16[:].unsqueeze(1).unsqueeze(1).to_broadcast([P, 2 * NBLK, 2, HALF]), ALU.mult)
                        last.then_inc(qp_ready, 1)
                    dve.wait_ge(v_done, b + 1)
                    for to, bias_sb in ((v, bv_sb[:].unsqueeze(1).to_broadcast([P, 2, D])), (v_far, vends_sb[:])):
                        last = nc.vector.tensor_tensor(to[r][:], pa[:, 0, :].rearrange("p (s d) -> p s d", s=2),
                                                       bias_sb, ALU.add)
                    last.then_inc(v_ready, 1)

                def maxima(b, g):
                    dve.wait_ge(s_done, NGRP * b + g + 1)
                    nc.vector.tensor_reduce(neg_max[g % 2][:], s_ps[:, :, 0:L], AX.X, ALU.max, negate=True)\
                        .then_inc(max_ready, 1)
                    dve.wait_ge(max_ready, NGRP * b + g + 1)
                    nc.vector.tensor_scalar(bias[g % 2][:], neg_max[g % 2][:], SCALE, None, ALU.mult)\
                        .then_inc(bias_ready, 1)

                def read_eT(b, g):
                    dve.wait_ge(t_done, NGRP * b + g + 1)
                    nc.vector.tensor_copy(eT[:, 2:4], t_ps[:, 2:4]).then_inc(eT_v, 1)

                def keep(b, g, r, first):
                    dve.wait_ge(pv_done, NGRP * b + g + 1)
                    if not (first and g == 0):
                        dve.wait_ge(o_part, NGRP * b + g)
                    if g == 0 and not first:
                        dve.wait_ge(o_ready, b)
                    nc.vector.tensor_tensor(kept[:], pv_ps[:], mask_pv[:].unsqueeze(1).to_broadcast([P, GB, 2 * D]),
                                            ALU.mult).then_inc(kept_ready, 1)
                    dve.wait_ge(kept_ready, NGRP * b + g + 1)
                    nc.vector.tensor_reduce(o[:, GB * g:GB * g + GB, :],
                                            kept[:].rearrange("p n (k d) -> p n d k", d=HD), AX.X, ALU.add)\
                        .then_inc(o_part, 1)
                    if g == NGRP - 1:
                        nc.vector.reciprocal(rden[:], den[r][:]).then_inc(rden_ready, 1)
                        dve.wait_ge(rden_ready, b + 1)
                        dve.wait_ge(o_part, NGRP * b + NGRP)
                        if not first:
                            dve.wait_ge(o_out, 16 * b)
                        nc.vector.tensor_tensor(o_norm[:], o[:], rden[:].unsqueeze(2).to_broadcast([P, NBLK, HD]),
                                                ALU.mult).then_inc(o_ready, 1)

                def add_out(b):
                    dve.wait_ge(out_done, b + 1)
                    hb = h[:, bass.ds(2 * b, 2), :]
                    nc.vector.tensor_tensor(hb, hb, pb[:, 0, :].rearrange("p (s d) -> p s d", s=2), ALU.add)\
                        .then_inc(h_ready, 1)
                    dve.wait_ge(h_ready, 2 * b + 1)
                    nc.vector.tensor_tensor(hb, hb, bo_sb[:].unsqueeze(1).to_broadcast([P, 2, D]), ALU.add)\
                        .then_inc(h_ready, 1)
                    dve.wait_ge(h_ready, 2 * b + 2)
                    for s in range(2):
                        nc.vector.bn_stats(one_tile(stats, 2 * b + s), one_tile(h, 2 * b + s))

                def slot(b, g, r, first, last):
                    if g == 0 and not last:
                        read_x(b + 1)
                    read_eT(b, g)
                    if g + 1 < NGRP:
                        maxima(b, g + 1)
                    elif not last:
                        maxima(b + 1, 0)
                    if g == 1 and not last:
                        q_remainder(b + 1)
                    if g == 2 and not last:
                        read_rest(b + 1, 1 - r)
                    keep(b, g, r, first)
                    if g == 3 and not first:
                        add_out(b - 1)

                def head():
                    for r in range(2):
                        nc.vector.memset(e[r][:, :, L:T], 0.0)
                    dve.wait_ge(w_in, 16 * len(loads))
                    nc.vector.tensor_copy(rep_r[:], rep_sb[:])
                    nc.vector.tensor_tensor(vends_sb[:], vends_sb[:], bv_sb[:].unsqueeze(1).to_broadcast([P, 2, D]),
                                            ALU.add).then_inc(ready, 1)
                    dve.wait_ge(ready, 1)
                    read_x(0)
                    q_remainder(0)
                    read_rest(0, 0)
                    maxima(0, 0)

                run(nc.vector, slot, head, lambda: add_out(B - 1))


ROUTE_SCALE = 2.5


def route_top2(nc, K, logits, scatter_at, gather_at, weight):
    wide = [P, NT, E1N]
    CH = 512 // E1N
    with Bench(nc, "route1") as m:
        work, total = m.sb("work", wide), m.sb("total", wide)
        onehot = [m.sb(f"onehot{k}", wide) for k in range(TOPK1)]
        both = m.sb("both", wide, BF16)
        run = m.sb("run", wide)
        best, first = m.sb("best", [P, TOPK1, NT]), m.sb("first", [P, TOPK1, NT])
        place, valid = m.sb("place", [P, TOPK1, NT]), m.sb("valid", [P, TOPK1, NT])
        row, other = m.sb("row", [P, TOPK1, NT]), m.sb("other", [P, TOPK1, NT])
        sig, sums = m.sb("sig", [P, TOPK1, NT]), m.sb("sums", [P, NT])
        count_ps = m.ps("count_ps", wide)
        vec, both_ready, totals_done, totals_read, within_done = (m.sem(n) for n in (
            "vec", "both_ready", "totals_done", "totals_read", "within_done"))
        best_ready, sig_ready = m.sem("best_ready"), m.sem("sig_ready")
        with nc.Block() as block:
            @block.vector
            def _(dve):
                link = Chain(dve, vec)
                rank = K["rank1"][:].unsqueeze(1).to_broadcast(wide)
                real = K["real"][:].unsqueeze(2).to_broadcast(wide)
                values = logits
                for k in range(TOPK1):
                    link(nc.vector.tensor_reduce(best[:, k], values[:], AX.X, ALU.max))
                    link(nc.vector.tensor_tensor(work[:], values[:],
                                                 best[:, k].unsqueeze(2).to_broadcast(wide), ALU.is_equal))
                    link(nc.vector.tensor_tensor(work[:], work[:], rank, ALU.mult))
                    link(nc.vector.tensor_reduce(first[:, k], work[:], AX.X, ALU.max))
                    link(nc.vector.tensor_tensor(onehot[k][:], rank,
                                                 first[:, k].unsqueeze(2).to_broadcast(wide), ALU.is_equal))
                    if k == 0:
                        link(nc.vector.scalar_tensor_tensor(logits[:], onehot[0][:], -3.0e38, logits[:],
                                                            ALU.mult, ALU.add))
                nc.vector.memset(sums[:], 0.0).then_inc(best_ready, 1)
                link(nc.vector.tensor_tensor(work[:], onehot[0][:], onehot[1][:], ALU.add))
                nc.vector.tensor_tensor(both[:], work[:], real, ALU.mult).then_inc(both_ready, 1)
                dve.wait_ge(totals_done, 1)
                nc.vector.tensor_copy(total[:], count_ps[:]).then_inc(totals_read, 1)
                dve.wait_ge(totals_read, 1)
                now, then, k = total, run, 1
                spare = work
                while k < NT:
                    nc.vector.tensor_copy(then[:, 0:k], now[:, 0:k])
                    link(nc.vector.tensor_tensor(then[:, k:NT], now[:, k:NT], now[:, 0:NT - k], ALU.add))
                    now, then, k = then, (spare if then is run else run), 2 * k
                dve.wait_ge(within_done, 1)
                link(nc.vector.tensor_tensor(then[:], now[:], total[:], ALU.subtract))
                link(nc.vector.tensor_tensor(then[:], then[:], count_ps[:], ALU.add))
                for k in range(TOPK1):
                    link(nc.vector.tensor_tensor(onehot[k][:], onehot[k][:], then[:], ALU.mult))
                    link(nc.vector.tensor_reduce(place[:, k], onehot[k][:], AX.X, ALU.add))
                real2 = K["real"][:].unsqueeze(1).to_broadcast([P, TOPK1, NT])
                link(nc.vector.tensor_scalar(valid[:], place[:], float(CAP), None, ALU.is_lt))
                link(nc.vector.tensor_tensor(valid[:], valid[:], real2, ALU.mult))
                link(nc.vector.tensor_scalar(row[:], first[:], -float(CAP), float(CAP * E1N), ALU.mult, ALU.add))
                link(nc.vector.tensor_tensor(row[:], row[:], place[:], ALU.add))
                link(nc.vector.tensor_tensor(row[:], row[:], valid[:], ALU.mult))
                link(nc.vector.tensor_scalar(other[:], valid[:], -1.0, 1.0, ALU.mult, ALU.add))
                link(nc.vector.scalar_tensor_tensor(place[:], other[:], float(SLOTS1), row[:], ALU.mult, ALU.add))
                link(nc.vector.tensor_copy(gather_at[:], place[:]))
                link(nc.vector.tensor_tensor(other[:], other[:], K["spill"][:].rearrange("p (k n) -> p k n", k=TOPK1),
                                             ALU.mult))
                link(nc.vector.tensor_tensor(other[:], other[:], row[:], ALU.add))
                nc.vector.tensor_copy(scatter_at[:], other[:])
                dve.wait_ge(sig_ready, 1)
                link(nc.vector.tensor_tensor(sums[:], sig[:, 0], sig[:, 1], ALU.add))
                link(nc.vector.tensor_scalar(sums[:], sums[:], 1e-20, None, ALU.add))
                link(nc.vector.reciprocal(sums[:], sums[:]))
                link(nc.vector.tensor_tensor(sig[:], sig[:], sums[:].unsqueeze(1).to_broadcast([P, TOPK1, NT]),
                                             ALU.mult))
                link(nc.vector.scalar_tensor_tensor(weight[:], sig[:], ROUTE_SCALE, valid[:], ALU.mult, ALU.mult))

            @block.scalar
            def _(act):
                act.wait_ge(best_ready, 1)
                nc.scalar.activation(sig[:], best[:], ACT.Sigmoid).then_inc(sig_ready, 1)

            @block.tensor
            def _(pe):
                def count(ones):
                    for c in range(NT // CH):
                        last = nc.tensor.matmul(count_ps[:, CH * c:CH * c + CH, :], ones[:],
                                                both[:, CH * c:CH * c + CH, :], start=True, stop=True)
                    return last

                pe.wait_ge(both_ready, 1)
                count(K["ones_b"]).then_inc(totals_done, 1)
                pe.wait_ge(totals_read, 1)
                count(K["after_b"]).then_inc(within_done, 1)


def scatter_and_share(nc, K, h, mean, rstd, x_slots, scatter_at, sw1, sw3, sw2):
    ident = K["ident"]
    with Bench(nc, "share") as m:
        sw1_sb, sw3_sb, sw2_sb = m.sb("sw1", [P, P]), m.sb("sw3", [P, P]), m.sb("sw2", [P, D])
        x = [m.sb(f"x{j}", [P, D]) for j in range(2 * G)]
        tick = m.sb("tick", [P, 2])
        at = [m.sb(f"at{j}", [P, TOPK1], U32) for j in range(2 * G)]
        xT, gate, act1 = m.sb("xT", [P, G * P]), m.sb("gate", [P, G * P]), m.sb("act1", [P, G * P])
        pt, p1, p3, py = (m.ps(n, [P, G * P]) for n in ("pt", "p1", "p3", "py"))
        w_in, x_ready, tick_ready, xT_ps, xT_ready, up_done, gate_ready, half_ready, act_ready, y_done, h_ready = (
            m.sem(n) for n in "w_in x_ready tick_ready xT_ps xT_ready up_done gate_ready half_ready act_ready y_done h_ready".split())
        sent = [m.sem(f"sent{j}") for j in range(2 * G)]
        NG = NT // G
        with nc.Block() as block:
            @block.sync
            def _(sp):
                for dst, src in ((sw1_sb, sw1), (sw3_sb, sw3), (sw2_sb, sw2)):
                    sp.dma_start(dst[:], src).then_inc(w_in, 16)
                sp.wait_ge(w_in, 48)

            @block.vector
            def _(dve):
                def rows(i, r, first=False):
                    for j in range(G):
                        q = r * G + j
                        n = (2 * i + r) * G + j
                        if not first:
                            dve.wait_ge(sent[q], 16 * TOPK1 * i)
                        nc.vector.tensor_copy(at[q][:].unsqueeze(2), scatter_at[:, :, bass.ds(n, 1)])
                        normalise(nc, x[q][:], h, mean, rstd, n).then_inc(x_ready, 1)

                def share(g):
                    dve.wait_ge(gate_ready, g + 1)
                    nc.vector.tensor_tensor(act1[:], gate[:], p1[:], ALU.mult).then_inc(half_ready, 1)
                    dve.wait_ge(half_ready, g + 1)
                    nc.vector.tensor_tensor(act1[:], act1[:], p3[:], ALU.mult).then_inc(act_ready, 1)
                    dve.wait_ge(y_done, g + 1)
                    ht = h[:, bass.ds(g * G, G), :]
                    nc.vector.tensor_tensor(ht, ht, py[:].rearrange("p (n d) -> p n d", d=D), ALU.add)\
                        .then_inc(h_ready, 1)

                rows(0, 0, first=True)
                rows(0, 1, first=True)
                share(0)
                with nc.vector.Fori(1, NG // 2) as i:
                    rows(i, 0)
                    share(2 * i - 1)
                    rows(i, 1)
                    share(2 * i)
                share(NG - 1)

            @block.gpsimd
            def _(pool):
                nc.gpsimd.memset(tick[:], 0.0).then_inc(tick_ready, 1)
                with nc.gpsimd.Fori(0, NG // 2) as i:
                    for q in range(2 * G):
                        pool.wait_ge(tick_ready, i * 2 * G + q + 1)
                        pool.wait_ge(x_ready, i * 2 * G + q + 1)
                        nc.gpsimd.tensor_tensor(tick[:, 1:2], tick[:, 0:1], tick[:, 0:1], ALU.mult)\
                            .then_inc(tick_ready, 1)
                        for k in range(TOPK1):
                            nc.gpsimd.indirect_dma_start(
                                x_slots[:], bass.IndirectOffsetOnAxis(ap=at[q][:, k:k + 1], axis=0),
                                x[q][:], None).then_inc(sent[q], 16)
                for q in range(2 * G):
                    pool.wait_ge(sent[q], 16 * TOPK1 * (NG // 2))

            @block.scalar
            def _(act):
                with nc.scalar.Fori(0, NG) as g:
                    act.wait_ge(xT_ps, g + 1)
                    nc.scalar.activation(xT[:], pt[:], ACT.Copy).then_inc(xT_ready, 1)
                    act.wait_ge(up_done, g + 1)
                    nc.scalar.activation(gate[:], p1[:], ACT.Sigmoid).then_inc(gate_ready, 1)

            @block.tensor
            def _(pe):
                def group(g, r, first=False):
                    for j in range(G):
                        pe.wait_ge(x_ready, g * G + j + 1)
                        last = nc.tensor.transpose(pt[:, j * P:(j + 1) * P], x[r * G + j][:], ident[:])
                    last.then_inc(xT_ps, 1)
                    pe.wait_ge(xT_ready, g + 1)
                    nc.tensor.matmul(p1[:], sw1_sb[:], xT[:], start=True, stop=True)
                    nc.tensor.matmul(p3[:], sw3_sb[:], xT[:], start=True, stop=True).then_inc(up_done, 1)
                    pe.wait_ge(act_ready, g + 1)
                    if not first:
                        pe.wait_ge(h_ready, g)
                    for j in range(G):
                        last = nc.tensor.matmul(py[:, j * P:(j + 1) * P], act1[:, j * P:(j + 1) * P], sw2_sb[:],
                                                start=True, stop=True)
                    last.then_inc(y_done, 1)

                pe.wait_ge(w_in, 48)
                group(0, 0, first=True)
                group(1, 1)
                with nc.tensor.Fori(1, NG // 2) as i:
                    group(2 * i, 0)
                    group(2 * i + 1, 1)


def experts_top2(nc, K, x_slots, y_slots, w13, w2):
    ident = K["ident"]
    RT = CAP // P
    with Bench(nc, "exp1") as m:
        x = [m.sb(f"x{j}", [P, RT, D]) for j in range(G)]
        wu = [m.sb(f"wu{j}", [P, 2 * HID1]) for j in range(G)]
        wd = [m.sb(f"wd{j}", [HID1, D]) for j in range(G)]
        xT = [m.sb(f"xT{j}", [P, CAP]) for j in range(G)]
        gate = [m.sb(f"gate{j}", [HID1, CAP]) for j in range(G)]
        half = [m.sb(f"half{j}", [HID1, CAP]) for j in range(G)]
        hid = [m.sb(f"hid{j}", [HID1, CAP]) for j in range(G)]
        y = [m.sb(f"y{j}", [P, RT, D]) for j in range(G)]
        pa = [m.ps(f"pa{j}", [P, 512]) for j in range(G)]
        pb = [m.ps(f"pb{j}", [P, 2, CAP]) for j in range(G)]
        x_in = [m.sem(f"x_in{j}") for j in range(G)]
        y_out = [m.sem(f"y_out{j}") for j in range(G)]
        xT_ps, xT_ready, up_done, gate_ready, half_ready, hid_ready, y_done, y_ready = (
            m.sem(n) for n in "xT_ps xT_ready up_done gate_ready half_ready hid_ready y_done y_ready".split())
        N = E1N // G
        with nc.Block() as block:
            @block.sync
            def _(sp):
                def load(ex, j):
                    sp.dma_start(x[j][:], x_slots[bass.ds(ex * CAP, CAP), :].rearrange("(t p) d -> p t d", p=P))\
                        .then_inc(x_in[j], 16)
                    sp.dma_start(wu[j][:], w13[bass.ds(ex * D, D), :]).then_inc(x_in[j], 16)
                    sp.dma_start(wd[j][:], w2[bass.ds(ex * HID1, HID1), :]).then_inc(x_in[j], 16)

                def store(i):
                    for j in range(G):
                        sp.wait_ge(y_ready, i * G + j + 1)
                        sp.dma_start(y_slots[bass.ds((i * G + j) * CAP, CAP), :].rearrange("(t p) d -> p t d", p=P),
                                     y[j][:]).then_inc(y_out[j], 16)

                for j in range(G):
                    load(j, j)
                with nc.sync.Fori(0, N - 1) as i:
                    for j in range(G):
                        sp.wait_ge(y_ready, i * G + j + 1)
                        load((i + 1) * G + j, j)
                    store(i)
                store(N - 1)
                for j in range(G):
                    sp.wait_ge(y_out[j], 16 * N)

            @block.vector
            def _(dve):
                def pass_(i, first=False):
                    for j in range(G):
                        n = i * G + j
                        dve.wait_ge(gate_ready, n + 1)
                        nc.vector.tensor_tensor(half[j][:], gate[j][:], pb[j][0:HID1, 0, :], ALU.mult)\
                            .then_inc(half_ready, 1)
                        dve.wait_ge(half_ready, n + 1)
                        nc.vector.tensor_tensor(hid[j][:], half[j][:], pb[j][0:HID1, 1, :], ALU.mult)\
                            .then_inc(hid_ready, 1)
                    for j in range(G):
                        dve.wait_ge(y_done, i * G + j + 1)
                        if not first:
                            dve.wait_ge(y_out[j], 16 * i)
                        nc.vector.tensor_copy(y[j][:], pa[j][:, CAP:2 * CAP].rearrange("p (t d) -> p t d", d=D))\
                            .then_inc(y_ready, 1)

                pass_(0, first=True)
                with nc.vector.Fori(1, N) as i:
                    pass_(i)

            @block.scalar
            def _(act):
                with nc.scalar.Fori(0, N) as i:
                    for j in range(G):
                        act.wait_ge(xT_ps, i * G + j + 1)
                        nc.scalar.activation(xT[j][:], pa[j][:, 0:CAP], ACT.Copy).then_inc(xT_ready, 1)
                    for j in range(G):
                        act.wait_ge(up_done, i * G + j + 1)
                        nc.scalar.activation(gate[j][:], pb[j][0:HID1, 0, :], ACT.Sigmoid).then_inc(gate_ready, 1)

            @block.tensor
            def _(pe):
                with nc.tensor.Fori(0, N) as i:
                    for j in range(G):
                        pe.wait_ge(x_in[j], 48 * (i + 1))
                        for t in range(RT):
                            last = nc.tensor.transpose(pa[j][:, t * P:(t + 1) * P], x[j][:, t, :], ident[:])
                        last.then_inc(xT_ps, 1)
                    for j in range(G):
                        pe.wait_ge(xT_ready, i * G + j + 1)
                        for n in range(2):
                            last = nc.tensor.matmul(pb[j][0:HID1, n, :], wu[j][:, n * HID1:(n + 1) * HID1], xT[j][:],
                                                    start=True, stop=True)
                        last.then_inc(up_done, 1)
                    for j in range(G):
                        pe.wait_ge(hid_ready, i * G + j + 1)
                        for t in range(RT):
                            last = nc.tensor.matmul(pa[j][:, CAP + t * P:CAP + (t + 1) * P],
                                                    hid[j][:, t * P:(t + 1) * P], wd[j][:], start=True, stop=True)
                        last.then_inc(y_done, 1)


def load_constants(nc, K, tables, in_bf16, x_slots, results, zeros, cleared):
    with Bench(nc, "const") as m:
        const_in, zeroed = m.sem("const_in"), m.sem("zeroed")
        wide = {n: m.sb(f"wide_{n}", list(K[n].shape)) for n in in_bf16}
        with nc.Block() as block:
            @block.sync
            def _(sp):
                for name in K:
                    sp.dma_start((wide.get(name) or K[name])[:], tables[name]).then_inc(const_in, 16)
                sp.wait_ge(zeroed, 1)
                clear_slots(x_slots, results, zeros, cleared, sp)
                sp.wait_ge(const_in, 16 * len(K))

            @block.vector
            def _(dve):
                nc.vector.memset(zeros[:], 0.0).then_inc(zeroed, 1)
                dve.wait_ge(const_in, 16 * len(K))
                for name in in_bf16:
                    nc.vector.tensor_copy(K[name][:], wide[name][:])


def await_cleared(nc, cleared):
    with nc.Block() as block:
        @block.sync
        def _(sp):
            sp.wait_ge(cleared, 16 * CLEARS)


def store_output(nc, h, out):
    with Bench(nc, "store") as m:
        stored = m.sem("stored")
        with nc.Block() as block:
            @block.sync
            def _(sp):
                for s in range(2):
                    sp.dma_start(out[:, s * P:s * P + ROWS[s], :].rearrange("b p d -> p b d"),
                                 h[0:ROWS[s]].rearrange("p (b s) d -> p b s d", s=2)[:, :, s, :])\
                        .then_inc(stored, 16)
                sp.wait_ge(stored, 32)


def shape_tables():
    f = np.float32
    p, col = np.arange(P)[:, None], np.arange(T)[None, :]
    after = (col > p).astype(f)
    real = np.ones((P, NT), f)
    real[ROWS[1]:, 1::2] = 0
    tile, k = np.arange(NT)[None, :], np.arange(TOPK1)[None, :, None]
    head, query = p // HALF % H, p % HALF
    spill = SLOTS + k * (NT * P) + np.arange(NT)[None, None, :] * P + p[:, :, None]
    inc = {
        "after": after,
        "upto": (col >= p).astype(f),
        "ident": np.eye(P, dtype=f),
        "inv03": np.full((P, 1), 1.0 / 0.3, f),
        "after_b": after[:, :P],
        "ones_b": np.ones((P, P), f),
        "real": real,
        "pad_to": (1 - real) * (SLOTS + tile),
        "pad_from": (1 - real) * SLOTS0,
        "spill": spill.reshape(P, TOPK1 * NT),
        "rank0": np.tile(np.arange(E0, 0, -1), (P, 1)),
        "rank1": np.tile(np.arange(E1N, 0, -1), (P, 1)),
        "multiples": np.tile(P * np.arange(NT), (P, 1)),
        "tile_no": np.tile(np.arange(ST0), (P, 1)),
        "mask16": p // HD == np.arange(H),
        "mask_pv": np.concatenate([head == np.arange(D) // HD, query == np.arange(D) // HD], 1),
    }
    return {n: np.ascontiguousarray(a, dtype=f) for n, a in inc.items()}


def layouts(a):
    W, NLOW = a["L0_tok_W"], C + C * C + C ** 3

    def level(lo, hi):
        return W[:, lo:hi].reshape(D, (hi - lo) // C, C).transpose(1, 2, 0).reshape(-1, C * D)

    query = np.arange(HALF)[:, None, None]
    key_at = np.clip(np.arange(KWIN) - (REACH + HALF) - query, -MAX_REL, MAX_REL) + MAX_REL
    value_at = np.clip(np.arange(P)[:, None] - (np.arange(VWIN)[None, :] - P), -MAX_REL, MAX_REL) + MAX_REL
    rel_k, rel_v = a["L1_attn_rel_k"], a["L1_attn_rel_v"]
    far_keys = np.zeros((P, FARWIN), np.float32)
    far_keys[:, :T - BQ - REACH] = np.tile(rel_k[0], H)[:, None]
    far_keys[:, T + REACH:] = np.tile(rel_k[2 * MAX_REL], H)[:, None]
    row, col = np.arange(P)[:, None, None], np.arange(P)[None, None, :]
    repeat_head = ((row // HD == np.arange(H)[None, :, None]) & (row % HD == col % HD)).astype(np.float32)
    w1, b1, w2 = a["L0_ffn_W1"], a["L0_ffn_b1"], a["L0_ffn_W2"]
    lay = {
        "x_t": a["x"].transpose(1, 0, 2).reshape(T, B * CIN),
        "w_main": level(NLOW, W.shape[1]),
        "w_low": np.concatenate([level(C + C * C, NLOW), level(C, C + C * C), level(0, C)]),
        "tok_b": a["L0_tok_b"],
        "fuz_wq": a["L0_attn_Wq"].T, "fuz_bq": a["L0_attn_bq"][:, None],
        "fuz_wk": a["L0_attn_Wk"].T, "fuz_bk": a["L0_attn_bk"][:, None],
        "gate0": a["L0_ffn_Wr"], "gate0_b": a["L0_ffn_br"],
        "exp0_w1": np.concatenate([w1.transpose(1, 0, 2), b1.reshape(E0, HID0 // P, P).transpose(2, 0, 1)], 2),
        "exp0_w2": w2.reshape(E0, HID0 // P, P, D).transpose(2, 0, 1, 3).reshape(P, E0, -1),
        "exp0_b2": a["L0_ffn_b2"].reshape(-1),
        "rel_wq": a["L1_attn_Wq"], "rel_bq": a["L1_attn_bq"][:, None],
        "rel_wk": a["L1_attn_Wk"], "rel_bk": a["L1_attn_bk"][:, None],
        "rel_wv": a["L1_attn_Wv"], "rel_bv": a["L1_attn_bv"],
        "rel_wo": a["L1_attn_Wo"], "rel_bo": a["L1_attn_bo"],
        "rel_rep": repeat_head,
        "rel_far": far_keys,
        "rel_vends": np.stack([np.tile(rel_v[0], H), np.tile(rel_v[2 * MAX_REL], H)]),
        "rel_ktab": rel_k[key_at, np.arange(HD)[None, :, None]].reshape(P, KWIN),
        "rel_vtab": rel_v[value_at],
        "gate1": a["L1_ffn_gate_w"].T,
        "sw1": a["L1_ffn_sw1"], "sw3": a["L1_ffn_sw3"], "sw2": a["L1_ffn_sw2"],
        "exp1_w13": np.concatenate([a["L1_ffn_w1"], a["L1_ffn_w3"]], 2).reshape(E1N * D, 2 * HID1),
        "exp1_w2": a["L1_ffn_w2"].reshape(E1N * HID1, D),
    }
    t = np.diff(np.linspace(0.0, 1.0, T, dtype=np.float32))
    lay["step_time"] = np.stack([t[:P], np.concatenate([t[P:], np.zeros(P - ROWS[1], np.float32)])], 1)
    return {n: np.ascontiguousarray(v) for n, v in lay.items()}


def moe0(nc, K, h, mean, rstd, stats, x_slots, y0_slots, w):
    with Bench(nc, "moe0") as q:
        logits = q.sb("logits", [P, NT, E0])
        to, back = q.sb("to", [P, 1, NT], U32), q.sb("back", [P, 1, NT], U32)
        tile_expert = q.sb("tile_expert", [P, ST0], U32)
        router_logits(nc, K, h, mean, rstd, logits, w["gate0"], w["gate0_b"], E0, "logits0")
        route_top1(nc, K, logits, to, back, tile_expert)
        scatter_rows(nc, h, mean, rstd, x_slots, to, 1, "scatter0")
        experts_top1(nc, K, x_slots, y0_slots, tile_expert, w["exp0_w1"], w["exp0_w2"], w["exp0_b2"])
        gather_rows(nc, h, stats, y0_slots, back, None, 1, "gather0")


def moe1(nc, K, h, mean, rstd, x_slots, y1_slots, w):
    with Bench(nc, "moe1") as q:
        to, back = q.sb("to", [P, TOPK1, NT], U32), q.sb("back", [P, TOPK1, NT], U32)
        weight = q.sb("weight", [P, TOPK1, NT])
        with Bench(nc, "choice") as c:
            logits = c.sb("logits", [P, NT, E1N])
            router_logits(nc, K, h, mean, rstd, logits, w["gate1"], None, E1N, "logits1")
            route_top2(nc, K, logits, to, back, weight)
        scatter_and_share(nc, K, h, mean, rstd, x_slots, to, w["sw1"], w["sw3"], w["sw2"])
        experts_top2(nc, K, x_slots, y1_slots, w["exp1_w13"], w["exp1_w2"])
        gather_rows(nc, h, None, y1_slots, back, [weight[:, 0], weight[:, 1]], TOPK1, "gather1")


def build(nc, t, w, out):
    in_bf16 = ("after_b", "ones_b")
    x_slots = nc.dram_tensor("x_slots", (SLOTS + TOPK1 * NT * P, D), FP32, kind="Internal").ap()
    y0_slots = nc.dram_tensor("y0_slots", (SLOTS0 + 1, D), FP32, kind="Internal").ap()
    y1_slots = nc.dram_tensor("y1_slots", (SLOTS1 + 1, D), FP32, kind="Internal").ap()
    o_rows = [nc.dram_tensor(f"o_rows{r}", (2, P, P), FP32, kind="Internal").ap() for r in range(2)]
    with Bench(nc, "all") as m:
        h = m.sb("h", [P, NT, D])
        stats, mean, rstd = m.sb("stats", [P, NT, 6]), m.sb("mean", [P, NT]), m.sb("rstd", [P, NT])
        cleared = m.sem("cleared")
        K = {n: m.sb(f"k_{n}", list(a.shape), BF16 if n in in_bf16 else FP32) for n, a in t.items()}
        with Bench(nc, "early") as early:
            zeros = early.sb("zeros", [P, 4 * D])
            load_constants(nc, K, t, in_bf16, x_slots, [(y0_slots, SLOTS0), (y1_slots, SLOTS1)], zeros, cleared)
            signature_tokens(nc, K, h, stats, w["x_t"], w["step_time"], w["w_main"], w["w_low"], w["tok_b"])
            norm_factors(nc, stats, mean, rstd, "norm0")
            fuzzy_attention(nc, K, h, mean, rstd, stats, w["fuz_wq"], w["fuz_bq"], w["fuz_wk"], w["fuz_bk"])
            norm_factors(nc, stats, mean, rstd, "norm1")
            await_cleared(nc, cleared)
        moe0(nc, K, h, mean, rstd, stats, x_slots, y0_slots, w)
        norm_factors(nc, stats, mean, rstd, "norm2")
        relative_attention(nc, K, h, mean, rstd, stats, o_rows, *(w[f"rel_{n}"] for n in (
            "wq bq wk bk wv bv wo bo rep far vends ktab vtab").split()))
        norm_factors(nc, stats, mean, rstd, "norm3")
        moe1(nc, K, h, mean, rstd, x_slots, y1_slots, w)
        store_output(nc, h, out)


def kernel(**inputs):
    import numpy as _np
    import concourse.bacc as _bacc
    from concourse.bass_utils import run_bass_kernel_spmd as _run

    nc = _bacc.Bacc("TRN2", target_bir_lowering=False, num_devices=1)
    arrays = {}

    def dram(name, a):
        arrays[name] = a
        return nc.dram_tensor(name, a.shape, mybir.dt.from_np(a.dtype), kind="ExternalInput").ap()

    tables = {n: dram(f"table_{n}", a) for n, a in shape_tables().items()}
    laid = {n: dram(f"in_{n}", a) for n, a in layouts({k: _np.asarray(v) for k, v in inputs.items()}).items()}
    out = nc.dram_tensor("out_dram", (B, L, D), FP32, kind="ExternalOutput").ap()
    build(nc, tables, laid, out)
    r = _run(nc, [arrays], core_ids=[0])
    return r.results[0]["out_dram"]
```

```python
import concourse.bass as bass
from concourse import mybir
from contextlib import ExitStack
import numpy as np

FP32 = mybir.dt.float32
FP32R = mybir.dt.float32r
BF16 = mybir.dt.bfloat16
U32 = mybir.dt.uint32
ALU = mybir.AluOpType
ACT = mybir.ActivationFunctionType
AX = mybir.AxisListType

P = 128
B, T, CIN, D = 32, 256, 7, 128
L = T - 1
ROWS = (P, L - P)
C = CIN + 1
NT = 2 * B
EPS = 1e-5
G = 4


class Bench:

    def __init__(self, nc, stage):
        self.nc, self.stage, self.stack, self.sems = nc, stage, ExitStack(), []

    def __enter__(self):
        self.stack.__enter__()
        return self

    def __exit__(self, *e):
        if self.sems:
            self.nc.clear_and_free_semaphores(self.sems)
            self.nc.all_engine_barrier()
        return self.stack.__exit__(*e)

    def sb(self, name, shape, dt=FP32):
        return self.stack.enter_context(self.nc.sbuf_tensor(f"{self.stage}_{name}", shape, dt))

    def ps(self, name, shape, dt=FP32):
        return self.stack.enter_context(self.nc.psum_tensor(f"{self.stage}_{name}", shape, dt))

    def sem(self, name):
        self.sems.append(self.nc.alloc_semaphore(f"{self.stage}_{name}"))
        return self.sems[-1]


class Ahead:

    def __init__(self, bench, tensors):
        self.loaded, self.tensors = bench.sem("loaded"), tensors
        self.sb = {name: bench.sb(name, shape) for name, (shape, _) in tensors.items()}

    def start(self, nc):
        with nc.Block() as block:
            @block.sync
            def _(sp):
                for name, (_, src) in self.tensors.items():
                    sp.dma_start(self.sb[name][:], src).then_inc(self.loaded, 16)

    def wait(self, eng):
        eng.wait_ge(self.loaded, 16 * len(self.tensors))


class Chain:

    def __init__(self, eng, sem, base=0):
        self.eng, self.sem, self.n = eng, sem, base

    def __call__(self, instruction):
        instruction.then_inc(self.sem, 1)
        self.n = self.n + 1
        self.eng.wait_ge(self.sem, self.n)


def outer(nc_eng, out, left, right, n, a, c):
    return nc_eng.tensor_tensor(
        out,
        left.unsqueeze(3).to_broadcast([P, n, a, c]),
        right.unsqueeze(2).to_broadcast([P, n, a, c]),
        ALU.mult)


THREE = ((0, 0), (0, 1), (1, 0))


def rest(engine, out, value, rounded):
    return engine.tensor_tensor(out, value, rounded.bitcast(FP32), ALU.subtract)


class Steps:

    def __init__(self, n, unroll):
        self.passes, self.unroll = n // unroll, unroll

    def run(self, engine, step, ahead):
        for n in range(-ahead, self.unroll):
            step(n // self.unroll, n % self.unroll)
        with engine.Fori(1, self.passes - 1) as i:
            for j in range(self.unroll):
                step(i, j)
        for j in range(self.unroll):
            step(self.passes - 1, j)

    def later(self, i, j, k):
        i, j = i + (j + k) // self.unroll, (j + k) % self.unroll
        return None if isinstance(i, int) and not 0 <= i < self.passes else (i, j)

    def old(self, i, j, k):
        return not isinstance(i, int) or self.unroll * i + j >= k


def signature_tokens(nc, K, h, stats, x_t, step_time, w_main, w_low, tok_b):
    NA = C ** 3 // P
    LOW = C ** 2 + C + 1
    after, upto, ident = K["after"], K["upto"], K["ident"]
    with Bench(nc, "tok") as m:
        x0 = m.sb("x0", [P, 2, B * CIN])
        x1 = m.sb("x1", [P, 2, B * CIN])
        dt_sb = m.sb("dt", [P, 2])
        v = m.sb("v", [P, B, 2, C])
        v_r, v_q = m.sb("v_r", [P, B, 2, C]), m.sb("v_q", [P, B, 2, C])
        g1 = m.sb("g1", [P, B, 2, C])
        g1v = m.sb("g1v", [P, NT, C, C])
        r2_pre = m.sb("r2_pre", [P, NT, C, C])
        q2_pre = m.sb("q2_pre", [P, NT, C, C])
        low = m.sb("low", [P, 2, LOW])
        q2 = m.sb("q2", [P, 2, C * C])
        r2v = m.sb("r2v", [P, 2, C ** 3])
        q2v = m.sb("q2v", [P, 2, C ** 3])
        r2v_p = [m.sb(f"r2v_{k}", [P, 2, C ** 3], FP32R) for k in "hl"]
        q2v_p = [m.sb(f"q2v_{k}", [P, 2, C ** 3], FP32R) for k in "hl"]
        feat = [m.sb(f"feat_{k}", [P, 2, NA + 1, P], FP32R) for k in "hl"]
        w = m.sb("w", [P, NA + 1, C * D])
        w_p = [m.sb(f"w_{k}", [P, NA + 1, C * D], FP32R) for k in "hl"]
        after_r, ident_r = m.sb("after_r", [P, T], FP32R), m.sb("ident_r", [P, P], FP32R)
        bias = m.sb("bias", [P, D])
        prod = m.sb("prod", [P, 2, C, D])
        inc = m.sb("inc", [P, 2, D])
        a3_ps = m.ps("a3_ps", [P, NA, 2, P])
        low_ps = m.ps("low_ps", [P, 512])
        small_ps = m.ps("small_ps", [P, 512])
        main_ps = [m.ps(f"main_ps{s}", [P, C * D]) for s in range(2)]
        e1_ps = main_ps[0]
        lowT_ps = low_ps[:, 0:2 * P]
        h_ps = small_ps[:, 0:2 * D].rearrange("p (s d) -> p s d", s=2)
        e2_ps = small_ps[:, 2 * D:2 * D + 2 * C * C]

        x_in, w_in, zeroed = m.sem("x_in"), m.sem("w_in"), m.sem("zeroed")
        vec, v_ready, e1_ready = m.sem("vec"), m.sem("v_ready"), m.sem("e1_ready")
        pre_ready, vq_ready, q2_pre_ready = m.sem("pre_ready"), m.sem("vq_ready"), m.sem("q2_pre_ready")
        e2_ready, low_ready, q2_ready = m.sem("e2_ready"), m.sem("low_ready"), m.sem("q2_ready")
        r2v_ready, q2v_ready = m.sem("r2v_ready"), m.sem("q2v_ready")
        r2v_round, r2v_rest = m.sem("r2v_round"), m.sem("r2v_rest")
        q2v_round, q2v_rest = m.sem("q2v_round"), m.sem("q2v_rest")
        w_round, w_rest = m.sem("w_round"), m.sem("w_rest")
        a3_ready, feat_round, feat_rest = m.sem("a3_ready"), m.sem("feat_round"), m.sem("feat_rest")
        main_ready, prod_ready, inc_ready = m.sem("main_ready"), m.sem("prod_ready"), m.sem("inc_ready")
        h_ready, h_done = m.sem("h_ready"), m.sem("h_done")

        with nc.Block() as block:

            @block.sync
            def _(sp):
                sp.dma_start(x0[:, 0, :], x_t[0:P, :]).then_inc(x_in, 16)
                sp.dma_start(x1[:, 0, :], x_t[1:P + 1, :]).then_inc(x_in, 16)
                sp.dma_start(x0[0:ROWS[1], 1, :], x_t[P:L, :]).then_inc(x_in, 16)
                sp.dma_start(x1[0:ROWS[1], 1, :], x_t[P + 1:T, :]).then_inc(x_in, 16)
                sp.dma_start(dt_sb[:], step_time).then_inc(x_in, 16)
                for j in range(NA):
                    sp.dma_start(w[:, j, :], w_main[j * P:(j + 1) * P, :]).then_inc(w_in, 16)
                sp.dma_start(w[0:LOW, NA, :], w_low).then_inc(w_in, 16)
                sp.dma_start(bias[:], tok_b.partition_broadcast(P)).then_inc(w_in, 16)
                sp.wait_ge(w_in, 16 * (NA + 2))

            def tile_view(t):
                return t[:].rearrange("p b s c -> p (b s) c")

            @block.vector
            def _(dve):
                link = Chain(dve, vec)
                link(nc.vector.memset(v[:], 0.0))
                nc.vector.tensor_copy(after_r[:], after[:])
                nc.vector.tensor_copy(ident_r[:], ident[:])
                nc.vector.memset(low[:, :, LOW - 1:LOW], 1.0)
                dve.wait_ge(x_in, 16 * 5)
                for s in range(2):
                    n = ROWS[s]
                    nc.vector.tensor_tensor(
                        v[0:n, :, s, 1:C],
                        x1[0:n, s, :].rearrange("p (b c) -> p b c", c=CIN),
                        x0[0:n, s, :].rearrange("p (b c) -> p b c", c=CIN), ALU.subtract)
                    link(nc.vector.tensor_copy(v[:, :, s, 0:1],
                                               dt_sb[:, s:s + 1].unsqueeze(1).to_broadcast([P, B, 1])))
                nc.vector.memset(q2[:], 0.0).then_inc(v_ready, 1)
                e1 = e1_ps[:, 0:NT * C].rearrange("p (b s c) -> p b s c", b=B, s=2)
                dve.wait_ge(e1_ready, 1)
                link(nc.vector.scalar_tensor_tensor(g1[:], v[:], 0.5, e1, ALU.mult, ALU.add))
                for div, scale, v_s in ((4.0, 1.0 / 6.0, v_q), (3.0, 0.5, v_r)):
                    link(nc.vector.scalar_tensor_tensor(v_s[:], v[:], 1.0 / div, e1, ALU.mult, ALU.add))
                    last = nc.vector.tensor_scalar(v_s[:], v_s[:], scale, None, ALU.mult)
                    if v_s is v_q:
                        last.then_inc(vq_ready, 1)
                    else:
                        link(last)
                link(outer(nc.vector, g1v[:], tile_view(g1), tile_view(v), NT, C, C))
                link(outer(nc.vector, r2_pre[:], tile_view(v_r), tile_view(v), NT, C, C))
                nc.vector.memset(inc[:], 0.0).then_inc(pre_ready, 1)

                vt, g1t = tile_view(v), tile_view(g1)

                def features(b, first=False):
                    dve.wait_ge(e2_ready, b + 1)
                    e2 = e2_ps.rearrange("p (s k) -> p s k", s=2)
                    flat = "p n a c -> p n (a c)"
                    nc.vector.tensor_tensor(low[:, :, 0:C * C], e2,
                                            r2_pre[:, bass.ds(2 * b, 2)].rearrange(flat), ALU.add)
                    nc.vector.tensor_copy(low[:, :, C * C:C * C + C], g1t[:, bass.ds(2 * b, 2), :])\
                        .then_inc(low_ready, 1)
                    if not first:
                        dve.wait_ge(q2v_ready, b)
                    nc.vector.scalar_tensor_tensor(q2[:], e2, 0.5, q2_pre[:, bass.ds(2 * b, 2)].rearrange(flat),
                                                   ALU.mult, ALU.add).then_inc(q2_ready, 1)
                    dve.wait_ge(low_ready, b + 1)
                    outer(nc.vector, r2v[:].rearrange("p n (a c) -> p n a c", c=C), low[:, :, 0:C * C],
                          vt[:, bass.ds(2 * b, 2), :], 2, C * C, C).then_inc(r2v_ready, 1)

                def combine(b, s, first=False):
                    dve.wait_ge(main_ready, 2 * b + s + 1)
                    if not first:
                        dve.wait_ge(inc_ready, 2 * b + s - 1)
                    nc.vector.tensor_tensor(
                        prod[:, s], main_ps[s][:].rearrange("p (c o) -> p c o", c=C),
                        vt[:, bass.ds(2 * b + s, 1), :].rearrange("p n c -> p (n c)").unsqueeze(2)
                        .to_broadcast([P, C, D]), ALU.mult).then_inc(prod_ready, 1)
                    dve.wait_ge(prod_ready, 2 * b + s + 1)
                    if s == 0 and not first:
                        dve.wait_ge(h_ready, b)
                    nc.vector.tensor_reduce(inc[:, s, :], prod[:, s].rearrange("p c o -> p o c"),
                                            AX.X, ALU.add).then_inc(inc_ready, 1)

                def finish(b):
                    dve.wait_ge(h_ready, b + 1)
                    nc.vector.tensor_tensor(h[:, bass.ds(2 * b, 2), :], h_ps,
                                            bias[:].unsqueeze(1).to_broadcast([P, 2, D]),
                                            ALU.add).then_inc(h_done, 1)
                    dve.wait_ge(h_done, b + 1)
                    for s in range(2):
                        nc.vector.bn_stats(stats[:, bass.ds(2 * b + s, 1), :].rearrange("p n k -> p (n k)"),
                                           h[:, bass.ds(2 * b + s, 1), :].rearrange("p n k -> p (n k)"))

                def q2v_remainder(b):
                    dve.wait_ge(q2v_round, b + 1)
                    rest(nc.vector, q2v_p[1][:], q2v[:], q2v_p[0][:]).then_inc(q2v_rest, 1)

                def feat_remainder(b, s):
                    dve.wait_ge(feat_round, 2 * b + s + 1)
                    rest(nc.vector, feat[1][:, s, 0:NA, :], a3_ps[:, :, s, :], feat[0][:, s, 0:NA, :])
                    rest(nc.vector, feat[1][0:LOW, s, NA, :], lowT_ps[0:LOW, s * P:(s + 1) * P],
                         feat[0][0:LOW, s, NA, :]).then_inc(feat_rest, 1)

                dve.wait_ge(w_in, 16 * (NA + 2))
                dve.wait_ge(w_round, 1)
                rest(nc.vector, w_p[1][:, 0:NA, :], w[:, 0:NA, :], w_p[0][:, 0:NA, :])
                rest(nc.vector, w_p[1][0:LOW, NA, :], w[0:LOW, NA, :], w_p[0][0:LOW, NA, :]).then_inc(w_rest, 1)
                dve.wait_ge(q2_pre_ready, 1)
                features(0, first=True)
                q2v_remainder(0)
                feat_remainder(0, 0)
                feat_remainder(0, 1)
                features(1)
                q2v_remainder(1)
                combine(0, 0, first=True)
                feat_remainder(1, 0)
                features(2)
                combine(0, 1, first=True)
                feat_remainder(1, 1)
                q2v_remainder(2)
                with nc.vector.Fori(1, B - 2) as b:
                    combine(b, 0)
                    finish(b - 1)
                    feat_remainder(b + 1, 0)
                    features(b + 2)
                    combine(b, 1)
                    feat_remainder(b + 1, 1)
                    q2v_remainder(b + 2)
                combine(B - 2, 0)
                finish(B - 3)
                feat_remainder(B - 1, 0)
                combine(B - 2, 1)
                feat_remainder(B - 1, 1)
                combine(B - 1, 0)
                finish(B - 2)
                combine(B - 1, 1)
                finish(B - 1)

            @block.gpsimd
            def _(pool):
                vt = tile_view(v)

                def outer_q2(b):
                    pool.wait_ge(q2_ready, b + 1)
                    outer(nc.gpsimd, q2v[:].rearrange("p n (a c) -> p n a c", c=C), q2[:],
                          vt[:, bass.ds(2 * b, 2), :], 2, C * C, C).then_inc(q2v_ready, 1)

                def r2v_remainder(b):
                    pool.wait_ge(r2v_round, b + 1)
                    rest(nc.gpsimd, r2v_p[1][:], r2v[:], r2v_p[0][:]).then_inc(r2v_rest, 1)

                pool.wait_ge(vq_ready, 1)
                outer(nc.gpsimd, q2_pre[:], tile_view(v_q), vt, NT, C, C).then_inc(q2_pre_ready, 1)
                outer_q2(0)
                r2v_remainder(0)
                with nc.gpsimd.Fori(1, B) as b:
                    pool.wait_ge(e2_ready, b + 1)
                    outer_q2(b)
                    r2v_remainder(b)

            @block.scalar
            def _(act):
                def rounded(b):
                    act.wait_ge(r2v_ready, b + 1)
                    nc.scalar.activation(r2v_p[0][:], r2v[:], ACT.Copy).then_inc(r2v_round, 1)
                    act.wait_ge(q2v_ready, b + 1)
                    nc.scalar.activation(q2v_p[0][:], q2v[:], ACT.Copy).then_inc(q2v_round, 1)

                def evacuate(b, s, first=False):
                    act.wait_ge(a3_ready, b + 1)
                    if not first:
                        act.wait_ge(main_ready, 2 * b - 1 + s)
                        act.wait_ge(feat_rest, 2 * b + s)
                    nc.scalar.activation(feat[0][:, s, 0:NA, :], a3_ps[:, :, s, :], ACT.Copy)
                    nc.scalar.activation(feat[0][0:LOW, s, NA, :], lowT_ps[0:LOW, s * P:(s + 1) * P],
                                         ACT.Copy).then_inc(feat_round, 1)

                act.wait_ge(w_in, 16 * (NA + 2))
                nc.scalar.activation(w_p[0][:, 0:NA, :], w[:, 0:NA, :], ACT.Copy)
                nc.scalar.activation(w_p[0][0:LOW, NA, :], w[0:LOW, NA, :], ACT.Copy).then_inc(w_round, 1)
                rounded(0)
                evacuate(0, 0, first=True)
                act.wait_ge(feat_rest, 1)
                evacuate(0, 1, first=True)
                rounded(1)
                with nc.scalar.Fori(1, B - 1) as b:
                    evacuate(b, 0)
                    rounded(b + 1)
                    evacuate(b, 1)
                evacuate(B - 1, 0)
                evacuate(B - 1, 1)

            @block.tensor
            def _(pe):
                def level2(b, first=False):
                    if not first:
                        pe.wait_ge(h_done, b - 2)
                    gv = g1v[:].rearrange("p n a c -> p n (a c)")
                    nc.tensor.matmul(e2_ps[:, 0:64], after[:, 0:P], gv[:, bass.ds(2 * b, 1), :],
                                     start=True, stop=True)
                    nc.tensor.matmul(e2_ps[:, 64:128], after[:, P:T], gv[:, bass.ds(2 * b, 1), :],
                                     start=True, stop=False)
                    nc.tensor.matmul(e2_ps[:, 64:128], after[:, 0:P], gv[:, bass.ds(2 * b + 1, 1), :],
                                     start=False, stop=True).then_inc(e2_ready, 1)

                def level3(b, first=False):
                    pe.wait_ge(low_ready, b + 1)
                    if not first:
                        pe.wait_ge(feat_rest, 2 * b)
                    for s in range(2):
                        nc.tensor.transpose(lowT_ps[0:LOW, s * P:(s + 1) * P], low[:, s, :], ident[:])
                    pe.wait_ge(q2v_rest, b + 1)
                    pe.wait_ge(r2v_rest, b + 1)
                    for j in range(NA):
                        cols = slice(j * P, (j + 1) * P)
                        for k in range(2):
                            for s in range(2):
                                nc.tensor.matmul(a3_ps[:, j, s, :], q2v_p[k][:, s, cols], ident_r[:],
                                                 start=(k == 0 and s == 0), stop=False, skip_group_check=True)
                            nc.tensor.matmul(a3_ps[:, j, 1, :], r2v_p[k][:, 1, cols], after_r[:, 0:P],
                                             start=False, stop=False, skip_group_check=True)
                            last = nc.tensor.matmul(a3_ps[:, j], r2v_p[k][:, 0, cols], after_r[:],
                                                    start=False, stop=(k == 1), skip_group_check=True)
                    last.then_inc(a3_ready, 1)

                def main(b, s, first=False):
                    pe.wait_ge(feat_rest, 2 * b + s + 1)
                    if not first:
                        pe.wait_ge(prod_ready, 2 * b + s - 1)
                    for half in range(2):
                        cols = slice(half * 512, (half + 1) * 512)
                        for j in range(NA + 1):
                            n = P if j < NA else LOW
                            for fk, wk in THREE:
                                last = nc.tensor.matmul(main_ps[s][:, cols], feat[fk][0:n, s, j, :],
                                                        w_p[wk][0:n, j, cols],
                                                        start=(j == 0 and (fk, wk) == (0, 0)),
                                                        stop=(j == NA and (fk, wk) == (1, 0)))
                    last.then_inc(main_ready, 1)

                def running_sum(b, first=False, ahead=3):
                    pe.wait_ge(q2_ready, b + ahead)
                    pe.wait_ge(inc_ready, 2 * b + 2)
                    if not first:
                        pe.wait_ge(h_done, b)
                    nc.tensor.matmul(h_ps[:, 0, :], upto[:, 0:P], inc[:, 0, :], start=True, stop=True)
                    nc.tensor.matmul(h_ps[:, 1, :], upto[:, P:T], inc[:, 0, :], start=True, stop=False)
                    nc.tensor.matmul(h_ps[:, 1, :], upto[:, 0:P], inc[:, 1, :], start=False,
                                     stop=True).then_inc(h_ready, 1)

                pe.wait_ge(v_ready, 1)
                e1 = e1_ps[:, 0:NT * C].rearrange("p (b s c) -> p b s c", b=B, s=2)
                nc.tensor.matmul(e1[:, :, 0, :], after[:, 0:P], v[:, :, 0, :], start=True, stop=False,
                                 skip_group_check=True)
                nc.tensor.matmul(e1[:, :, 1, :], after[:, P:T], v[:, :, 0, :], start=False, stop=False,
                                 skip_group_check=True)
                nc.tensor.matmul(e1[:, :, 1, :], after[:, 0:P], v[:, :, 1, :], start=False,
                                 stop=True, skip_group_check=True).then_inc(e1_ready, 1)
                pe.wait_ge(pre_ready, 1)
                level2(0, first=True)
                level3(0, first=True)
                pe.wait_ge(w_rest, 1)
                level2(1, first=True)
                main(0, 0, first=True)
                level3(1)
                level2(2, first=True)
                main(0, 1, first=True)
                main(1, 0)
                running_sum(0, first=True)
                level3(2)
                level2(3)
                main(1, 1)
                with nc.tensor.Fori(2, B - 2) as b:
                    main(b, 0)
                    running_sum(b - 1)
                    level3(b + 1)
                    level2(b + 2)
                    main(b, 1)
                main(B - 2, 0)
                running_sum(B - 3)
                level3(B - 1)
                main(B - 2, 1)
                main(B - 1, 0)
                running_sum(B - 2, ahead=2)
                main(B - 1, 1)
                running_sum(B - 1, ahead=1)


def norm_factors(nc, stats, mean, rstd, stage):
    with Bench(nc, stage) as m:
        spread = m.sb("spread", [P, NT])
        var = m.sb("var", [P, NT])
        vec, var_ready, std_ready = m.sem("vec"), m.sem("var_ready"), m.sem("std_ready")
        mean_e, m2_e, mean_o, m2_o = (stats[:, :, k] for k in (1, 2, 4, 5))
        with nc.Block() as block:
            @block.vector
            def _(dve):
                link = Chain(dve, vec)
                link(nc.vector.tensor_tensor(mean[:], mean_e, mean_o, ALU.add))
                link(nc.vector.tensor_scalar(mean[:], mean[:], 0.5, None, ALU.mult))
                link(nc.vector.tensor_tensor(spread[:], mean_e, mean_o, ALU.subtract))
                link(nc.vector.scalar_tensor_tensor(spread[:], spread[:], 0.25, spread[:],
                                                    ALU.mult, ALU.mult))
                link(nc.vector.tensor_tensor(var[:], m2_e, m2_o, ALU.add))
                link(nc.vector.scalar_tensor_tensor(var[:], var[:], 1.0 / D, spread[:],
                                                    ALU.mult, ALU.add))
                nc.vector.tensor_scalar(var[:], var[:], EPS, None, ALU.add).then_inc(var_ready, 1)
                dve.wait_ge(std_ready, 1)
                nc.vector.reciprocal(rstd[:], var[:])

            @block.scalar
            def _(act):
                act.wait_ge(var_ready, 1)
                nc.scalar.activation(var[:], var[:], ACT.Sqrt).then_inc(std_ready, 1)


def one_tile(t, n):
    return t[:, bass.ds(n, 1), :].rearrange("p n k -> p (n k)")


def one_column(t, n):
    return t[:, bass.ds(n, 1)]


def normalise(nc, out, h, mean, rstd, n):
    return nc.vector.tensor_scalar(out, one_tile(h, n), one_column(mean, n), one_column(rstd, n),
                                   ALU.subtract, ALU.mult)


def normalise_act(nc, out, h, shift, rstd, n):
    return nc.scalar.activation(out, one_tile(h, n), ACT.Identity, bias=one_column(shift, n), scale=one_column(rstd, n))


def fuzzy_attention(nc, K, h, mean, rstd, stats, wq, bq, wk, bk, behind):
    ident = K["ident"]
    INV = 1.0 / 0.3
    U = 8
    steps = Steps(B, U)
    later, old = steps.later, steps.old
    with Bench(nc, "fuz") as m:
        def ring(name, shape, n=2):
            return [m.sb(f"{name}{j}", shape) for j in range(n)]

        wq_sb, wk_sb = m.sb("wq", [P, D]), m.sb("wk", [P, D])
        bq_sb, bk_sb = m.sb("bq", [P, 1]), m.sb("bk", [P, 1])
        x = ring("x", [P, 2, D], U)
        xT, qT, kT = (ring(n, [P, T]) for n in ("xT", "qT", "kT"))
        e, fall, f, fT = (ring(n, [P, 2, T]) for n in ("e", "fall", "f", "fT"))
        neg_max, total, inv, rise_by, fall_by = (ring(n, [P, 2]) for n in (
            "neg_max", "total", "inv", "rise_by", "fall_by"))
        turn_ps, qk_ps = m.ps("turn_ps", [P, 2, T]), m.ps("qk_ps", [P, 2, T])
        score_ps, fT_ps, out_ps = ([m.ps(f"{n}{j}", [P, 2, T]) for j in range(2)] for n in (
            "score_ps", "fT_ps", "out_ps"))
        w_in = m.sem("w_in")
        (x_ready, turned, xT_ready, qk_done, qk_ready, score_done, max_ready, e_ready, inv_ready, by_ready,
         fall_ready, f_ready, fT_done, fT_ready, out_done, h_ready) = (m.sem(n) for n in (
             "x_ready turned xT_ready qk_done qk_ready score_done max_ready e_ready inv_ready by_ready "
             "fall_ready f_ready fT_done fT_ready out_done h_ready").split())

        def at(i, j, k, *work):
            if later(i, j, k):
                for w in work:
                    w(*later(i, j, k))

        with nc.Block() as block:
            @block.sync
            def _(sp):
                for dst, src in ((wq_sb, wq), (wk_sb, wk), (bq_sb, bq), (bk_sb, bk)):
                    sp.dma_start(dst[:], src).then_inc(w_in, 16)
                behind(sp)
                sp.wait_ge(w_in, 64)

            @block.vector
            def _(dve):
                def rows(i, j):
                    b = U * i + j
                    if old(i, j, U):
                        dve.wait_ge(out_done, b - U + 1)
                    normalise(nc, x[j][:, 0, :], h, mean, rstd, 2 * b)
                    normalise(nc, x[j][:, 1, :], h, mean, rstd, 2 * b + 1).then_inc(x_ready, 1)

                def maxima(i, j):
                    b, r = U * i + j, j % 2
                    dve.wait_ge(score_done, b + 1)
                    if old(i, j, 2):
                        dve.wait_ge(e_ready, b - 1)
                    nc.vector.tensor_reduce(neg_max[r][:], score_ps[r][:, :, 0:L], AX.X, ALU.max,
                                            negate=True).then_inc(max_ready, 1)

                def factors(i, j):
                    b, r = U * i + j, j % 2
                    dve.wait_ge(e_ready, b + 1)
                    if old(i, j, 2):
                        dve.wait_ge(fall_ready, b - 1)
                        dve.wait_ge(f_ready, b - 1)
                    nc.vector.reciprocal(inv[r][:], total[r][:]).then_inc(inv_ready, 1)
                    dve.wait_ge(inv_ready, b + 1)
                    nc.vector.tensor_scalar(rise_by[r][:], inv[r][:], INV, None, ALU.mult)
                    nc.vector.tensor_scalar(fall_by[r][:], inv[r][:], -INV, None, ALU.mult).then_inc(by_ready, 1)

                def membership(i, j):
                    b, r = U * i + j, j % 2
                    dve.wait_ge(fall_ready, b + 1)
                    if old(i, j, 2):
                        dve.wait_ge(fT_done, b - 1)
                    for s in range(2):
                        last = nc.vector.scalar_tensor_tensor(f[r][:, s, 0:L], e[r][:, s, 0:L], rise_by[r][:, s:s + 1],
                                                              fall[r][:, s, 0:L], ALU.mult, ALU.min)
                    last.then_inc(f_ready, 1)

                def add(i, j):
                    b, r = U * i + j, j % 2
                    dve.wait_ge(out_done, b + 1)
                    dve.wait_ge(x_ready, b + 1)
                    hb = h[:, bass.ds(2 * b, 2), :]
                    nc.vector.tensor_tensor(hb, hb, out_ps[r][:, :, 0:D], ALU.add).then_inc(h_ready, 1)
                    dve.wait_ge(h_ready, b + 1)
                    for s in range(2):
                        nc.vector.bn_stats(one_tile(stats, 2 * b + s), one_tile(h, 2 * b + s))

                def step(i, j):
                    at(i, j, 2, maxima)
                    at(i, j, 1, membership)
                    at(i, j, 4, rows)
                    at(i, j, 2, factors)
                    at(i, j, 0, add)

                for r in range(2):
                    nc.vector.memset(f[r][:, :, L:T], 0.0)
                steps.run(nc.vector, step, 4)

            @block.scalar
            def _(act):
                def exps(i, j):
                    b, r = U * i + j, j % 2
                    act.wait_ge(max_ready, b + 1)
                    if old(i, j, 2):
                        act.wait_ge(f_ready, b - 1)
                        act.wait_ge(fall_ready, b - 1)
                        act.wait_ge(inv_ready, b - 1)
                    for s in range(2):
                        last = nc.scalar.activation(e[r][:, s, 0:L], score_ps[r][:, s, 0:L], ACT.Exp,
                                                    bias=neg_max[r][:, s:s + 1], accum_out=total[r][:, s:s + 1])
                    last.then_inc(e_ready, 1)

                def read_turned(i, j):
                    b = U * i + j
                    act.wait_ge(turned, b + 1)
                    if old(i, j, 2):
                        act.wait_ge(qk_done, b - 1)
                    nc.scalar.activation(xT[j % 2][:], turn_ps[:, 0, :], ACT.Copy).then_inc(xT_ready, 1)

                def read_qk(i, j):
                    b = U * i + j
                    act.wait_ge(qk_done, b + 1)
                    if old(i, j, 2):
                        act.wait_ge(score_done, b - 1)
                    nc.scalar.activation(qT[j % 2][:], qk_ps[:, 0, :], ACT.Identity, bias=bq_sb[:])
                    nc.scalar.activation(kT[j % 2][:], qk_ps[:, 1, :], ACT.Identity, bias=bk_sb[:])\
                        .then_inc(qk_ready, 1)

                def falling(i, j):
                    b, r = U * i + j, j % 2
                    act.wait_ge(by_ready, b + 1)
                    if old(i, j, 2):
                        act.wait_ge(f_ready, b - 1)
                    for s in range(2):
                        last = nc.scalar.activation(fall[r][:, s, 0:L], e[r][:, s, 0:L], ACT.Relu,
                                                    bias=K["inv03"][:], scale=fall_by[r][:, s:s + 1])
                    last.then_inc(fall_ready, 1)

                def read_fT(i, j):
                    b, r = U * i + j, j % 2
                    act.wait_ge(fT_done, b + 1)
                    if old(i, j, 2):
                        act.wait_ge(out_done, b - 1)
                    nc.scalar.activation(fT[r][:], fT_ps[r][:], ACT.Copy).then_inc(fT_ready, 1)

                def step(i, j):
                    at(i, j, 3, read_turned)
                    at(i, j, 2, exps)
                    at(i, j, 3, read_qk)
                    at(i, j, 2, falling)
                    at(i, j, 1, read_fT)

                act.wait_ge(w_in, 64)
                steps.run(nc.scalar, step, 3)

            @block.tensor
            def _(pe):
                def turn(i, j):
                    b = U * i + j
                    pe.wait_ge(x_ready, b + 1)
                    if old(i, j, 1):
                        pe.wait_ge(xT_ready, b)
                    for s in range(2):
                        last = nc.tensor.transpose(turn_ps[:, 0, s * P:(s + 1) * P], x[j][:, s, :], ident[:])
                    last.then_inc(turned, 1)

                def project(i, j):
                    b = U * i + j
                    pe.wait_ge(xT_ready, b + 1)
                    if old(i, j, 1):
                        pe.wait_ge(qk_ready, b)
                    nc.tensor.matmul(qk_ps[:, 0, :], wq_sb[:], xT[j % 2][:], start=True, stop=True)
                    nc.tensor.matmul(qk_ps[:, 1, :], wk_sb[:], xT[j % 2][:], start=True, stop=True)\
                        .then_inc(qk_done, 1)

                def scores(i, j):
                    b, r = U * i + j, j % 2
                    pe.wait_ge(qk_ready, b + 1)
                    if old(i, j, 2):
                        pe.wait_ge(e_ready, b - 1)
                    for s in range(2):
                        last = nc.tensor.matmul(score_ps[r][:, s, 0:L], qT[r][:, s * P:(s + 1) * P],
                                                kT[r][:, 0:L], start=True, stop=True)
                    last.then_inc(score_done, 1)

                def turn_f(i, j):
                    b, r = U * i + j, j % 2
                    pe.wait_ge(f_ready, b + 1)
                    if old(i, j, 2):
                        pe.wait_ge(fT_ready, b - 1)
                    for s in range(2):
                        for t in range(2):
                            last = nc.tensor.transpose(fT_ps[r][:, t, s * P:(s + 1) * P],
                                                       f[r][:, s, t * P:(t + 1) * P], ident[:])
                    last.then_inc(fT_done, 1)

                def result(i, j):
                    b, r = U * i + j, j % 2
                    pe.wait_ge(fT_ready, b + 1)
                    if old(i, j, 2):
                        pe.wait_ge(h_ready, b - 1)
                    for s in range(2):
                        for t in range(2):
                            last = nc.tensor.matmul(out_ps[r][:, s, 0:D], fT[r][:, t, s * P:(s + 1) * P],
                                                    x[j][:, t, :], start=(t == 0), stop=(t == 1))
                    last.then_inc(out_done, 1)

                def step(i, j):
                    at(i, j, 3, turn)
                    at(i, j, 2, scores)
                    at(i, j, 0, result)
                    at(i, j, 3, project)
                    at(i, j, 1, turn_f)

                pe.wait_ge(w_in, 64)
                steps.run(nc.tensor, step, 3)


E0, HID0 = 8, 512
ST0 = (B * L + E0 * (P - 1)) // P + 1
ST0 += -ST0 % G
E1N, HID1, CAP, TOPK1 = 64, 64, 256, 2
SLOTS0, SLOTS1 = ST0 * P, E1N * CAP
SLOTS = max(SLOTS0, SLOTS1)


CLEARS = SLOTS // (16 * P) + 2


def clear_slots(x_slots, results, zeros, cleared, eng):
    per, again = zeros.shape[1] // D, 4
    n = per * again
    for r in range(0, SLOTS, P * n):
        eng.dma_start(x_slots[r:r + P * n, :].rearrange("(p k n) d -> p k (n d)", p=P, k=again),
                      zeros[:].unsqueeze(1).to_broadcast([P, again, per * D])).then_inc(cleared, 16)
    for y_slots, rows in results:
        eng.dma_start(y_slots[rows:rows + 1, :], zeros[0:1, 0:D]).then_inc(cleared, 16)


def router_logits(nc, K, h, mean, rstd, logits, gate, gate_bias, n_exp, stage):
    ident = K["ident"]
    with Bench(nc, stage) as m:
        gate_sb = m.sb("gate", [P, n_exp])
        bias = m.sb("bias", [P, n_exp])
        x = [m.sb(f"x{j}", [P, G, D]) for j in range(2)]
        xT = [m.sb(f"xT{j}", [P, G, P]) for j in range(2)]
        turn_ps = [m.ps(f"turn_ps{j}", [P, G, P]) for j in range(2)]
        logit_ps = [m.ps(f"logit_ps{j}", [P, 512]) for j in range(2)]
        w_in, x_ready, turned, xT_ready, logit_done, read = (m.sem(n) for n in (
            "w_in", "x_ready", "turned", "xT_ready", "logit_done", "read"))
        loads = 1 if gate_bias is None else 2
        steps = Steps(NT // G, 2)
        later, old = steps.later, steps.old
        with nc.Block() as block:
            @block.sync
            def _(sp):
                sp.dma_start(gate_sb[:], gate).then_inc(w_in, 16)
                if gate_bias is not None:
                    sp.dma_start(bias[:], gate_bias.partition_broadcast(P)).then_inc(w_in, 16)
                sp.wait_ge(w_in, 16 * loads)

            @block.vector
            def _(dve):
                def rows(i, j):
                    g = 2 * i + j
                    if old(i, j, 2):
                        dve.wait_ge(turned, g - 1)
                    for k in range(G):
                        last = normalise(nc, x[j][:, k, :], h, mean, rstd, g * G + k)
                    last.then_inc(x_ready, 1)

                def read_logits(i, j):
                    g = 2 * i + j
                    dve.wait_ge(logit_done, g + 1)
                    to = logits[:, bass.ds(g * G, G), :]
                    src = logit_ps[j][:, 0:G * n_exp].rearrange("p (k e) -> p k e", e=n_exp)
                    if gate_bias is None:
                        nc.vector.tensor_copy(to, src).then_inc(read, 1)
                    else:
                        nc.vector.tensor_tensor(to, src, bias[:].unsqueeze(1).to_broadcast([P, G, n_exp]),
                                                ALU.add).then_inc(read, 1)

                def step(i, j):
                    if later(i, j, 2):
                        rows(*later(i, j, 2))
                    if later(i, j, 0):
                        read_logits(i, j)

                dve.wait_ge(w_in, 16 * loads)
                steps.run(nc.vector, step, 2)

            @block.scalar
            def _(act):
                def step(i, j):
                    g = 2 * i + j
                    act.wait_ge(turned, g + 1)
                    if old(i, j, 2):
                        act.wait_ge(logit_done, g - 1)
                    nc.scalar.activation(xT[j][:], turn_ps[j][:], ACT.Copy).then_inc(xT_ready, 1)

                steps.run(nc.scalar, step, 0)

            @block.tensor
            def _(pe):
                def turn(i, j):
                    g = 2 * i + j
                    pe.wait_ge(x_ready, g + 1)
                    if old(i, j, 2):
                        pe.wait_ge(xT_ready, g - 1)
                    for k in range(G):
                        last = nc.tensor.transpose(turn_ps[j][:, k, :], x[j][:, k, :], ident[:])
                    last.then_inc(turned, 1)

                def multiply(i, j):
                    g = 2 * i + j
                    pe.wait_ge(xT_ready, g + 1)
                    if old(i, j, 2):
                        pe.wait_ge(read, g - 1)
                    for k in range(G):
                        last = nc.tensor.matmul(logit_ps[j][:, k * n_exp:(k + 1) * n_exp], xT[j][:, k, :],
                                                gate_sb[:], start=True, stop=True)
                    last.then_inc(logit_done, 1)

                def step(i, j):
                    if later(i, j, 1):
                        turn(*later(i, j, 1))
                    if later(i, j, 0):
                        multiply(i, j)

                pe.wait_ge(w_in, 16 * loads)
                steps.run(nc.tensor, step, 1)


def route_top1(nc, K, logits, scatter_at, gather_at, tile_expert):
    wide = [P, NT, E0]
    with Bench(nc, "route0") as m:
        best, first, slot = m.sb("best", [P, NT]), m.sb("first", [P, NT]), m.sb("slot", [P, NT])
        work, onehot = m.sb("work", wide), m.sb("onehot", wide)
        onehot_b = m.sb("onehot_b", wide, BF16)
        total = m.sb("total", wide)
        runs = [m.sb(f"run{k}", wide) for k in range(2)]
        ends = [m.sb(f"ends{k}", [P, E0]) for k in range(2)]
        n_tiles, starts = m.sb("n_tiles", [P, E0]), m.sb("starts", [P, E0])
        more = m.sb("more", [P, E0, NT])
        past = m.sb("past", [P, ST0, E0])
        expert_f = m.sb("expert_f", [P, ST0])
        within_ps, total_ps = m.ps("within_ps", wide), m.ps("total_ps", wide)
        vec, onehot_ready, counted = m.sem("vec"), m.sem("onehot_ready"), m.sem("counted")
        with nc.Block() as block:
            @block.vector
            def _(dve):
                link = Chain(dve, vec)
                rank = K["rank0"][:].unsqueeze(1).to_broadcast(wide)
                link(nc.vector.tensor_reduce(best[:], logits[:], AX.X, ALU.max))
                link(nc.vector.tensor_tensor(work[:], logits[:], best[:].unsqueeze(2).to_broadcast(wide),
                                             ALU.is_equal))
                link(nc.vector.tensor_tensor(work[:], work[:], rank, ALU.mult))
                link(nc.vector.tensor_reduce(first[:], work[:], AX.X, ALU.max))
                link(nc.vector.tensor_tensor(work[:], rank, first[:].unsqueeze(2).to_broadcast(wide),
                                             ALU.is_equal))
                link(nc.vector.tensor_tensor(onehot[:], work[:],
                                             K["real"][:].unsqueeze(2).to_broadcast(wide), ALU.mult))
                nc.vector.tensor_copy(onehot_b[:], onehot[:]).then_inc(onehot_ready, 1)
                dve.wait_ge(counted, 1)
                link(nc.vector.tensor_copy(total[:], total_ps[:]))
                now, then = total, runs[0]
                k = 1
                flip = 0
                while k < NT:
                    then = runs[flip]
                    nc.vector.tensor_copy(then[:, 0:k], now[:, 0:k])
                    link(nc.vector.tensor_tensor(then[:, k:NT], now[:, k:NT], now[:, 0:NT - k], ALU.add))
                    now, flip, k = then, 1 - flip, 2 * k
                count = now[:, NT - 1, :]
                link(nc.vector.tensor_tensor(more[:], count.unsqueeze(2).to_broadcast([P, E0, NT]),
                                             K["multiples"][:].unsqueeze(1).to_broadcast([P, E0, NT]),
                                             ALU.is_gt))
                link(nc.vector.tensor_reduce(n_tiles[:], more[:], AX.X, ALU.add))
                upto, k, flip2 = n_tiles, 1, 0
                while k < E0:
                    nxt = ends[flip2]
                    nc.vector.tensor_copy(nxt[:, 0:k], upto[:, 0:k])
                    link(nc.vector.tensor_tensor(nxt[:, k:E0], upto[:, k:E0], upto[:, 0:E0 - k], ALU.add))
                    upto, flip2, k = nxt, 1 - flip2, 2 * k
                link(nc.vector.tensor_tensor(starts[:], upto[:], n_tiles[:], ALU.subtract))
                link(nc.vector.tensor_scalar(starts[:], starts[:], float(P), None, ALU.mult))
                link(nc.vector.tensor_tensor(past[:], K["tile_no"][:, 0:ST0].unsqueeze(2).to_broadcast([P, ST0, E0]),
                                             upto[:].unsqueeze(1).to_broadcast([P, ST0, E0]), ALU.is_ge))
                link(nc.vector.tensor_reduce(expert_f[:], past[:], AX.X, ALU.add))
                nc.vector.tensor_scalar(tile_expert[:], expert_f[:], float(E0 - 1), None, ALU.min)
                link(nc.vector.tensor_tensor(work[:], now[:], total[:], ALU.subtract))
                link(nc.vector.tensor_tensor(work[:], work[:], within_ps[:], ALU.add))
                link(nc.vector.tensor_tensor(work[:], work[:], starts[:].unsqueeze(1).to_broadcast(wide), ALU.add))
                link(nc.vector.tensor_tensor(work[:], work[:], onehot[:], ALU.mult))
                link(nc.vector.tensor_reduce(slot[:], work[:], AX.X, ALU.add))
                nc.vector.tensor_tensor(scatter_at[:, 0, :], slot[:], K["pad_to"][:], ALU.add)
                nc.vector.tensor_tensor(gather_at[:, 0, :], slot[:], K["pad_from"][:], ALU.add)

            @block.tensor
            def _(pe):
                pe.wait_ge(onehot_ready, 1)
                nc.tensor.matmul(within_ps[:], K["after_b"][:], onehot_b[:], start=True, stop=True)
                nc.tensor.matmul(total_ps[:], K["ones_b"][:], onehot_b[:], start=True, stop=True)\
                    .then_inc(counted, 1)


def scatter_rows(nc, h, mean, rstd, x_slots, scatter_at, n_to, stage):
    with Bench(nc, stage) as m:
        x = [m.sb(f"x{j}", [P, D]) for j in range(G)]
        tick = m.sb("tick", [P, 2])
        at = [m.sb(f"at{j}", [P, n_to], U32) for j in range(G)]
        x_ready, tick_ready = m.sem("x_ready"), m.sem("tick_ready")
        sent = [m.sem(f"sent{j}") for j in range(G)]
        with nc.Block() as block:
            @block.vector
            def _(dve):
                def rows(i, first=False):
                    for j in range(G):
                        if not first:
                            dve.wait_ge(sent[j], 16 * n_to * i)
                        nc.vector.tensor_copy(at[j][:].unsqueeze(2), scatter_at[:, 0:n_to, bass.ds(i * G + j, 1)])
                        normalise(nc, x[j][:], h, mean, rstd, i * G + j).then_inc(x_ready, 1)

                rows(0, first=True)
                with nc.vector.Fori(1, NT // G) as i:
                    rows(i)

            @block.gpsimd
            def _(pool):
                nc.gpsimd.memset(tick[:], 0.0).then_inc(tick_ready, 1)
                pool.wait_ge(tick_ready, 1)
                with nc.gpsimd.Fori(0, NT // G) as i:
                    for j in range(G):
                        pool.wait_ge(tick_ready, i * G + j + 1)
                        pool.wait_ge(x_ready, i * G + j + 1)
                        nc.gpsimd.tensor_tensor(tick[:, 1:2], tick[:, 0:1], tick[:, 0:1], ALU.mult)\
                            .then_inc(tick_ready, 1)
                        for k in range(n_to):
                            nc.gpsimd.indirect_dma_start(
                                x_slots[:], bass.IndirectOffsetOnAxis(ap=at[j][:, k:k + 1], axis=0),
                                x[j][:], None).then_inc(sent[j], 16)
                for j in range(G):
                    pool.wait_ge(sent[j], 16 * n_to * (NT // G))


def gather_rows(nc, h, stats, y_slots, gather_at, weight, n_from, stage):
    with Bench(nc, stage) as m:
        y = [m.sb(f"y{j}", [P, n_from, D]) for j in range(2 * G)]
        tick = m.sb("tick", [P, 2])
        at = [m.sb(f"at{j}", [P, n_from], U32) for j in range(2 * G)]
        at_ready, h_ready, tick_ready = m.sem("at_ready"), m.sem("h_ready"), m.sem("tick_ready")
        got = [m.sem(f"got{j}") for j in range(2 * G)]
        W = 2 * G
        with nc.Block() as block:
            @block.vector
            def _(dve):
                def indices(i, j):
                    nc.vector.tensor_copy(at[j][:].unsqueeze(2), gather_at[:, 0:n_from, bass.ds(i * W + j, 1)])\
                        .then_inc(at_ready, 1)

                def add(i, j):
                    dve.wait_ge(got[j], 16 * n_from * (i + 1))
                    n = i * W + j
                    for k in range(n_from):
                        ht = one_tile(h, n)
                        if weight is None:
                            nc.vector.tensor_tensor(ht, ht, y[j][:, k, :], ALU.add).then_inc(h_ready, 1)
                        else:
                            nc.vector.scalar_tensor_tensor(ht, y[j][:, k, :], one_column(weight[k], n), ht,
                                                           ALU.mult, ALU.add).then_inc(h_ready, 1)
                        dve.wait_ge(h_ready, n_from * n + k + 1)
                    if stats is not None:
                        nc.vector.bn_stats(one_tile(stats, n), one_tile(h, n))

                for j in range(W):
                    indices(0, j)
                with nc.vector.Fori(0, NT // W - 1) as i:
                    for j in range(W):
                        add(i, j)
                        indices(i + 1, j)
                for j in range(W):
                    add(NT // W - 1, j)

            @block.gpsimd
            def _(pool):
                nc.gpsimd.memset(tick[:], 0.0).then_inc(tick_ready, 1)
                pool.wait_ge(tick_ready, 1)
                with nc.gpsimd.Fori(0, NT // W) as i:
                    for j in range(W):
                        pool.wait_ge(tick_ready, i * W + j + 1)
                        pool.wait_ge(at_ready, i * W + j + 1)
                        nc.gpsimd.tensor_tensor(tick[:, 1:2], tick[:, 0:1], tick[:, 0:1], ALU.mult)\
                            .then_inc(tick_ready, 1)
                        for k in range(n_from):
                            nc.gpsimd.indirect_dma_start(
                                y[j][:, k, :], None, y_slots[:],
                                bass.IndirectOffsetOnAxis(ap=at[j][:, k:k + 1], axis=0)).then_inc(got[j], 16)


def experts_top1(nc, K, x_slots, y_slots, tile_expert, loaded):
    ident = K["ident"]
    HC = HID0 // P
    WIDE = HID0 + HC
    with Bench(nc, "exp0") as m:
        w1_sb, w2_sb, b2_sb = (loaded.sb[n] for n in ("w1", "w2", "b2"))
        w1n = [m.sb(f"w1_{j}", [P, WIDE]) for j in range(4)]
        w2n = [m.sb(f"w2_{j}", [P, HC * D]) for j in range(2)]
        x = [m.sb(f"x{j}", [P, D]) for j in range(4)]
        xT = [m.sb(f"xT{j}", [P, P]) for j in range(2)]
        hid = [m.sb(f"hid{j}", [P, HC, P]) for j in range(2)]
        y = [m.sb(f"y{j}", [P, D]) for j in range(4)]
        turn_ps = [m.ps(f"turn_ps{j}", [P, 512]) for j in range(2)]
        hid_ps = [[m.ps(f"hid_ps{j}_{k}", [P, 512]) for k in range(2)] for j in range(2)]
        y_ps = [m.ps(f"y_ps{j}", [P, 512]) for j in range(2)]
        x_in = [m.sem(f"x_in{j}") for j in range(4)]
        y_out = [m.sem(f"y_out{j}") for j in range(4)]
        turned, xT_ready, w1_ready, w2_ready, hid_done, hid_a, hid_v, y_done, y_ready = (m.sem(n) for n in (
            "turned xT_ready w1_ready w2_ready hid_done hid_a hid_v y_done y_ready").split())
        steps = Steps(ST0, 4)
        later, old, run = steps.later, steps.old, steps.run
        with nc.Block() as block:
            @block.sync
            def _(sp):
                def load(n, j):
                    sp.dma_start(x[j][:], x_slots[bass.ds(n * P, P), :]).then_inc(x_in[j], 16)

                def step(i, j):
                    n = 4 * i + j
                    sp.wait_ge(turned, n + 1)
                    if later(i, j, 4):
                        load(n + 4, j)
                    sp.wait_ge(y_ready, n + 1)
                    sp.dma_start(y_slots[bass.ds(n * P, P), :], y[j][:]).then_inc(y_out[j], 16)

                for j in range(4):
                    load(j, j)
                run(nc.sync, step, 0)
                for j in range(4):
                    sp.wait_ge(y_out[j], 16 * (ST0 // 4))
                loaded.wait(sp)

            def hidden(eng, relu, i, j, k, ready):
                n = 4 * i + j
                eng.wait_ge(hid_done, n + 1)
                eng.wait_ge(w1_ready, n + 1)
                if old(i, j, 2):
                    eng.wait_ge(y_done, n - 1)
                for c in range(HC // 2):
                    cc = k * (HC // 2) + c
                    last = relu(hid[j % 2][:, cc, :], hid_ps[j % 2][k][:, c * P:(c + 1) * P],
                                w1n[j][:, HID0 + cc:HID0 + cc + 1])
                last.then_inc(ready, 1)

            @block.vector
            def _(dve):
                def expert(n):
                    return nc.vector.value_load(tile_expert[0:1, bass.ds(n, 1)], min_val=0, max_val=E0 - 1)

                def weights(i, j):
                    n = 4 * i + j
                    if old(i, j, 4):
                        dve.wait_ge(hid_done, n - 3)
                        dve.wait_ge(hid_a, n - 3)
                        dve.wait_ge(hid_v, n - 3)
                    ex = expert(n)
                    nc.vector.tensor_copy(w1n[j][:], w1_sb[:, bass.ds(ex, 1), :].rearrange("p a n -> p (a n)"))\
                        .then_inc(w1_ready, 1)

                def relu(out, in_, bias):
                    return nc.vector.tensor_scalar(out, in_, bias, 0.0, ALU.add, ALU.max)

                def result(i, j):
                    n = 4 * i + j
                    ex = expert(n)
                    dve.wait_ge(y_done, n + 1)
                    if old(i, j, 4):
                        dve.wait_ge(y_out[j], 16 * i)
                    nc.vector.tensor_tensor(y[j][:], y_ps[j % 2][:, 0:D],
                                            b2_sb[:, bass.ds(ex, 1), :].rearrange("p a n -> p (a n)"),
                                            ALU.add).then_inc(y_ready, 1)

                def step(i, j):
                    if later(i, j, 1):
                        hidden(dve, relu, *later(i, j, 1), 1, hid_v)
                    if later(i, j, 0):
                        result(i, j)
                    if later(i, j, 3):
                        weights(*later(i, j, 3))

                loaded.wait(dve)
                run(nc.vector, step, 3)

            @block.scalar
            def _(act):
                def read_turned(i, j):
                    n = 4 * i + j
                    act.wait_ge(turned, n + 1)
                    if old(i, j, 2):
                        act.wait_ge(hid_done, n - 1)
                    nc.scalar.activation(xT[j % 2][:], turn_ps[j % 2][:, 0:P], ACT.Copy).then_inc(xT_ready, 1)

                def weights(i, j):
                    n = 4 * i + j
                    ex = nc.scalar.value_load(tile_expert[0:1, bass.ds(n, 1)], min_val=0, max_val=E0 - 1)
                    if old(i, j, 2):
                        act.wait_ge(y_done, n - 1)
                    nc.scalar.activation(w2n[j % 2][:], w2_sb[:, bass.ds(ex, 1), :].rearrange("p a n -> p (a n)"),
                                         ACT.Copy).then_inc(w2_ready, 1)

                def relu(out, in_, bias):
                    return nc.scalar.activation(out, in_, ACT.Relu, bias=bias)

                def step(i, j):
                    if later(i, j, 2):
                        read_turned(*later(i, j, 2))
                    if later(i, j, 1):
                        hidden(act, relu, *later(i, j, 1), 0, hid_a)
                        weights(*later(i, j, 1))

                loaded.wait(act)
                run(nc.scalar, step, 2)

            @block.tensor
            def _(pe):
                def turn(i, j):
                    n = 4 * i + j
                    pe.wait_ge(x_in[j], 16 * i + 16)
                    if old(i, j, 2):
                        pe.wait_ge(xT_ready, n - 1)
                    nc.tensor.transpose(turn_ps[j % 2][:, 0:P], x[j][:], ident[:]).then_inc(turned, 1)

                def up(i, j):
                    n = 4 * i + j
                    pe.wait_ge(xT_ready, n + 1)
                    pe.wait_ge(w1_ready, n + 1)
                    if old(i, j, 2):
                        pe.wait_ge(hid_a, n - 1)
                        pe.wait_ge(hid_v, n - 1)
                    for c in range(HC):
                        k, cc = c // (HC // 2), c % (HC // 2)
                        last = nc.tensor.matmul(hid_ps[j % 2][k][:, cc * P:(cc + 1) * P],
                                                w1n[j][:, c * P:(c + 1) * P], xT[j % 2][:], start=True, stop=True)
                    last.then_inc(hid_done, 1)

                def down(i, j):
                    n = 4 * i + j
                    pe.wait_ge(hid_a, n + 1)
                    pe.wait_ge(hid_v, n + 1)
                    pe.wait_ge(w2_ready, n + 1)
                    if old(i, j, 2):
                        pe.wait_ge(y_ready, n - 1)
                    for c in range(HC):
                        last = nc.tensor.matmul(y_ps[j % 2][:, 0:D], hid[j % 2][:, c, :],
                                                w2n[j % 2][:, c * D:(c + 1) * D],
                                                start=(c == 0), stop=(c == HC - 1))
                    last.then_inc(y_done, 1)

                def step(i, j):
                    if later(i, j, 2):
                        turn(*later(i, j, 2))
                    if later(i, j, 1):
                        up(*later(i, j, 1))
                    if later(i, j, 0):
                        down(i, j)

                run(nc.tensor, step, 2)


H, HD, MAX_REL = 8, 16, 68
HALF = 8
BQ = 2 * HALF
NBLK = T // BQ
GB = 4
NGRP = NBLK // GB
REACH = MAX_REL - 1
KWIN = 2 * REACH + BQ + HALF
VWIN = P + T
FARWIN = 2 * T - BQ


def near_tiles(blk):
    q0 = BQ * blk
    return [t for t in range(2) if t * P - (q0 + BQ - 1) < MAX_REL and t * P + P - 1 - q0 > -MAX_REL]


def attention_weights(bench, w):
    def rows(name):
        return w[name].partition_broadcast(P)

    return Ahead(bench, {
        "wq": ([P, D], w["rel_wq"]), "bq": ([P, 1], w["rel_bq"]),
        "wk": ([P, D], w["rel_wk"]), "bk": ([P, 1], w["rel_bk"]),
        "wv": ([P, D], w["rel_wv"]), "bv": ([P, D], rows("rel_bv")),
        "wo": ([P, D], w["rel_wo"]), "bo": ([P, D], rows("rel_bo")),
        "far_keys": ([P, FARWIN], w["rel_far"]),
        "value_ends": ([P, 2, D], rows("rel_vends")),
        "key_table": ([P, KWIN], w["rel_ktab"]), "value_table": ([P, VWIN, HD], w["rel_vtab"])})


def relative_attention(nc, K, h, mean, rstd, stats, o_rows, q_rows, weights):
    SCALE = 1.0 / float(D) ** 0.5
    ident = K["ident"]
    with Bench(nc, "rel") as m:
        wq_sb, bq_sb, wk_sb, bk_sb, wv_sb, bv_sb, wo_sb, bo_sb, far_sb, vends_sb, ktab, vtab = (
            weights.sb[n] for n in "wq bq wk bk wv bv wo bo far_keys value_ends key_table value_table".split())
        x, xT, qT = m.sb("x", [P, 2, D]), m.sb("xT", [P, T]), m.sb("qT", [P, T])
        q_p = [m.sb(f"qT_{k}", [P, T], FP32R) for k in "hl"]
        kT = [m.sb(f"kT{r}", [P, T]) for r in range(2)]
        k_grp = [m.sb(f"k_grp{r}", [P, GB, T]) for r in range(2)]
        v = [m.sb(f"v{r}", [P, 2, D]) for r in range(2)]
        v_far = [m.sb(f"v_far{r}", [P, 2, D]) for r in range(2)]
        k_grp_p = [[m.sb(f"k_grp{r}_{k}", [P, GB, T], FP32R) for k in "hl"] for r in range(2)]
        q_head = [[m.sb(f"q_head{r}_{k}", [P, 2 * NBLK, H, HALF], FP32R) for k in "hl"] for r in range(2)]
        q_rep = m.sb("q_rep", [P, H, T])
        q_pos = [m.sb(f"q_pos{r}", [P, 2 * NBLK, H, HALF]) for r in range(2)]
        den = [m.sb(f"den{r}", [P, NBLK]) for r in range(2)]
        e = [m.sb(f"e{r}", [P, GB, T]) for r in range(2)]
        neg_max = [m.sb(f"neg_max{r}", [P, GB]) for r in range(2)]
        bias = [m.sb(f"bias{r}", [P, GB]) for r in range(2)]
        eT = m.sb("eT", [P, GB, 2, P])
        kept = m.sb("kept", [P, GB, 2 * D])
        o, o_norm, rden = m.sb("o", [P, NBLK, HD]), m.sb("o_norm", [P, NBLK, HD]), m.sb("rden", [P, NBLK])
        o_tok = m.sb("o_tok", [P, 2, D])
        oT = m.sb("oT", [P, T])
        s_ps = m.ps("s_ps", [P, GB, T])
        t_ps = m.ps("t_ps", [P, GB, 2, P])
        pv_ps = m.ps("pv_ps", [P, GB, 2 * D])
        pa, pb = m.ps("pa", [P, 2, T]), m.ps("pb", [P, 2, T])
        (ready, x_ready, xT_done, xT_ready, qk_done, q_ready, k_ready, kg_ready, kh_ready, kl_ready, ql_ready, qh_ready, q_out, q_in,
         qp_ready, v_done, v_ready, s_done, max_ready, bias_ready, e_ready, t_done, eT_a, eT_v,
         pv_done, kept_ready, o_part, rden_ready, o_ready, o_out, o_in, oT_done, oT_ready, out_done,
         h_ready) = (m.sem(n) for n in (
             "ready x_ready xT_done xT_ready qk_done q_ready k_ready kg_ready kh_ready kl_ready ql_ready qh_ready q_out q_in "
             "qp_ready v_done v_ready s_done max_ready bias_ready e_ready t_done eT_a eT_v "
             "pv_done kept_ready o_part rden_ready o_ready o_out o_in oT_done oT_ready out_done "
             "h_ready").split())
        mask16, mask_pv = K["mask16"], K["mask_pv"]
        def run(engine, slot, head, tail):
            def pair(i, first=False, last=False):
                for r in range(2):
                    for g in range(NGRP):
                        slot(2 * i + r, g, r, first and r == 0, last and r == 1)
            head()
            pair(0, first=True)
            with engine.Fori(1, B // 2 - 1) as i:
                pair(i)
            pair(B // 2 - 1, last=True)
            tail()

        with nc.Block() as block:
            @block.sync
            def _(sp):
                def repeat_queries(b, r, first=False):
                    sp.wait_ge(q_ready, b + 1)
                    sp.dma_start(q_rows[r], qT[:]).then_inc(q_out, 16)
                    sp.wait_ge(q_out, 16 * b + 16)
                    if not first:
                        sp.wait_ge(qp_ready, b)
                    for i in range(HALF):
                        sp.dma_start(q_rep[i * HD:(i + 1) * HD], q_rows[r].rearrange("(h d) q -> d h q", d=HD))\
                            .then_inc(q_in, 16)

                def turn_rows(b, r, first=False):
                    sp.wait_ge(o_ready, b + 1)
                    sp.dma_start(o_rows[r].rearrange("s p k -> p s k"),
                                 o_norm[:].rearrange("p (s n) d -> p s (n d)", s=2)).then_inc(o_out, 16)
                    sp.wait_ge(o_out, 16 * b + 16)
                    if not first:
                        sp.wait_ge(oT_done, b)
                    for s in range(2):
                        for a in range(2):
                            sp.dma_start(o_tok[64 * a:64 * a + 64, s, :].rearrange("p (h d) -> p h d", h=H),
                                         o_rows[r][s, 64 * a:64 * a + 64, :]
                                         .rearrange("(h i) (n d) -> (i n) h d", h=H, d=HD)).then_inc(o_in, 16)

                repeat_queries(0, 0, first=True)
                for b in range(2):
                    repeat_queries(b + 1, 1 - b)
                    turn_rows(b, b, first=(b == 0))
                with nc.sync.Fori(1, B // 2 - 1) as i:
                    for r in range(2):
                        repeat_queries(2 * i + r + 1, 1 - r)
                        turn_rows(2 * i + r, r)
                repeat_queries(B - 1, 1)
                turn_rows(B - 2, 0)
                turn_rows(B - 1, 1)
                sp.wait_ge(o_in, 64 * B)

            @block.tensor
            def _(pe):
                def turn_x(b):
                    pe.wait_ge(x_ready, b + 1)
                    for s in range(2):
                        last = nc.tensor.transpose(pa[:, 0, s * P:(s + 1) * P], x[:, s, :], ident[:])
                    last.then_inc(xT_done, 1)

                def project_qk(b):
                    pe.wait_ge(xT_ready, b + 1)
                    nc.tensor.matmul(pa[:, 0, :], wq_sb[:], xT[:], start=True, stop=True)
                    nc.tensor.matmul(pa[:, 1, :], wk_sb[:], xT[:], start=True, stop=True).then_inc(qk_done, 1)

                def project_v(b):
                    pe.wait_ge(k_ready, b + 1)
                    for s in range(2):
                        last = nc.tensor.matmul(pa[:, 0, s * P:(s + 1) * P], xT[:, s * P:(s + 1) * P], wv_sb[:],
                                                start=True, stop=True)
                    last.then_inc(v_done, 1)

                def scores(b, g, r, first=False):
                    if g == 0:
                        pe.wait_ge(qh_ready, 2 * b + 2)
                        pe.wait_ge(qp_ready, b + 1)
                    pe.wait_ge(kh_ready, NGRP * b + g + 1)
                    pe.wait_ge(kl_ready, NGRP * b + g + 1)
                    if not first:
                        pe.wait_ge(e_ready, NGRP * b + g)
                    for n in range(GB):
                        blk = GB * g + n
                        for qk, kk in THREE:
                            nc.tensor.matmul(s_ps[:, n, :],
                                             q_head[r][qk][:, 2 * blk:2 * blk + 2].rearrange("p a h i -> p (a h i)"),
                                             k_grp_p[g % 2][kk][:, n, :],
                                             start=((qk, kk) == (0, 0) and n % 2 == 0), stop=False,
                                             skip_group_check=True)
                    for n in range(GB):
                        blk = GB * g + n
                        q0 = BQ * blk
                        near = max(0, q0 - REACH), min(L, q0 + BQ + REACH)
                        for a in range(2):
                            off = REACH + HALF - q0 - HALF * a
                            last = nc.tensor.matmul(
                                s_ps[64 * a:64 * a + 64, n, near[0]:near[1]],
                                q_pos[r][:, 2 * blk + a].rearrange("p h i -> p (h i)"),
                                ktab[:, near[0] + off:near[1] + off], start=False, stop=True,
                                skip_group_check=True)
                    last.then_inc(s_done, 1)

                def turn_e(b, g):
                    pe.wait_ge(e_ready, NGRP * b + g + 1)
                    for n in range(GB):
                        for t in range(2):
                            last = nc.tensor.transpose(t_ps[:, n, t, :], e[g % 2][:, n, t * P:(t + 1) * P], ident[:])
                    last.then_inc(t_done, 1)

                def values(b, g, r, first=False):
                    pe.wait_ge(eT_a, NGRP * b + g + 1)
                    pe.wait_ge(eT_v, NGRP * b + g + 1)
                    if g == 0:
                        pe.wait_ge(v_ready, b + 1)
                    if not first:
                        pe.wait_ge(kept_ready, NGRP * b + g)
                    for n in range(GB):
                        blk = GB * g + n
                        for t in range(2):
                            values_of = v if t in near_tiles(blk) else v_far
                            nc.tensor.matmul(pv_ps[:, n, 0:D], eT[:, n, t, :], values_of[r][:, t, :],
                                             start=(t == 0), stop=(t == 1), skip_group_check=True)
                    for n in range(GB):
                        blk = GB * g + n
                        near = near_tiles(blk)
                        for t in near:
                            for a in range(2):
                                u = P + BQ * blk + HALF * a - P * t
                                last = nc.tensor.matmul(
                                    pv_ps[64 * a:64 * a + 64, n, D:2 * D], eT[:, n, t, 64 * a:64 * a + 64],
                                    vtab[:, u:u + HALF, :].rearrange("p u d -> p (u d)"),
                                    start=(t == near[0]), stop=(t == near[-1]), skip_group_check=True)
                    last.then_inc(pv_done, 1)

                def turn_o(b):
                    pe.wait_ge(o_in, 64 * b + 64)
                    if not isinstance(b, int) or b > 0:
                        pe.wait_ge(h_ready, 2 * b - 1)
                    for s in range(2):
                        last = nc.tensor.transpose(pb[:, 0, s * P:(s + 1) * P], o_tok[:, s, :], ident[:])
                    last.then_inc(oT_done, 1)

                def project_out(b):
                    pe.wait_ge(oT_ready, b + 1)
                    for s in range(2):
                        last = nc.tensor.matmul(pb[:, 0, s * P:(s + 1) * P], oT[:, s * P:(s + 1) * P], wo_sb[:],
                                                start=True, stop=True)
                    last.then_inc(out_done, 1)

                def slot(b, g, r, first, last):
                    turn_e(b, g)
                    if g + 1 < NGRP:
                        scores(b, g + 1, r)
                    elif not last:
                        scores(b + 1, 0, 1 - r)
                    if g == 0 and not last:
                        turn_x(b + 1)
                    if g == 1 and not last:
                        project_v(b + 1)
                    if g == 3 and not first:
                        turn_o(b - 1)
                    values(b, g, r, first and g == 0)
                    if g == 0 and not last:
                        project_qk(b + 1)
                    if g == 3 and not first:
                        project_out(b - 1)

                def head():
                    weights.wait(pe)
                    turn_x(0)
                    project_qk(0)
                    project_v(0)
                    scores(0, 0, 0, first=True)

                def tail():
                    turn_o(B - 1)
                    project_out(B - 1)

                run(nc.tensor, slot, head, tail)

            @block.scalar
            def _(act):
                def read_x(b):
                    act.wait_ge(xT_done, b + 1)
                    nc.scalar.activation(xT[:], pa[:, 0, :], ACT.Copy).then_inc(xT_ready, 1)

                def read_qk(b, r):
                    act.wait_ge(qk_done, b + 1)
                    if not isinstance(b, int) or b > 0:
                        act.wait_ge(q_out, 16 * b)
                        act.wait_ge(qh_ready, 2 * b)
                    nc.scalar.activation(q_p[0][:], pa[:, 0, :], ACT.Identity, bias=bq_sb[:])
                    nc.scalar.activation(qT[:], pa[:, 0, :], ACT.Identity, bias=bq_sb[:]).then_inc(q_ready, 1)
                    nc.scalar.activation(kT[r][:], pa[:, 1, :], ACT.Identity, bias=bk_sb[:]).then_inc(k_ready, 1)

                def exps(b, g, r):
                    act.wait_ge(bias_ready, NGRP * b + g + 1)
                    for n in range(GB):
                        last = nc.scalar.activation(e[g % 2][:, n, 0:L], s_ps[:, n, 0:L], ACT.Exp,
                                                    bias=bias[g % 2][:, n:n + 1], scale=SCALE,
                                                    accum_out=den[r][:, GB * g + n:GB * g + n + 1])
                    last.then_inc(e_ready, 1)

                def round_keys(b, g):
                    act.wait_ge(kg_ready, NGRP * b + g + 1)
                    if not isinstance(b, int) or NGRP * b + g >= 2:
                        act.wait_ge(s_done, NGRP * b + g - 1)
                    nc.scalar.activation(k_grp_p[g % 2][0][:], k_grp[g % 2][:], ACT.Copy).then_inc(kh_ready, 1)

                def read_eT(b, g):
                    act.wait_ge(t_done, NGRP * b + g + 1)
                    nc.scalar.activation(eT[:, 0:2], t_ps[:, 0:2], ACT.Copy).then_inc(eT_a, 1)

                def read_o(b):
                    act.wait_ge(oT_done, b + 1)
                    for s in range(2):
                        last = nc.scalar.activation(
                            oT[:, s * P:(s + 1) * P].rearrange("p (n a i) -> p a i n", a=2, i=HALF),
                            pb[:, 0, s * P:(s + 1) * P].rearrange("p (a i n) -> p a i n", a=2, i=HALF), ACT.Copy)
                    last.then_inc(oT_ready, 1)

                def slot(b, g, r, first, last):
                    read_eT(b, g)
                    if g < 2:
                        round_keys(b, g + 2)
                    elif not last:
                        round_keys(b + 1, g - 2)
                    if g + 1 < NGRP:
                        exps(b, g + 1, r)
                    elif not last:
                        exps(b + 1, 0, 1 - r)
                    if g == 0 and not last:
                        read_x(b + 1)
                        read_qk(b + 1, 1 - r)
                    if g == 3 and not first:
                        read_o(b - 1)

                def head():
                    act.wait_ge(ready, 1)
                    read_x(0)
                    read_qk(0, 0)
                    for g in range(2):
                        round_keys(0, g)
                    exps(0, 0, 0)

                run(nc.scalar, slot, head, lambda: read_o(B - 1))

            @block.gpsimd
            def _(pool):
                wide = [P, 2 * NBLK, H, HALF]

                def queries(b, r, k):
                    wide = [P, 2 * NBLK, H, HALF]
                    pool.wait_ge(ql_ready, b + 1)
                    nc.gpsimd.tensor_tensor(
                        q_head[r][k][:],
                        q_p[k][:].bitcast(FP32).rearrange("p (n i) -> p n i", i=HALF).unsqueeze(2).to_broadcast(wide),
                        mask16[:].unsqueeze(1).unsqueeze(3).to_broadcast(wide), ALU.mult).then_inc(qh_ready, 1)

                def keys(b, g, r, early=False):
                    if g == 0:
                        pool.wait_ge(k_ready, b + 1)
                    if not early:
                        pool.wait_ge(kh_ready, NGRP * b + g - 1)
                        pool.wait_ge(kl_ready, NGRP * b + g - 1)
                    for n in range(GB):
                        u = T - BQ - BQ * (GB * g + n)
                        last = nc.gpsimd.tensor_tensor(k_grp[g % 2][:, n, :], kT[r][:], far_sb[:, u:u + T], ALU.add)
                    last.then_inc(kg_ready, 1)

                def slot(b, g, r, first, last):
                    if g < 2:
                        keys(b, g + 2, r)
                    elif not last:
                        keys(b + 1, g - 2, 1 - r)
                    if g in (1, 2) and not last:
                        queries(b + 1, 1 - r, g - 1)

                def head():
                    weights.wait(pool)
                    keys(0, 0, 0, early=True)
                    queries(0, 0, 0)
                    queries(0, 0, 1)
                    keys(0, 1, 0, early=True)

                run(nc.gpsimd, slot, head, lambda: None)

            @block.vector
            def _(dve):
                def read_x(b):
                    normalise(nc, x[:, 0, :], h, mean, rstd, 2 * b)
                    normalise(nc, x[:, 1, :], h, mean, rstd, 2 * b + 1).then_inc(x_ready, 1)

                def q_remainder(b):
                    dve.wait_ge(q_ready, b + 1)
                    rest(nc.vector, q_p[1][:], qT[:], q_p[0][:]).then_inc(ql_ready, 1)

                def positions(b, r):
                    wide = [P, 2 * NBLK, H, HALF]
                    dve.wait_ge(q_in, 16 * HALF * (b + 1))
                    nc.vector.tensor_tensor(
                        q_pos[r][:], q_rep[:].rearrange("p h (n i) -> p n h i", i=HALF),
                        mask16[:].unsqueeze(1).unsqueeze(1).to_broadcast(wide), ALU.mult).then_inc(qp_ready, 1)

                def keys_remainder(b, g):
                    dve.wait_ge(kh_ready, NGRP * b + g + 1)
                    rest(nc.vector, k_grp_p[g % 2][1][:], k_grp[g % 2][:], k_grp_p[g % 2][0][:]).then_inc(kl_ready, 1)

                def read_v(b, r):
                    dve.wait_ge(v_done, b + 1)
                    for to, bias_sb in ((v, bv_sb[:].unsqueeze(1).to_broadcast([P, 2, D])), (v_far, vends_sb[:])):
                        last = nc.vector.tensor_tensor(to[r][:], pa[:, 0, :].rearrange("p (s d) -> p s d", s=2),
                                                       bias_sb, ALU.add)
                    last.then_inc(v_ready, 1)

                def maxima(b, g):
                    dve.wait_ge(s_done, NGRP * b + g + 1)
                    nc.vector.tensor_reduce(neg_max[g % 2][:], s_ps[:, :, 0:L], AX.X, ALU.max, negate=True)\
                        .then_inc(max_ready, 1)
                    dve.wait_ge(max_ready, NGRP * b + g + 1)
                    nc.vector.tensor_scalar(bias[g % 2][:], neg_max[g % 2][:], SCALE, None, ALU.mult)\
                        .then_inc(bias_ready, 1)

                def read_eT(b, g):
                    dve.wait_ge(t_done, NGRP * b + g + 1)
                    nc.vector.tensor_copy(eT[:, 2:4], t_ps[:, 2:4]).then_inc(eT_v, 1)

                def keep(b, g, r, first):
                    dve.wait_ge(pv_done, NGRP * b + g + 1)
                    if not (first and g == 0):
                        dve.wait_ge(o_part, NGRP * b + g)
                    if g == 0 and not first:
                        dve.wait_ge(o_ready, b)
                    nc.vector.tensor_tensor(kept[:], pv_ps[:], mask_pv[:].unsqueeze(1).to_broadcast([P, GB, 2 * D]),
                                            ALU.mult).then_inc(kept_ready, 1)
                    dve.wait_ge(kept_ready, NGRP * b + g + 1)
                    nc.vector.tensor_reduce(o[:, GB * g:GB * g + GB, :],
                                            kept[:].rearrange("p n (k d) -> p n d k", d=HD), AX.X, ALU.add)\
                        .then_inc(o_part, 1)
                    if g == NGRP - 1:
                        nc.vector.reciprocal(rden[:], den[r][:]).then_inc(rden_ready, 1)
                        dve.wait_ge(rden_ready, b + 1)
                        dve.wait_ge(o_part, NGRP * b + NGRP)
                        if not first:
                            dve.wait_ge(o_out, 16 * b)
                        nc.vector.tensor_tensor(o_norm[:], o[:], rden[:].unsqueeze(2).to_broadcast([P, NBLK, HD]),
                                                ALU.mult).then_inc(o_ready, 1)

                def add_out(b):
                    dve.wait_ge(out_done, b + 1)
                    hb = h[:, bass.ds(2 * b, 2), :]
                    nc.vector.tensor_tensor(hb, hb, pb[:, 0, :].rearrange("p (s d) -> p s d", s=2), ALU.add)\
                        .then_inc(h_ready, 1)
                    dve.wait_ge(h_ready, 2 * b + 1)
                    nc.vector.tensor_tensor(hb, hb, bo_sb[:].unsqueeze(1).to_broadcast([P, 2, D]), ALU.add)\
                        .then_inc(h_ready, 1)
                    dve.wait_ge(h_ready, 2 * b + 2)
                    for s in range(2):
                        nc.vector.bn_stats(one_tile(stats, 2 * b + s), one_tile(h, 2 * b + s))

                def slot(b, g, r, first, last):
                    if g == 1 and not last:
                        q_remainder(b + 1)
                    read_eT(b, g)
                    if g == 0 and not last:
                        read_x(b + 1)
                    if g + 1 < NGRP:
                        maxima(b, g + 1)
                    elif not last:
                        maxima(b + 1, 0)
                    if g < 2:
                        keys_remainder(b, g + 2)
                    elif not last:
                        keys_remainder(b + 1, g - 2)
                    if g == 1 and not last:
                        read_v(b + 1, 1 - r)
                    if g == 2 and not last:
                        positions(b + 1, 1 - r)
                    if g == 0 and not (isinstance(b, int) and b < 2):
                        add_out(b - 2)
                    keep(b, g, r, first)

                def head():
                    for r in range(2):
                        nc.vector.memset(e[r][:, :, L:T], 0.0)
                    weights.wait(dve)
                    nc.vector.tensor_tensor(vends_sb[:], vends_sb[:], bv_sb[:].unsqueeze(1).to_broadcast([P, 2, D]),
                                            ALU.add).then_inc(ready, 1)
                    dve.wait_ge(ready, 1)
                    read_x(0)
                    q_remainder(0)
                    read_v(0, 0)
                    for g in range(2):
                        keys_remainder(0, g)
                    positions(0, 0)
                    maxima(0, 0)

                def tail():
                    add_out(B - 2)
                    add_out(B - 1)

                run(nc.vector, slot, head, tail)


ROUTE_SCALE = 2.5


def choose_and_send(nc, K, h, shift, rstd, x_slots, gather_at, weight, gate_w):
    ident = K["ident"]
    CT = 512 // E1N
    N = NT // CT
    wide, small = [P, CT, E1N], [P, TOPK1, CT]
    steps = Steps(N, 2)
    later, old = steps.later, steps.old
    with Bench(nc, "send") as m:
        gate_sb = m.sb("gate_w", [P, E1N])
        x = [m.sb(f"x{j}", [P, CT, D]) for j in range(2)]
        xT = [m.sb(f"xT{j}", [P, CT, P]) for j in range(2)]
        at = [m.sb(f"at{j}", small, U32) for j in range(2)]
        logits, work = m.sb("logits", wide), m.sb("work", wide)
        mask, rank_b = m.sb("mask", wide, BF16), m.sb("rank_b", [P, E1N], BF16)
        onehot = [m.sb(f"onehot{k}", wide, BF16) for k in range(TOPK1)]
        first = m.sb("first", small, BF16)
        both = [m.sb(f"both{j}", wide, BF16) for j in range(2)]
        before = m.sb("before", [P, E1N])
        before_b = [m.sb(f"before_b{j}", [P, E1N], BF16) for j in range(2)]
        chunk_sum = m.sb("chunk_sum", [P, E1N])
        best, place, valid, row, other, sig, share_of = (m.sb(n, small) for n in (
            "best place valid row other sig share_of").split())
        sums = m.sb("sums", [P, CT])
        tick = m.sb("tick", [P, 1])
        turn_ps = [m.ps(f"turn_ps{k}", [P, G, P]) for k in range(2)]
        logit_ps, count_ps = m.ps("logit_ps", wide), m.ps("count_ps", wide)
        (w_in, vec, x_ready, turned, xT_ready, logit_done, logit_read, both_ready, sig_ready,
         count_done, at_ready, tick_ready) = (
            m.sem(n) for n in (
                "w_in vec x_ready turned xT_ready logit_done logit_read both_ready sig_ready "
                "count_done at_ready tick_ready").split())
        sent = [m.sem(f"sent{j}") for j in range(2)]
        PER_CHUNK = 16 * TOPK1 * CT
        LINKS_A, LINKS_B = 14, 18
        with nc.Block() as block:
            @block.sync
            def _(sp):
                sp.dma_start(gate_sb[:], gate_w).then_inc(w_in, 16)
                sp.wait_ge(w_in, 16)

            @block.vector
            def _(dve):
                def choose(i, j):
                    c = 2 * i + j
                    base = (LINKS_A + LINKS_B) * c
                    link = Chain(dve, vec, base)
                    rank = rank_b[:].unsqueeze(1).to_broadcast(wide)
                    dve.wait_ge(logit_read, c + 1)
                    for k in range(TOPK1):
                        link(nc.vector.tensor_reduce(best[:, k], logits[:], AX.X, ALU.max))
                        link(nc.vector.tensor_tensor(mask[:], logits[:], best[:, k].unsqueeze(2).to_broadcast(wide),
                                                     ALU.is_equal))
                        link(nc.vector.tensor_tensor(mask[:], mask[:], rank, ALU.mult))
                        link(nc.vector.tensor_reduce(first[:, k], mask[:], AX.X, ALU.max))
                        link(nc.vector.tensor_tensor(onehot[k][:], rank, first[:, k].unsqueeze(2).to_broadcast(wide),
                                                     ALU.is_equal))
                        if k == 0:
                            link(nc.vector.scalar_tensor_tensor(logits[:], onehot[0][:], -3.0e38, logits[:],
                                                                ALU.mult, ALU.add))
                    link(nc.vector.tensor_copy(before_b[j][:], before[:]))
                    link(nc.vector.tensor_tensor(mask[:], onehot[0][:], onehot[1][:], ALU.add))
                    nc.vector.tensor_tensor(both[j][:], mask[:], K["real"][:, bass.ds(c * CT, CT)].unsqueeze(2)
                                            .to_broadcast(wide), ALU.mult).then_inc(both_ready, 1)
                    dve.wait_ge(both_ready, c + 1)
                    link(nc.vector.tensor_reduce(chunk_sum[:], both[j][:].rearrange("p t e -> p e t"), AX.X, ALU.add))
                    assert not isinstance(c, int) or link.n == base + LINKS_A

                def locate(i, j):
                    c = 2 * i + j
                    base = (LINKS_A + LINKS_B) * c + LINKS_A
                    link = Chain(dve, vec, base)
                    tiles = bass.ds(c * CT, CT)
                    dve.wait_ge(count_done, c + 1)
                    link(nc.vector.tensor_tensor(before[:], before[:], chunk_sum[:], ALU.add))
                    for k in range(TOPK1):
                        link(nc.vector.tensor_tensor(work[:], onehot[k][:], count_ps[:], ALU.mult))
                        link(nc.vector.tensor_reduce(place[:, k], work[:], AX.X, ALU.add))
                    link(nc.vector.tensor_scalar(valid[:], place[:], float(CAP), None, ALU.is_lt))
                    link(nc.vector.tensor_tensor(valid[:], valid[:], K["real"][:, tiles].unsqueeze(1)
                                                 .to_broadcast(small), ALU.mult))
                    link(nc.vector.tensor_scalar(row[:], first[:], -float(CAP), float(CAP * E1N), ALU.mult, ALU.add))
                    link(nc.vector.tensor_tensor(row[:], row[:], place[:], ALU.add))
                    link(nc.vector.tensor_tensor(row[:], row[:], valid[:], ALU.mult))
                    link(nc.vector.tensor_scalar(other[:], valid[:], -1.0, 1.0, ALU.mult, ALU.add))
                    link(nc.vector.scalar_tensor_tensor(gather_at[:, :, tiles], other[:], float(SLOTS1), row[:],
                                                        ALU.mult, ALU.add))
                    link(nc.vector.tensor_tensor(other[:], other[:], K["spill"][:].rearrange(
                        "p (k n) -> p k n", k=TOPK1)[:, :, tiles], ALU.mult))
                    nc.vector.tensor_tensor(at[j][:], other[:], row[:], ALU.add).then_inc(at_ready, 1)
                    dve.wait_ge(sig_ready, c + 1)
                    link(nc.vector.tensor_tensor(sums[:], sig[:, 0], sig[:, 1], ALU.add))
                    link(nc.vector.tensor_scalar(sums[:], sums[:], 1e-20, None, ALU.add))
                    link(nc.vector.reciprocal(sums[:], sums[:]))
                    link(nc.vector.tensor_tensor(share_of[:], sig[:], sums[:].unsqueeze(1).to_broadcast(small),
                                                 ALU.mult))
                    link(nc.vector.scalar_tensor_tensor(weight[:, :, tiles], share_of[:], ROUTE_SCALE, valid[:],
                                                        ALU.mult, ALU.mult))
                    dve.wait_ge(at_ready, c + 1)
                    assert not isinstance(c, int) or link.n == base + LINKS_B

                def step(i, j):
                    if later(i, j, 0):
                        locate(i, j)
                    if later(i, j, 1):
                        choose(*later(i, j, 1))

                nc.vector.memset(before[:], 0.0)
                nc.vector.tensor_copy(rank_b[:], K["rank1"][:])
                steps.run(nc.vector, step, 1)

            @block.gpsimd
            def _(pool):
                def step(i, j):
                    c = 2 * i + j
                    pool.wait_ge(tick_ready, c + 1)
                    pool.wait_ge(at_ready, c + 1)
                    nc.gpsimd.tensor_tensor(tick[:], tick[:], tick[:], ALU.mult)\
                        .then_inc(tick_ready, 1)
                    for t in range(CT):
                        for k in range(TOPK1):
                            nc.gpsimd.indirect_dma_start(
                                x_slots[:], bass.IndirectOffsetOnAxis(ap=at[j][:, k, t:t + 1], axis=0),
                                x[j][:, t, :], None).then_inc(sent[j], 16)

                nc.gpsimd.memset(tick[:], 0.0).then_inc(tick_ready, 1)
                steps.run(nc.gpsimd, step, 0)
                for j in range(2):
                    pool.wait_ge(sent[j], PER_CHUNK * (N // 2))

            @block.scalar
            def _(act):
                def rows(i, j):
                    c = 2 * i + j
                    if old(i, j, 2):
                        act.wait_ge(sent[j], PER_CHUNK * i)
                        act.wait_ge(turned, 2 * c - 2)
                    for t in range(CT):
                        last = normalise_act(nc, x[j][:, t, :], h, shift, rstd, c * CT + t)
                    last.then_inc(x_ready, 1)

                def read_turned(i, j):
                    c = 2 * i + j
                    for k in range(2):
                        act.wait_ge(turned, 2 * c + k + 1)
                        if old(i, j, 2):
                            act.wait_ge(logit_done, c - 1)
                        nc.scalar.activation(xT[j][:, k * G:(k + 1) * G, :], turn_ps[k][:], ACT.Copy)\
                            .then_inc(xT_ready, 1)

                def read_logits(i, j):
                    c = 2 * i + j
                    act.wait_ge(logit_done, c + 1)
                    if old(i, j, 1):
                        act.wait_ge(both_ready, c)
                    nc.scalar.activation(logits[:], logit_ps[:], ACT.Copy).then_inc(logit_read, 1)

                def scores(i, j):
                    act.wait_ge(both_ready, 2 * i + j + 1)
                    nc.scalar.activation(sig[:], best[:], ACT.Sigmoid).then_inc(sig_ready, 1)

                def step(i, j):
                    if later(i, j, 1):
                        rows(*later(i, j, 1))
                        read_turned(*later(i, j, 1))
                        read_logits(*later(i, j, 1))
                        scores(*later(i, j, 1))

                steps.run(nc.scalar, step, 1)

            @block.tensor
            def _(pe):
                def turn(i, j):
                    c = 2 * i + j
                    pe.wait_ge(x_ready, c + 1)
                    for k in range(2):
                        if old(i, j, 1):
                            pe.wait_ge(xT_ready, 2 * c + k - 1)
                        for t in range(G):
                            last = nc.tensor.transpose(turn_ps[k][:, t, :], x[j][:, k * G + t, :], ident[:])
                        last.then_inc(turned, 1)

                def multiply(i, j):
                    c = 2 * i + j
                    pe.wait_ge(xT_ready, 2 * c + 2)
                    if old(i, j, 1):
                        pe.wait_ge(logit_read, c)
                    for t in range(CT):
                        last = nc.tensor.matmul(logit_ps[:, t, :], xT[j][:, t, :], gate_sb[:], start=True, stop=True)
                    last.then_inc(logit_done, 1)

                def count(i, j):
                    c = 2 * i + j
                    pe.wait_ge(both_ready, c + 1)
                    if old(i, j, 1):
                        pe.wait_ge(at_ready, c)
                    nc.tensor.matmul(count_ps[:], K["after_b"][:], both[j][:], start=True, stop=False,
                                     skip_group_check=True)
                    for t in range(CT - 1):
                        n = CT - 1 - t
                        nc.tensor.matmul(count_ps[:, t + 1:CT, :], K["ones_b"][:],
                                         both[j][:, t:t + 1, :].to_broadcast([P, n, E1N]),
                                         start=False, stop=False, skip_group_check=True)
                    nc.tensor.matmul(count_ps[:], K["ones_b"][:], before_b[j][:].unsqueeze(1).to_broadcast(wide),
                                     start=False, stop=True, skip_group_check=True).then_inc(count_done, 1)

                def step(i, j):
                    if later(i, j, 1):
                        turn(*later(i, j, 1))
                        multiply(*later(i, j, 1))
                        count(*later(i, j, 1))

                pe.wait_ge(w_in, 16)
                steps.run(nc.tensor, step, 1)


def experts_top2(nc, K, x_slots, y_slots, w13, w2):
    ident = K["ident"]
    RT = 2 * CAP // P
    N = E1N // 2
    U = 4
    steps = Steps(N, U)
    later, old, run = steps.later, steps.old, steps.run
    with Bench(nc, "exp1") as m:
        x = [m.sb(f"x{j}", [P, RT, D]) for j in range(U)]
        wu = [m.sb(f"wu{j}", [P, 2, 2 * HID1]) for j in range(U)]
        wd = [m.sb(f"wd{j}", [2 * HID1, D]) for j in range(U)]
        y = [m.sb(f"y{j}", [P, RT, D]) for j in range(U)]
        xT = [m.sb(f"xT{j}", [P, 2, CAP]) for j in range(2)]
        gate, half, hid = ([m.sb(f"{name}{j}", [2 * HID1, CAP]) for j in range(2)] for name in ("gate", "half", "hid"))
        turn_ps = [m.ps(f"turn_ps{j}", [P, 2, CAP]) for j in range(2)]
        up_ps = [m.ps(f"up_ps{j}", [2 * HID1, 2, CAP]) for j in range(2)]
        down_ps = [[m.ps(f"down_ps{j}_{e}", [P, 512]) for e in range(2)] for j in range(2)]
        x_in = [m.sem(f"x_in{j}") for j in range(U)]
        y_out = [m.sem(f"y_out{j}") for j in range(U)]
        turned, xT_ready, up_done, gate_ready, half_ready, hid_ready, y_done, y_ready = (
            m.sem(n) for n in "turned xT_ready up_done gate_ready half_ready hid_ready y_done y_ready".split())

        with nc.Block() as block:
            @block.sync
            def _(sp):
                def load(i, j):
                    n = U * i + j
                    sp.dma_start(x[j][:], x_slots[bass.ds(n * 2 * CAP, 2 * CAP), :].rearrange("(t p) d -> p t d", p=P))\
                        .then_inc(x_in[j], 16)
                    sp.dma_start(wu[j][:], w13[bass.ds(n * 2 * D, 2 * D), :].rearrange("(e p) k -> p e k", p=P))\
                        .then_inc(x_in[j], 16)
                    sp.dma_start(wd[j][:], w2[bass.ds(n * 2 * HID1, 2 * HID1), :]).then_inc(x_in[j], 16)

                def step(i, j):
                    n = U * i + j
                    sp.wait_ge(y_done, n + 1)
                    if later(i, j, U):
                        load(i + 1, j)
                    sp.wait_ge(y_ready, n + 1)
                    sp.dma_start(y_slots[bass.ds(n * 2 * CAP, 2 * CAP), :].rearrange("(t p) d -> p t d", p=P),
                                 y[j][:]).then_inc(y_out[j], 16)

                for j in range(U):
                    load(0, j)
                run(nc.sync, step, 0)
                for j in range(U):
                    sp.wait_ge(y_out[j], 16 * (N // U))

            @block.tensor
            def _(pe):
                def turn(i, j):
                    n = U * i + j
                    pe.wait_ge(x_in[j], 48 * i + 48)
                    if old(i, j, 2):
                        pe.wait_ge(xT_ready, n - 1)
                    for e in range(2):
                        for t in range(CAP // P):
                            last = nc.tensor.transpose(turn_ps[j % 2][:, e, t * P:(t + 1) * P],
                                                       x[j][:, e * (CAP // P) + t, :], ident[:])
                    last.then_inc(turned, 1)

                def up(i, j):
                    n = U * i + j
                    pe.wait_ge(xT_ready, n + 1)
                    if old(i, j, 2):
                        pe.wait_ge(hid_ready, n - 1)
                    for k in range(2):
                        for e in range(2):
                            last = nc.tensor.matmul(up_ps[j % 2][e * HID1:(e + 1) * HID1, k, :],
                                                    wu[j][:, e, k * HID1:(k + 1) * HID1], xT[j % 2][:, e, :],
                                                    start=True, stop=True, skip_group_check=True)
                    last.then_inc(up_done, 1)

                def down(i, j):
                    n = U * i + j
                    pe.wait_ge(hid_ready, n + 1)
                    if old(i, j, 2):
                        pe.wait_ge(y_ready, n - 1)
                    for t in range(CAP // P):
                        for e in range(2):
                            of_e = slice(e * HID1, (e + 1) * HID1)
                            last = nc.tensor.matmul(down_ps[j % 2][e][:, t * D:(t + 1) * D],
                                                    hid[j % 2][of_e, t * P:(t + 1) * P], wd[j][of_e, :],
                                                    start=True, stop=True, skip_group_check=True)
                    last.then_inc(y_done, 1)

                def step(i, j):
                    if later(i, j, 2):
                        turn(*later(i, j, 2))
                    if later(i, j, 1):
                        up(*later(i, j, 1))
                    if later(i, j, 0):
                        down(i, j)

                run(nc.tensor, step, 2)

            @block.scalar
            def _(act):
                def read_turned(i, j):
                    n = U * i + j
                    act.wait_ge(turned, n + 1)
                    if old(i, j, 2):
                        act.wait_ge(up_done, n - 1)
                    nc.scalar.activation(xT[j % 2][:], turn_ps[j % 2][:], ACT.Copy).then_inc(xT_ready, 1)

                def gates(i, j):
                    n = U * i + j
                    act.wait_ge(up_done, n + 1)
                    if old(i, j, 2):
                        act.wait_ge(half_ready, n - 1)
                    nc.scalar.activation(gate[j % 2][:], up_ps[j % 2][:, 0, :], ACT.Sigmoid).then_inc(gate_ready, 1)

                def step(i, j):
                    if later(i, j, 2):
                        read_turned(*later(i, j, 2))
                    if later(i, j, 1):
                        gates(*later(i, j, 1))

                run(nc.scalar, step, 2)

            @block.vector
            def _(dve):
                def hidden(i, j):
                    n = U * i + j
                    dve.wait_ge(gate_ready, n + 1)
                    if old(i, j, 2):
                        dve.wait_ge(hid_ready, n - 1)
                        dve.wait_ge(y_done, n - 1)
                    nc.vector.tensor_tensor(half[j % 2][:], gate[j % 2][:], up_ps[j % 2][:, 0, :], ALU.mult)\
                        .then_inc(half_ready, 1)
                    dve.wait_ge(half_ready, n + 1)
                    nc.vector.tensor_tensor(hid[j % 2][:], half[j % 2][:], up_ps[j % 2][:, 1, :], ALU.mult)\
                        .then_inc(hid_ready, 1)

                def read_down(i, j):
                    n = U * i + j
                    dve.wait_ge(y_done, n + 1)
                    if old(i, j, U):
                        dve.wait_ge(y_out[j], 16 * i)
                    for e in range(2):
                        last = nc.vector.tensor_copy(y[j][:, e * (CAP // P):(e + 1) * (CAP // P), :],
                                                     down_ps[j % 2][e][:, 0:CAP // P * D].rearrange("p (t d) -> p t d", d=D))
                    last.then_inc(y_ready, 1)

                def step(i, j):
                    if later(i, j, 1):
                        hidden(*later(i, j, 1))
                    if later(i, j, 0):
                        read_down(i, j)

                run(nc.vector, step, 1)


def gather_and_share(nc, K, h, shift, rstd, y_slots, gather_at, weight, sw1, sw3, sw2, out):
    ident = K["ident"]
    W = TOPK1 * G * 16
    steps = Steps(NT // G, 2)
    later, old = steps.later, steps.old
    with Bench(nc, "final") as m:
        sw1_sb, sw3_sb, sw2_sb = m.sb("sw1", [P, P]), m.sb("sw3", [P, P]), m.sb("sw2", [P, D])
        x = [m.sb(f"x{j}", [P, G, D]) for j in range(2)]
        xT = [m.sb(f"xT{j}", [P, G, P]) for j in range(2)]
        y = [m.sb(f"y{j}", [P, G, TOPK1, D]) for j in range(2)]
        at = [m.sb(f"at{j}", [P, TOPK1, G], U32) for j in range(2)]
        gate, hid = m.sb("gate", [P, G * P]), m.sb("hid", [P, G * P])
        tick = m.sb("tick", [P, 1])
        turn_ps, p1, p3, py = ([m.ps(f"{n}{j}", [P, G, P]) for j in range(2)] for n in ("turn_ps", "p1", "p3", "py"))
        (w_in, x_ready, turned, xT_ready, up_done, gate_ready, half_ready, hid_ready, y_done, at_ready, tick_ready,
         first_added, shared_added, h_ready, stored) = (m.sem(n) for n in (
             "w_in x_ready turned xT_ready up_done gate_ready half_ready hid_ready y_done at_ready tick_ready "
             "first_added shared_added h_ready stored").split())
        got = [m.sem(f"got{j}") for j in range(2)]
        with nc.Block() as block:
            @block.sync
            def _(sp):
                def step(i, j):
                    g = 2 * i + j
                    sp.wait_ge(h_ready, g + 1)
                    for s in range(2):
                        sp.dma_start(out[bass.ds(2 * g, 2), s * P:s * P + ROWS[s], :].rearrange("b p d -> p b d"),
                                     h[0:ROWS[s], bass.ds(g * G, G), :]
                                     .rearrange("p (b s) d -> p b s d", s=2)[:, :, s, :]).then_inc(stored, 16)

                for dst, src in ((sw1_sb, sw1), (sw3_sb, sw3), (sw2_sb, sw2)):
                    sp.dma_start(dst[:], src).then_inc(w_in, 16)
                steps.run(nc.sync, step, 0)
                sp.wait_ge(w_in, 48)
                sp.wait_ge(stored, 32 * (NT // G))

            @block.gpsimd
            def _(pool):
                def step(i, j):
                    g = 2 * i + j
                    pool.wait_ge(tick_ready, g + 1)
                    pool.wait_ge(at_ready, g + 1)
                    nc.gpsimd.tensor_tensor(tick[:], tick[:], tick[:], ALU.mult).then_inc(tick_ready, 1)
                    for t in range(G):
                        for k in range(TOPK1):
                            nc.gpsimd.indirect_dma_start(
                                y[j][:, t, k, :], None, y_slots[:],
                                bass.IndirectOffsetOnAxis(ap=at[j][:, k, t:t + 1], axis=0)).then_inc(got[j], 16)

                nc.gpsimd.memset(tick[:], 0.0).then_inc(tick_ready, 1)
                steps.run(nc.gpsimd, step, 0)

            @block.scalar
            def _(act):
                def rows(i, j):
                    g = 2 * i + j
                    if old(i, j, 2):
                        act.wait_ge(turned, g - 1)
                    for t in range(G):
                        last = normalise_act(nc, x[j][:, t, :], h, shift, rstd, g * G + t)
                    last.then_inc(x_ready, 1)

                def read_turned(i, j):
                    g = 2 * i + j
                    act.wait_ge(turned, g + 1)
                    if old(i, j, 2):
                        act.wait_ge(up_done, g - 1)
                    nc.scalar.activation(xT[j][:], turn_ps[j][:], ACT.Copy).then_inc(xT_ready, 1)

                def gates(i, j):
                    g = 2 * i + j
                    act.wait_ge(up_done, g + 1)
                    if old(i, j, 1):
                        act.wait_ge(half_ready, g)
                    nc.scalar.activation(gate[:], p1[j][:].rearrange("p g d -> p (g d)"), ACT.Sigmoid)\
                        .then_inc(gate_ready, 1)

                def step(i, j):
                    if later(i, j, 2):
                        rows(*later(i, j, 2))
                    if later(i, j, 1):
                        read_turned(*later(i, j, 1))
                    if later(i, j, 0):
                        gates(i, j)

                steps.run(nc.scalar, step, 2)

            @block.vector
            def _(dve):
                def indices(i, j):
                    nc.vector.tensor_copy(at[j][:], gather_at[:, :, bass.ds((2 * i + j) * G, G)]).then_inc(at_ready, 1)

                def add_expert(i, j, k):
                    for t in range(G):
                        n = (2 * i + j) * G + t
                        last = nc.vector.scalar_tensor_tensor(one_tile(h, n), y[j][:, t, k, :],
                                                              one_column(weight[:, k], n), one_tile(h, n),
                                                              ALU.mult, ALU.add)
                    return last

                def finish(i, j):
                    g = 2 * i + j
                    dve.wait_ge(gate_ready, g + 1)
                    if old(i, j, 1):
                        dve.wait_ge(y_done, g)
                    flat = "p g d -> p (g d)"
                    nc.vector.tensor_tensor(hid[:], gate[:], p1[j][:].rearrange(flat), ALU.mult).then_inc(half_ready, 1)
                    dve.wait_ge(half_ready, g + 1)
                    nc.vector.tensor_tensor(hid[:], hid[:], p3[j][:].rearrange(flat), ALU.mult).then_inc(hid_ready, 1)
                    dve.wait_ge(x_ready, g + 1)
                    dve.wait_ge(got[j], W * (i + 1))
                    add_expert(i, j, 0).then_inc(first_added, 1)
                    dve.wait_ge(first_added, g + 1)
                    dve.wait_ge(y_done, g + 1)
                    ht = h[:, bass.ds(g * G, G), :]
                    nc.vector.tensor_tensor(ht, ht, py[j][:], ALU.add).then_inc(shared_added, 1)
                    dve.wait_ge(shared_added, g + 1)
                    add_expert(i, j, 1).then_inc(h_ready, 1)
                    dve.wait_ge(h_ready, g + 1)

                def step(i, j):
                    if later(i, j, 0):
                        finish(i, j)
                    if later(i, j, 2):
                        indices(*later(i, j, 2))

                steps.run(nc.vector, step, 2)

            @block.tensor
            def _(pe):
                def turn(i, j):
                    g = 2 * i + j
                    pe.wait_ge(x_ready, g + 1)
                    if old(i, j, 2):
                        pe.wait_ge(xT_ready, g - 1)
                    for t in range(G):
                        last = nc.tensor.transpose(turn_ps[j][:, t, :], x[j][:, t, :], ident[:])
                    last.then_inc(turned, 1)

                def up(i, j):
                    g = 2 * i + j
                    pe.wait_ge(xT_ready, g + 1)
                    if old(i, j, 2):
                        pe.wait_ge(hid_ready, g - 1)
                    nc.tensor.matmul(p1[j][:], sw1_sb[:], xT[j][:], start=True, stop=True)
                    nc.tensor.matmul(p3[j][:], sw3_sb[:], xT[j][:], start=True, stop=True).then_inc(up_done, 1)

                def down(i, j):
                    g = 2 * i + j
                    pe.wait_ge(hid_ready, g + 1)
                    if old(i, j, 2):
                        pe.wait_ge(shared_added, g - 1)
                    for t in range(G):
                        last = nc.tensor.matmul(py[j][:, t, :], hid[:, t * P:(t + 1) * P], sw2_sb[:],
                                                start=True, stop=True)
                    last.then_inc(y_done, 1)

                def step(i, j):
                    if later(i, j, 0):
                        up(i, j)
                    if later(i, j, 1):
                        turn(*later(i, j, 1))
                    if later(i, j, 0):
                        down(i, j)

                pe.wait_ge(w_in, 48)
                steps.run(nc.tensor, step, 1)


def load_constants(nc, K, tables, in_bf16, zeros):
    with Bench(nc, "const") as m:
        const_in = m.sem("const_in")
        wide = {n: m.sb(f"wide_{n}", list(K[n].shape)) for n in in_bf16}
        with nc.Block() as block:
            @block.sync
            def _(sp):
                for name in K:
                    sp.dma_start((wide.get(name) or K[name])[:], tables[name]).then_inc(const_in, 16)
                sp.wait_ge(const_in, 16 * len(K))

            @block.vector
            def _(dve):
                nc.vector.memset(zeros[:], 0.0)
                dve.wait_ge(const_in, 16 * len(K))
                for name in in_bf16:
                    nc.vector.tensor_copy(K[name][:], wide[name][:])


def await_cleared(nc, cleared):
    with nc.Block() as block:
        @block.sync
        def _(sp):
            sp.wait_ge(cleared, 16 * CLEARS)


def shape_tables():
    f = np.float32
    p, col = np.arange(P)[:, None], np.arange(T)[None, :]
    after = (col > p).astype(f)
    real = np.ones((P, NT), f)
    real[ROWS[1]:, 1::2] = 0
    tile, k = np.arange(NT)[None, :], np.arange(TOPK1)[None, :, None]
    head, query = p // HALF % H, p % HALF
    spill = SLOTS + k * (NT * P) + np.arange(NT)[None, None, :] * P + p[:, :, None]
    inc = {
        "after": after,
        "upto": (col >= p).astype(f),
        "ident": np.eye(P, dtype=f),
        "inv03": np.full((P, 1), 1.0 / 0.3, f),
        "after_b": after[:, :P],
        "ones_b": np.ones((P, P), f),
        "real": real,
        "pad_to": (1 - real) * (SLOTS + tile),
        "pad_from": (1 - real) * SLOTS0,
        "spill": spill.reshape(P, TOPK1 * NT),
        "rank0": np.tile(np.arange(E0, 0, -1), (P, 1)),
        "rank1": np.tile(np.arange(E1N, 0, -1), (P, 1)),
        "multiples": np.tile(P * np.arange(NT), (P, 1)),
        "tile_no": np.tile(np.arange(ST0), (P, 1)),
        "mask16": p // HD == np.arange(H),
        "mask_pv": np.concatenate([head == np.arange(D) // HD, query == np.arange(D) // HD], 1),
    }
    return {n: np.ascontiguousarray(a, dtype=f) for n, a in inc.items()}


def layouts(a):
    W, NLOW = a["L0_tok_W"], C + C * C + C ** 3

    def level(lo, hi):
        return W[:, lo:hi].reshape(D, (hi - lo) // C, C).transpose(1, 2, 0).reshape(-1, C * D)

    query = np.arange(HALF)[:, None, None]
    key_at = np.clip(np.arange(KWIN) - (REACH + HALF) - query, -MAX_REL, MAX_REL) + MAX_REL
    value_at = np.clip(np.arange(P)[:, None] - (np.arange(VWIN)[None, :] - P), -MAX_REL, MAX_REL) + MAX_REL
    rel_k, rel_v = a["L1_attn_rel_k"], a["L1_attn_rel_v"]
    far_keys = np.zeros((P, FARWIN), np.float32)
    far_keys[:, :T - BQ - REACH] = np.tile(rel_k[0], H)[:, None]
    far_keys[:, T + REACH:] = np.tile(rel_k[2 * MAX_REL], H)[:, None]
    w1, b1, w2 = a["L0_ffn_W1"], a["L0_ffn_b1"], a["L0_ffn_W2"]
    lay = {
        "x_t": a["x"].transpose(1, 0, 2).reshape(T, B * CIN),
        "w_main": level(NLOW, W.shape[1]),
        "w_low": np.concatenate([level(C + C * C, NLOW), level(C, C + C * C), level(0, C)]),
        "tok_b": a["L0_tok_b"],
        "fuz_wq": a["L0_attn_Wq"].T, "fuz_bq": a["L0_attn_bq"][:, None],
        "fuz_wk": a["L0_attn_Wk"].T, "fuz_bk": a["L0_attn_bk"][:, None],
        "gate0": a["L0_ffn_Wr"], "gate0_b": a["L0_ffn_br"],
        "exp0_w1": np.concatenate([w1.transpose(1, 0, 2), b1.reshape(E0, HID0 // P, P).transpose(2, 0, 1)], 2),
        "exp0_w2": w2.reshape(E0, HID0 // P, P, D).transpose(2, 0, 1, 3).reshape(P, E0, -1),
        "exp0_b2": a["L0_ffn_b2"].reshape(-1),
        "rel_wq": a["L1_attn_Wq"], "rel_bq": a["L1_attn_bq"][:, None],
        "rel_wk": a["L1_attn_Wk"], "rel_bk": a["L1_attn_bk"][:, None],
        "rel_wv": a["L1_attn_Wv"], "rel_bv": a["L1_attn_bv"],
        "rel_wo": a["L1_attn_Wo"], "rel_bo": a["L1_attn_bo"],
        "rel_far": far_keys,
        "rel_vends": np.stack([np.tile(rel_v[0], H), np.tile(rel_v[2 * MAX_REL], H)]),
        "rel_ktab": rel_k[key_at, np.arange(HD)[None, :, None]].reshape(P, KWIN),
        "rel_vtab": rel_v[value_at],
        "gate1": a["L1_ffn_gate_w"].T,
        "sw1": a["L1_ffn_sw1"], "sw3": a["L1_ffn_sw3"], "sw2": a["L1_ffn_sw2"],
        "exp1_w13": np.concatenate([a["L1_ffn_w1"], a["L1_ffn_w3"]], 2).reshape(E1N * D, 2 * HID1),
        "exp1_w2": a["L1_ffn_w2"].reshape(E1N * HID1, D),
    }
    t = np.diff(np.linspace(0.0, 1.0, T, dtype=np.float32))
    lay["step_time"] = np.stack([t[:P], np.concatenate([t[P:], np.zeros(P - ROWS[1], np.float32)])], 1)
    return {n: np.ascontiguousarray(v) for n, v in lay.items()}


def moe0(nc, K, h, mean, rstd, stats, x_slots, y0_slots, w, attention):
    with Bench(nc, "moe0") as q:
        weights = Ahead(q, {
            "w1": ([P, E0, HID0 + HID0 // P], w["exp0_w1"]),
            "w2": ([P, E0, HID0 // P * D], w["exp0_w2"]),
            "b2": ([P, E0, D], w["exp0_b2"].partition_broadcast(P).rearrange("p (e d) -> p e d", d=D))})
        logits = q.sb("logits", [P, NT, E0])
        to, back = q.sb("to", [P, 1, NT], U32), q.sb("back", [P, 1, NT], U32)
        tile_expert = q.sb("tile_expert", [P, ST0], U32)
        router_logits(nc, K, h, mean, rstd, logits, w["gate0"], w["gate0_b"], E0, "logits0")
        weights.start(nc)
        attention.start(nc)
        route_top1(nc, K, logits, to, back, tile_expert)
        scatter_rows(nc, h, mean, rstd, x_slots, to, 1, "scatter0")
        experts_top1(nc, K, x_slots, y0_slots, tile_expert, weights)
        gather_rows(nc, h, stats, y0_slots, back, None, 1, "gather0")


def moe1(nc, K, h, mean, rstd, x_slots, y1_slots, w, out):
    with Bench(nc, "moe1") as q:
        back = q.sb("back", [P, TOPK1, NT], U32)
        weight = q.sb("weight", [P, TOPK1, NT])
        shift = q.sb("shift", [P, NT])
        with nc.Block() as block:
            @block.vector
            def _(dve):
                nc.vector.scalar_tensor_tensor(shift[:], mean[:], -1.0, rstd[:], ALU.mult, ALU.mult)
        choose_and_send(nc, K, h, shift, rstd, x_slots, back, weight, w["gate1"])
        experts_top2(nc, K, x_slots, y1_slots, w["exp1_w13"], w["exp1_w2"])
        gather_and_share(nc, K, h, shift, rstd, y1_slots, back, weight, w["sw1"], w["sw3"], w["sw2"], out)


def build(nc, t, w, out):
    in_bf16 = ("after_b", "ones_b")
    x_slots = nc.dram_tensor("x_slots", (SLOTS + TOPK1 * NT * P, D), FP32, kind="Internal").ap()
    y0_slots = nc.dram_tensor("y0_slots", (SLOTS0 + 1, D), FP32, kind="Internal").ap()
    y1_slots = nc.dram_tensor("y1_slots", (SLOTS1 + 1, D), FP32, kind="Internal").ap()
    o_rows = [nc.dram_tensor(f"o_rows{r}", (2, P, P), FP32, kind="Internal").ap() for r in range(2)]
    q_rows = [nc.dram_tensor(f"q_rows{r}", (P, T), FP32, kind="Internal").ap() for r in range(2)]
    with Bench(nc, "all") as m:
        h = m.sb("h", [P, NT, D])
        stats, mean, rstd = m.sb("stats", [P, NT, 6]), m.sb("mean", [P, NT]), m.sb("rstd", [P, NT])
        cleared = m.sem("cleared")
        K = {n: m.sb(f"k_{n}", list(a.shape), BF16 if n in in_bf16 else FP32) for n, a in t.items()}
        with Bench(nc, "early") as early:
            zeros = early.sb("zeros", [P, 4 * D])
            load_constants(nc, K, t, in_bf16, zeros)
            signature_tokens(nc, K, h, stats, w["x_t"], w["step_time"], w["w_main"], w["w_low"], w["tok_b"])
            norm_factors(nc, stats, mean, rstd, "norm0")
            fuzzy_attention(nc, K, h, mean, rstd, stats, w["fuz_wq"], w["fuz_bq"], w["fuz_wk"], w["fuz_bk"],
                            lambda sp: clear_slots(x_slots, [(y0_slots, SLOTS0), (y1_slots, SLOTS1)], zeros, cleared, sp))
            norm_factors(nc, stats, mean, rstd, "norm1")
            await_cleared(nc, cleared)
        with Bench(nc, "attn") as attn:
            weights = attention_weights(attn, w)
            moe0(nc, K, h, mean, rstd, stats, x_slots, y0_slots, w, weights)
            norm_factors(nc, stats, mean, rstd, "norm2")
            relative_attention(nc, K, h, mean, rstd, stats, o_rows, q_rows, weights)
        norm_factors(nc, stats, mean, rstd, "norm3")
        moe1(nc, K, h, mean, rstd, x_slots, y1_slots, w, out)


def kernel(**inputs):
    import numpy as _np
    import concourse.bacc as _bacc
    from concourse.bass_utils import run_bass_kernel_spmd as _run

    nc = _bacc.Bacc("TRN2", target_bir_lowering=False, num_devices=1)
    arrays = {}

    def dram(name, a):
        arrays[name] = a
        return nc.dram_tensor(name, a.shape, mybir.dt.from_np(a.dtype), kind="ExternalInput").ap()

    tables = {n: dram(f"table_{n}", a) for n, a in shape_tables().items()}
    laid = {n: dram(f"in_{n}", a) for n, a in layouts({k: _np.asarray(v) for k, v in inputs.items()}).items()}
    out = nc.dram_tensor("out_dram", (B, L, D), FP32, kind="ExternalOutput").ap()
    build(nc, tables, laid, out)
    r = _run(nc, [arrays], core_ids=[0])
    return r.results[0]["out_dram"]
```
